# Optimizing a Trainium2 kernel written in Bass

```python
import numpy as np
import jax
import jax.numpy as jnp

def _softmax(x, axis=-1):
    return jax.nn.softmax(x, axis=axis)

def _gelu(x):
    return jax.nn.gelu(x, approximate=True)

def _silu(x):
    return jax.nn.silu(x)

def _sigmoid(x):
    return jax.nn.sigmoid(x)

def _layernorm(x, axis=-1, eps=1e-05):
    m = jnp.mean(x, axis=axis, keepdims=True)
    v = jnp.var(x, axis=axis, keepdims=True)
    return (x - m) / jnp.sqrt(v + eps)

def _scatter_add(tgt, idx, src, axis=0):
    return tgt.at[idx].add(src)

def _segment_sum(src, seg, n):
    return jax.ops.segment_sum(src, seg, n)
kernel_name = 'mk_sandwich_d2_jaxref_r8_4fbc19'

def setup_inputs(seed: int=0):
    np.random.seed(seed)
    _w = jnp.asarray

    def _L0_attn_setup():
        import jax, jax.numpy as jnp
        import numpy as np
        import math
        HIDDEN = 256
        NUM_HEADS = 16
        HEAD_DIM = HIDDEN // NUM_HEADS
        BATCH = 2
        SEQ = 512
        BLOCK = 128
        TOPK = 64
        NEG = -1000000000.0

        def _split_heads(x):
            n, t, _ = x.shape
            return x.reshape(n, t, NUM_HEADS, HEAD_DIM).transpose(0, 2, 1, 3)

        def _local_attention(q, k, v):
            n, h, t, d = q.shape
            nb = t // BLOCK
            half = BLOCK // 2
            qb = q.reshape(n, h, nb, BLOCK, d)
            win = jnp.arange(nb)[:, None] * BLOCK - half + jnp.arange(2 * BLOCK)[None, :]
            valid = (win >= 0) & (win < t)
            winc = jnp.clip(win, 0, t - 1)
            kb = k[:, :, winc, :]
            vb = v[:, :, winc, :]
            scores = jnp.einsum('nhbqd,nhbkd->nhbqk', qb, kb) / math.sqrt(d)
            scores = jnp.where(valid[None, None, :, None, :], scores, NEG)
            probs = jax.nn.softmax(scores, axis=-1)
            ctx = jnp.einsum('nhbqk,nhbkd->nhbqd', probs, vb)
            return ctx.reshape(n, h, t, d)

        def _global_index(q):
            n, h, t, d = q.shape
            norm = jnp.linalg.norm(q, axis=-1)
            _, top_idx = jax.lax.top_k(norm, TOPK - 2)
            bos = jnp.zeros((n, h, 1), jnp.int32)
            eos = jnp.full((n, h, 1), t - 1, jnp.int32)
            return jnp.concatenate([bos, top_idx.astype(jnp.int32), eos], axis=-1)
        key = jax.random.key(seed)
        ks = jax.random.split(key, 7)
        s = 1.0 / math.sqrt(HIDDEN)
        return {'hidden_states': jax.random.normal(ks[0], (BATCH, SEQ, HIDDEN), jnp.float32), 'Wq': jax.random.normal(ks[1], (HIDDEN, HIDDEN), jnp.float32) * s, 'bq': jnp.zeros((HIDDEN,), jnp.float32), 'Wk': jax.random.normal(ks[2], (HIDDEN, HIDDEN), jnp.float32) * s, 'bk': jnp.zeros((HIDDEN,), jnp.float32), 'Wv': jax.random.normal(ks[3], (HIDDEN, HIDDEN), jnp.float32) * s, 'bv': jnp.zeros((HIDDEN,), jnp.float32)}
    _L0_attn_in = _L0_attn_setup()

    def _L0_ffn_setup():
        import jax, jax.numpy as jnp
        import numpy as np
        E, H, I = (8, 256, 512)
        TOP_K = 1
        B, S = (1, 256)
        key = jax.random.key(seed)
        ks = jax.random.split(key, 7)
        std = 0.02
        return {'hidden_states': jax.random.normal(ks[0], (B, S, H), dtype=jnp.float32), 'router_w': jax.random.normal(ks[1], (E, H), dtype=jnp.float32) * std, 'gate_up_proj': jax.random.normal(ks[2], (E, H, 2 * I), dtype=jnp.float32) * std, 'down_proj': jax.random.normal(ks[3], (E, I, H), dtype=jnp.float32) * std, 'shared_gate_w': jax.random.normal(ks[4], (H, I), dtype=jnp.float32) * std, 'shared_up_w': jax.random.normal(ks[5], (H, I), dtype=jnp.float32) * std, 'shared_down_w': jax.random.normal(ks[6], (I, H), dtype=jnp.float32) * std}
    _L0_ffn_in = _L0_ffn_setup()

    def _L1_attn_setup():
        import jax, jax.numpy as jnp
        import numpy as np
        D_MODEL = 256
        D_INNER = 512
        D_STATE = 64
        N_QK_HEADS = 8
        N_V_HEADS = 64
        CHUNK = 128
        KSIZE = 4
        CONV_DIM = D_INNER + 2 * N_QK_HEADS * D_STATE
        PROJ_DIM = CONV_DIM + D_INNER + N_V_HEADS

        def segsum(x):
            T = x.shape[-1]
            xe = jnp.broadcast_to(x[..., None], x.shape + (T,))
            strict_lower = jnp.tril(jnp.ones((T, T), dtype=bool), -1)
            xe = jnp.where(strict_lower, xe, 0.0)
            s = jnp.cumsum(xe, axis=-2)
            lower = jnp.tril(jnp.ones((T, T), dtype=bool), 0)
            return jnp.where(lower, s, -jnp.inf)

        def ssd_chunk_scan(X, dA, Bm, Cm, chunk):
            b, l, h, p = X.shape
            g = Bm.shape[2]
            rep = h // g
            Bm = jnp.repeat(Bm, rep, axis=2)
            Cm = jnp.repeat(Cm, rep, axis=2)
            c = l // chunk
            X = X.reshape(b, c, chunk, h, p)
            Bm = Bm.reshape(b, c, chunk, h, -1)
            Cm = Cm.reshape(b, c, chunk, h, -1)
            A = jnp.transpose(dA.reshape(b, c, chunk, h), (0, 3, 1, 2))
            A_cum = jnp.cumsum(A, axis=-1)
            Lm = jnp.exp(segsum(A))
            Y_diag = jnp.einsum('bcshn,bczhn,bhcsz,bczhp->bcshp', Cm, Bm, Lm, X)
            decay_states = jnp.exp(A_cum[..., -1:] - A_cum)
            states = jnp.einsum('bcshn,bhcs,bcshp->bchpn', Bm, decay_states, X)
            states = jnp.concatenate([jnp.zeros_like(states[:, :1]), states], axis=1)
            chunk_sums = jnp.pad(A_cum[..., -1], ((0, 0), (0, 0), (1, 0)))
            decay_chunk = jnp.exp(segsum(chunk_sums))
            new_states = jnp.einsum('bhzc,bchpn->bzhpn', decay_chunk, states)
            states = new_states[:, :-1]
            state_decay_out = jnp.exp(A_cum)
            Y_off = jnp.einsum('bcshn,bchpn,bhcs->bcshp', Cm, states, state_decay_out)
            return (Y_diag + Y_off).reshape(b, l, h, p)
        key = jax.random.key(seed)
        ks = jax.random.split(key, 6)
        input_ = jax.random.normal(ks[0], (2, 512, D_MODEL), dtype=jnp.float32)
        in_proj_w = jax.random.normal(ks[1], (PROJ_DIM, D_MODEL), dtype=jnp.float32) * (2.0 / D_MODEL) ** 0.5
        cb = (CONV_DIM * KSIZE) ** (-0.5)
        conv1d_weight = jax.random.uniform(ks[2], (CONV_DIM, 1, KSIZE), dtype=jnp.float32, minval=-cb, maxval=cb)
        conv1d_bias = jax.random.uniform(ks[3], (CONV_DIM,), dtype=jnp.float32, minval=-0.5, maxval=0.5)
        z_bias = jnp.zeros((D_INNER,), dtype=jnp.float32)
        D = jnp.ones((N_V_HEADS,), dtype=jnp.float32)
        out_proj_w = jax.random.normal(ks[4], (D_MODEL, D_INNER), dtype=jnp.float32) * (2.0 / D_INNER) ** 0.5
        return {'input_': input_, 'in_proj_w': in_proj_w, 'conv1d_weight': conv1d_weight, 'conv1d_bias': conv1d_bias, 'z_bias': z_bias, 'D': D, 'out_proj_w': out_proj_w}
    _L1_attn_in = _L1_attn_setup()

    def _L1_ffn_setup():
        import jax, jax.numpy as jnp
        import numpy as np
        BLOCK_SIZE = 32
        HIDDEN_SIZE = 256
        MLP_DIM = 2048
        NVFP4_LUT = jnp.array([0.0, 0.5, 1.0, 1.5, 2.0, 3.0, 4.0, 6.0, 0.0, -0.5, -1.0, -1.5, -2.0, -3.0, -4.0, -6.0], dtype=jnp.float32)

        def dequant_nvfp4(W_packed, scales, block=BLOCK_SIZE):
            N = W_packed.shape[0]
            low = W_packed & 15
            high = W_packed >> 4 & 15
            idx = jnp.stack([low, high], axis=-1).reshape(N, -1)
            vals = NVFP4_LUT[idx]
            K = vals.shape[1]
            vals = vals.reshape(N, K // block, block) * scales[:, :, None]
            return vals.reshape(N, K)
        key = jax.random.key(seed)
        ks = jax.random.split(key, 7)
        x = jax.random.normal(ks[0], (4, 32, HIDDEN_SIZE), dtype=jnp.float32)
        gate_W_packed = jax.random.randint(ks[1], (MLP_DIM, HIDDEN_SIZE // 2), 0, 32, dtype=jnp.int32)
        gate_scales = jax.random.uniform(ks[2], (MLP_DIM, HIDDEN_SIZE // BLOCK_SIZE), dtype=jnp.float32) * 0.1 + 0.001
        up_W_packed = jax.random.randint(ks[3], (MLP_DIM, HIDDEN_SIZE // 2), 0, 32, dtype=jnp.int32)
        up_scales = jax.random.uniform(ks[4], (MLP_DIM, HIDDEN_SIZE // BLOCK_SIZE), dtype=jnp.float32) * 0.1 + 0.001
        down_W_packed = jax.random.randint(ks[5], (HIDDEN_SIZE, MLP_DIM // 2), 0, 32, dtype=jnp.int32)
        down_scales = jax.random.uniform(ks[6], (HIDDEN_SIZE, MLP_DIM // BLOCK_SIZE), dtype=jnp.float32) * 0.1 + 0.001
        return {'x': x, 'gate_W_packed': gate_W_packed, 'gate_scales': gate_scales, 'up_W_packed': up_W_packed, 'up_scales': up_scales, 'down_W_packed': down_W_packed, 'down_scales': down_scales}
    _L1_ffn_in = _L1_ffn_setup()
    _d = {'L0_attn_hidden_states': _L0_attn_in['hidden_states'], 'L0_attn_Wq': _L0_attn_in['Wq'], 'L0_attn_bq': _L0_attn_in['bq'], 'L0_attn_Wk': _L0_attn_in['Wk'], 'L0_attn_bk': _L0_attn_in['bk'], 'L0_attn_Wv': _L0_attn_in['Wv'], 'L0_attn_bv': _L0_attn_in['bv'], 'L0_ffn_router_w': _L0_ffn_in['router_w'], 'L0_ffn_gate_up_proj': _L0_ffn_in['gate_up_proj'], 'L0_ffn_down_proj': _L0_ffn_in['down_proj'], 'L0_ffn_shared_gate_w': _L0_ffn_in['shared_gate_w'], 'L0_ffn_shared_up_w': _L0_ffn_in['shared_up_w'], 'L0_ffn_shared_down_w': _L0_ffn_in['shared_down_w'], 'L1_attn_in_proj_w': _L1_attn_in['in_proj_w'], 'L1_attn_conv1d_weight': _L1_attn_in['conv1d_weight'], 'L1_attn_conv1d_bias': _L1_attn_in['conv1d_bias'], 'L1_attn_z_bias': _L1_attn_in['z_bias'], 'L1_attn_D': _L1_attn_in['D'], 'L1_attn_out_proj_w': _L1_attn_in['out_proj_w'], 'L1_ffn_gate_W_packed': _L1_ffn_in['gate_W_packed'], 'L1_ffn_gate_scales': _L1_ffn_in['gate_scales'], 'L1_ffn_up_W_packed': _L1_ffn_in['up_W_packed'], 'L1_ffn_up_scales': _L1_ffn_in['up_scales'], 'L1_ffn_down_W_packed': _L1_ffn_in['down_W_packed'], 'L1_ffn_down_scales': _L1_ffn_in['down_scales']}
    _x0 = _d['L0_attn_hidden_states']
    _d['L0_attn_hidden_states'] = jax.random.normal(jax.random.fold_in(jax.random.key(seed), 1), (1, 2048, 256), dtype=_x0.dtype)
    del _x0
    return _d

def reference(L0_attn_hidden_states, L0_attn_Wq, L0_attn_bq, L0_attn_Wk, L0_attn_bk, L0_attn_Wv, L0_attn_bv, L0_ffn_router_w, L0_ffn_gate_up_proj, L0_ffn_down_proj, L0_ffn_shared_gate_w, L0_ffn_shared_up_w, L0_ffn_shared_down_w, L1_attn_in_proj_w, L1_attn_conv1d_weight, L1_attn_conv1d_bias, L1_attn_z_bias, L1_attn_D, L1_attn_out_proj_w, L1_ffn_gate_W_packed, L1_ffn_gate_scales, L1_ffn_up_W_packed, L1_ffn_up_scales, L1_ffn_down_W_packed, L1_ffn_down_scales):

    def _L0_attn_ref(hidden_states, Wq, bq, Wk, bk, Wv, bv):
        import jax, jax.numpy as jnp
        import numpy as np
        import math
        HIDDEN = 256
        NUM_HEADS = 16
        HEAD_DIM = HIDDEN // NUM_HEADS
        BATCH = 2
        SEQ = 512
        BLOCK = 128
        TOPK = 64
        NEG = -1000000000.0

        def _split_heads(x):
            n, t, _ = x.shape
            return x.reshape(n, t, NUM_HEADS, HEAD_DIM).transpose(0, 2, 1, 3)

        def _local_attention(q, k, v):
            n, h, t, d = q.shape
            nb = t // BLOCK
            half = BLOCK // 2
            qb = q.reshape(n, h, nb, BLOCK, d)
            win = jnp.arange(nb)[:, None] * BLOCK - half + jnp.arange(2 * BLOCK)[None, :]
            valid = (win >= 0) & (win < t)
            winc = jnp.clip(win, 0, t - 1)
            kb = k[:, :, winc, :]
            vb = v[:, :, winc, :]
            scores = jnp.einsum('nhbqd,nhbkd->nhbqk', qb, kb) / math.sqrt(d)
            scores = jnp.where(valid[None, None, :, None, :], scores, NEG)
            probs = jax.nn.softmax(scores, axis=-1)
            ctx = jnp.einsum('nhbqk,nhbkd->nhbqd', probs, vb)
            return ctx.reshape(n, h, t, d)

        def _global_index(q):
            n, h, t, d = q.shape
            norm = jnp.linalg.norm(q, axis=-1)
            _, top_idx = jax.lax.top_k(norm, TOPK - 2)
            bos = jnp.zeros((n, h, 1), jnp.int32)
            eos = jnp.full((n, h, 1), t - 1, jnp.int32)
            return jnp.concatenate([bos, top_idx.astype(jnp.int32), eos], axis=-1)
        q = _split_heads(hidden_states @ Wq + bq)
        k = _split_heads(hidden_states @ Wk + bk)
        v = _split_heads(hidden_states @ Wv + bv)
        n, h, t, d = q.shape
        ctx = _local_attention(q, k, v)
        idx = _global_index(q)
        qg = jnp.take_along_axis(q, idx[..., None], axis=-2)
        g_scores = jnp.einsum('nhqd,nhkd->nhqk', qg, k) / math.sqrt(d)
        g_probs = jax.nn.softmax(g_scores, axis=-1)
        g_ctx = jnp.einsum('nhqk,nhkd->nhqd', g_probs, v)
        bn = jnp.arange(n)[:, None, None]
        bh = jnp.arange(h)[None, :, None]
        ctx = ctx.at[bn, bh, idx].set(g_ctx)
        out = ctx.transpose(0, 2, 1, 3).reshape(n, t, h * d)
        return out

    def _L0_ffn_ref(hidden_states, router_w, gate_up_proj, down_proj, shared_gate_w, shared_up_w, shared_down_w):
        import jax, jax.numpy as jnp
        import numpy as np
        E, H, I = (8, 256, 512)
        TOP_K = 1
        B, S = (1, 256)
        orig_shape = hidden_states.shape
        x = hidden_states.reshape(-1, H)
        T = x.shape[0]
        logits = x @ router_w.T
        top_vals, top_idx = jax.lax.top_k(logits, TOP_K)
        scores = jnp.full_like(logits, -jnp.inf)
        scores = scores.at[jnp.arange(T)[:, None], top_idx].set(top_vals)
        scores = jax.nn.sigmoid(scores.astype(jnp.float32)).astype(logits.dtype)
        xr = x[None, :, :] * scores.T[:, :, None]
        gate_up = jnp.einsum('eth,ehf->etf', xr, gate_up_proj)
        gate, up = jnp.split(gate_up, 2, axis=-1)
        routed = jnp.einsum('etf,efh->eth', up * jax.nn.silu(gate), down_proj)
        routed_sum = routed.sum(axis=0)
        shared = jax.nn.silu(x @ shared_gate_w) * (x @ shared_up_w) @ shared_down_w
        return (shared + routed_sum).reshape(orig_shape)

    def _L1_attn_ref(input_, in_proj_w, conv1d_weight, conv1d_bias, z_bias, D, out_proj_w):
        import jax, jax.numpy as jnp
        import numpy as np
        D_MODEL = 256
        D_INNER = 512
        D_STATE = 64
        N_QK_HEADS = 8
        N_V_HEADS = 64
        CHUNK = 128
        KSIZE = 4
        CONV_DIM = D_INNER + 2 * N_QK_HEADS * D_STATE
        PROJ_DIM = CONV_DIM + D_INNER + N_V_HEADS

        def segsum(x):
            T = x.shape[-1]
            xe = jnp.broadcast_to(x[..., None], x.shape + (T,))
            strict_lower = jnp.tril(jnp.ones((T, T), dtype=bool), -1)
            xe = jnp.where(strict_lower, xe, 0.0)
            s = jnp.cumsum(xe, axis=-2)
            lower = jnp.tril(jnp.ones((T, T), dtype=bool), 0)
            return jnp.where(lower, s, -jnp.inf)

        def ssd_chunk_scan(X, dA, Bm, Cm, chunk):
            b, l, h, p = X.shape
            g = Bm.shape[2]
            rep = h // g
            Bm = jnp.repeat(Bm, rep, axis=2)
            Cm = jnp.repeat(Cm, rep, axis=2)
            c = l // chunk
            X = X.reshape(b, c, chunk, h, p)
            Bm = Bm.reshape(b, c, chunk, h, -1)
            Cm = Cm.reshape(b, c, chunk, h, -1)
            A = jnp.transpose(dA.reshape(b, c, chunk, h), (0, 3, 1, 2))
            A_cum = jnp.cumsum(A, axis=-1)
            Lm = jnp.exp(segsum(A))
            Y_diag = jnp.einsum('bcshn,bczhn,bhcsz,bczhp->bcshp', Cm, Bm, Lm, X)
            decay_states = jnp.exp(A_cum[..., -1:] - A_cum)
            states = jnp.einsum('bcshn,bhcs,bcshp->bchpn', Bm, decay_states, X)
            states = jnp.concatenate([jnp.zeros_like(states[:, :1]), states], axis=1)
            chunk_sums = jnp.pad(A_cum[..., -1], ((0, 0), (0, 0), (1, 0)))
            decay_chunk = jnp.exp(segsum(chunk_sums))
            new_states = jnp.einsum('bhzc,bchpn->bzhpn', decay_chunk, states)
            states = new_states[:, :-1]
            state_decay_out = jnp.exp(A_cum)
            Y_off = jnp.einsum('bcshn,bchpn,bhcs->bcshp', Cm, states, state_decay_out)
            return (Y_diag + Y_off).reshape(b, l, h, p)
        b, L, _ = input_.shape
        xBCzA = jnp.einsum('bld,ed->ble', input_, in_proj_w)
        xBC = xBCzA[..., :CONV_DIM]
        z = xBCzA[..., CONV_DIM:CONV_DIM + D_INNER]
        A_log = xBCzA[..., CONV_DIM + D_INNER:]
        xt = jnp.transpose(xBC, (0, 2, 1))
        y = jax.lax.conv_general_dilated(xt, conv1d_weight, (1,), [(KSIZE - 1, 0)], feature_group_count=CONV_DIM, dimension_numbers=('NCH', 'OIH', 'NCH'))
        xBC = jax.nn.silu(jnp.transpose(y + conv1d_bias[None, :, None], (0, 2, 1)))
        x = xBC[..., :D_INNER].reshape(b, L, N_V_HEADS, D_INNER // N_V_HEADS)
        Bm = xBC[..., D_INNER:D_INNER + N_QK_HEADS * D_STATE].reshape(b, L, N_QK_HEADS, D_STATE)
        Cm = xBC[..., D_INNER + N_QK_HEADS * D_STATE:].reshape(b, L, N_QK_HEADS, D_STATE)
        dt = jax.nn.softplus(A_log)
        x_in = x / dt[..., None]
        y_ssm = ssd_chunk_scan(x_in * dt[..., None], -dt, Bm, Cm, CHUNK)
        Du = D[None, None, :, None] * x_in
        yf = (y_ssm + Du).reshape(b, L, D_INNER)
        out = jnp.einsum('bld,ed->ble', yf * jax.nn.silu(z + z_bias), out_proj_w)
        return out

    def _L1_ffn_ref(x, gate_W_packed, gate_scales, up_W_packed, up_scales, down_W_packed, down_scales):
        import jax, jax.numpy as jnp
        import numpy as np
        BLOCK_SIZE = 32
        HIDDEN_SIZE = 256
        MLP_DIM = 2048
        NVFP4_LUT = jnp.array([0.0, 0.5, 1.0, 1.5, 2.0, 3.0, 4.0, 6.0, 0.0, -0.5, -1.0, -1.5, -2.0, -3.0, -4.0, -6.0], dtype=jnp.float32)

        def dequant_nvfp4(W_packed, scales, block=BLOCK_SIZE):
            N = W_packed.shape[0]
            low = W_packed & 15
            high = W_packed >> 4 & 15
            idx = jnp.stack([low, high], axis=-1).reshape(N, -1)
            vals = NVFP4_LUT[idx]
            K = vals.shape[1]
            vals = vals.reshape(N, K // block, block) * scales[:, :, None]
            return vals.reshape(N, K)
        B, S, H = x.shape
        xt = x.reshape(B * S, H)
        Wg = dequant_nvfp4(gate_W_packed, gate_scales)
        Wu = dequant_nvfp4(up_W_packed, up_scales)
        Wd = dequant_nvfp4(down_W_packed, down_scales)
        gate = jnp.einsum('th,nh->tn', xt, Wg)
        up = jnp.einsum('th,nh->tn', xt, Wu)
        gelu = jnp.tanh(0.7978845608028654 * (gate + 0.044715 * gate ** 3)) * gate * 0.5 + gate * 0.5
        inter = gelu * up
        out = jnp.einsum('tn,hn->th', inter, Wd)
        return out.reshape(B, S, H)
    x = L0_attn_hidden_states
    x = x + _layernorm(_L0_attn_ref(_layernorm(x, axis=-1), L0_attn_Wq, L0_attn_bq, L0_attn_Wk, L0_attn_bk, L0_attn_Wv, L0_attn_bv), axis=-1)
    x = x + _layernorm(_L0_ffn_ref(_layernorm(x, axis=-1), L0_ffn_router_w, L0_ffn_gate_up_proj, L0_ffn_down_proj, L0_ffn_shared_gate_w, L0_ffn_shared_up_w, L0_ffn_shared_down_w), axis=-1)
    x = x + _layernorm(_L1_attn_ref(_layernorm(x, axis=-1), L1_attn_in_proj_w, L1_attn_conv1d_weight, L1_attn_conv1d_bias, L1_attn_z_bias, L1_attn_D, L1_attn_out_proj_w), axis=-1)
    x = x + _layernorm(_L1_ffn_ref(_layernorm(x, axis=-1), L1_ffn_gate_W_packed, L1_ffn_gate_scales, L1_ffn_up_W_packed, L1_ffn_up_scales, L1_ffn_down_W_packed, L1_ffn_down_scales), axis=-1)
    return x

_drawn_inputs = setup_inputs


def setup_inputs(seed=0):
    import zlib

    import numpy as np

    out = dict(_drawn_inputs(seed))
    spreads = {'L0_attn_bq': (0.0, 0.1),
     'L0_attn_bk': (0.0, 0.1),
     'L0_attn_bv': (0.0, 0.1),
     'L1_attn_z_bias': (0.0, 0.1),
     'L1_attn_D': (1.0, 0.2)}
    factors = {}
    for name, (base, spread) in spreads.items():
        noise = np.random.default_rng([zlib.crc32(name.encode()), seed]).standard_normal(out[name].shape)
        drawn = base * np.exp(spread * noise) if base else spread * noise
        out[name] = jnp.asarray(drawn.astype(out[name].dtype))
    for name, factor in factors.items():
        out[name] = (out[name] * factor).astype(out[name].dtype)
    return out
```

```python
import concourse.bass as bass
from concourse import mybir
from contextlib import ExitStack

F32 = mybir.dt.float32
BF16 = mybir.dt.bfloat16
I32 = mybir.dt.int32
U32 = mybir.dt.uint32
I16 = mybir.dt.int16
ALU = mybir.AluOpType
ACT = mybir.ActivationFunctionType
AX = mybir.AxisListType

P = 128
T = 2048
NT = T // P
H = 256
CT = H // P
EPS = 1e-5

NH, HD = 16, 16
HG = 4
NG = NH // HG
HALF = 64
TP = T + 2 * HALF
SLOTS = 64
VW = 32
SUM = HD
COMBOS = [(0, 0), (0, 1), (0, 2), (1, 0), (1, 1), (2, 0)]
KS = len(COMBOS) * HD
PADROW = KS
KMAX, KALL = KS + 1, KS + 4
PAD_SCORE = -1e30


class Shared:
    pass


class Tally:

    def __init__(self, sem):
        self.sem, self.n = sem, 0

    def mark(self, ins):
        ins.then_inc(self.sem, 1)
        self.n = self.n + 1
        return self.n

    def done(self, eng):
        eng.wait_ge(self.sem, self.n)


def residual_and_stats(nc, g, y, first, name, out=None):
    with ExitStack() as ctx:
        sem = lambda n: nc.alloc_semaphore(f"{name}_{n}")
        sb = lambda n, s, d=F32: ctx.enter_context(nc.sbuf_tensor(f"{name}_{n}", s, d))
        stats = sb("stats", [P, NT, 6])
        mv = sb("mv", [P, NT, 2])
        ve = sb("ve", [P, NT])
        sd = sb("sd", [P, NT])
        shift = sb("shift", [P, NT])
        chain, y_var, y_sd, y_scale, y_norm, x_new, x_var, x_sd, stored = [
            sem(n) for n in ("chain", "y_var", "y_sd", "y_scale", "y_norm", "x_new", "x_var", "x_sd", "stored")]
        with nc.Block() as block:

            @block.vector
            def _(dve):
                own = Tally(chain)

                def finish(var_sem, sd_sem):
                    own.done(dve)
                    for t in range(NT):
                        own.mark(dve.bn_aggr(mv[:, t, :], stats[:, t, :]))
                    own.done(dve)
                    dve.tensor_scalar(ve[:, :], mv[:, :, 1], EPS, None, ALU.add).then_inc(var_sem, 1)
                    own.mark(dve.tensor_copy(g.mean[:, :], mv[:, :, 0]))
                    dve.wait_ge(sd_sem, 1)
                    own.mark(dve.reciprocal(g.rstd[:, :], sd[:, :]))
                    own.done(dve)

                if not first:
                    with dve.Fori(0, NT // 4) as b:
                        for t in range(4):
                            dve.bn_stats(stats[:, b * 4 + t, :], y[:, b * 4 + t, :]).then_inc(chain, 1)
                    own.n = NT
                    finish(y_var, y_sd)
                    dve.scalar_tensor_tensor(out=shift[:, :], in0=g.mean[:, :], scalar=-1.0, in1=g.rstd[:, :],
                                             op0=ALU.mult, op1=ALU.mult).then_inc(y_scale, 1)
                    with dve.Fori(0, NT // 4) as b:
                        for t in range(4):
                            dve.wait_ge(y_norm, b * 4 + t + 1)
                            dve.tensor_tensor(g.x[:, b * 4 + t, :], g.x[:, b * 4 + t, :], y[:, b * 4 + t, :],
                                              ALU.add).then_inc(x_new, 1)
                        if out is None:
                            dve.wait_ge(x_new, b * 4 + 4)
                            for t in range(4):
                                dve.bn_stats(stats[:, b * 4 + t, :], g.x[:, b * 4 + t, :]).then_inc(chain, 1)
                else:
                    with dve.Fori(0, NT // 4) as b:
                        for t in range(4):
                            dve.bn_stats(stats[:, b * 4 + t, :], g.x[:, b * 4 + t, :]).then_inc(chain, 1)
                if out is None:
                    own.n += NT
                    finish(x_var, x_sd)

            if out is not None:
                @block.sync
                def _(sp):
                    for q in range(4):
                        sp.wait_ge(x_new, (q + 1) * NT // 4)
                        sp.dma_start(out.rearrange("a (t p) c -> p (a t) c", p=P)[:, q * NT // 4:(q + 1) * NT // 4, :],
                                     g.x[:, q * NT // 4:(q + 1) * NT // 4, :]).then_inc(stored, 16)
                    sp.wait_ge(stored, 64)

            @block.scalar
            def _(act):
                if not first:
                    act.wait_ge(y_var, 1)
                    act.activation(sd[:, :], ve[:, :], ACT.Sqrt).then_inc(y_sd, 1)
                    act.wait_ge(y_scale, 1)
                    with act.Fori(0, NT // 4) as b:
                        for u in range(4):
                            t = b * 4 + u
                            act.activation(y[:, t, :], y[:, t, :], ACT.Identity, bias=shift[:, bass.ds(t, 1)],
                                           scale=g.rstd[:, bass.ds(t, 1)]).then_inc(y_norm, 1)
                if out is None:
                    act.wait_ge(x_var, 1)
                    act.activation(sd[:, :], ve[:, :], ACT.Sqrt).then_inc(x_sd, 1)


def constants(nc, g, hidden):
    with ExitStack() as ctx:
        zeroed, made, loaded = [nc.alloc_semaphore(f"const_{n}")
                                for n in ("zeroed", "made", "loaded")]
        with nc.Block() as block:
            @block.gpsimd
            def _(pool):
                pool.memset(g.ident[:, :], 0.0).then_inc(zeroed, 1)
                pool.wait_ge(zeroed, 1)
                pool.affine_select(out=g.ident[:, :], in_=g.ident[:, :], compare_op=ALU.not_equal,
                                   fill=1.0, base=0, pattern=[[-1, P]],
                                   channel_multiplier=1).then_inc(made, 1)
                pool.wait_ge(made, 1)
                pool.tensor_copy(g.identb[:, :], g.ident[:, :]).then_inc(made, 1)

            @block.sync
            def _(sp):
                sp.dma_start(g.x[:, :, :], hidden.rearrange("a (t p) c -> p (a t) c", p=P)).then_inc(loaded, 16)
                sp.wait_ge(loaded, 16)


def project(nc, g, Wq, bq, Wk, bk, Wv, bv):
    with ExitStack() as ctx:
        sem = lambda n: nc.alloc_semaphore(f"proj_{n}")
        sb = lambda n, s, d=F32: ctx.enter_context(nc.sbuf_tensor(f"proj_{n}", s, d))
        pb = lambda n, s, d=F32: ctx.enter_context(nc.psum_tensor(f"proj_{n}", s, d))
        w = sb("w", [P, 3, CT, H])
        bqk = sb("bqk", [P, 2 * CT])
        bvb = sb("bvb", [P, H])
        heads = sb("heads", [P, CT, NH])
        xn = sb("xn", [P, 2, H])
        xnT = sb("xnT", [P, 2, CT, P])
        qkf = sb("qkf", [P, 2, 2 * CT, P])
        rest = sb("rest", [P, 2, 2 * CT, P])
        parts = sb("parts", [P, 3, 2 * CT, T], BF16)
        sq = sb("sq", [P, 2, CT, P])
        vrow = sb("vrow", [P, 2, NH, VW])
        qrow = sb("qrow", [P, 2, H])
        zero = sb("zero", [HALF, NH * VW])
        psT = pb("psT", [P, 2, H])
        psQK = pb("psQK", [P, 2, 2 * CT * P])
        psV = pb("psV", [P, 2, H])
        psR = pb("psR", [P, 2, H])
        psN = pb("psN", [NH, 2, 2 * H])
        (loaded, preset, normed, turned, xT_ready, qk_done, v_done, qk_ready, part1, rest1, part2,
         part3, squared, norm_done, norms_copied, v_ready, qT_done, q_ready, zeroed) = [sem(n) for n in (
             "loaded", "preset", "normed", "turned", "xT_ready", "qk_done", "v_done", "qk_ready",
             "part1", "rest1", "part2", "part3", "squared", "norm_done", "norms_copied", "v_ready",
             "qT_done", "q_ready", "zeroed")]
        parts_out = sem("parts_out")
        v_out = [sem(f"v_out{u}") for u in range(2)]
        q_out = [sem(f"q_out{u}") for u in range(2)]
        pads_out = sem("pads_out")
        NLOAD = 3 + 2 + 1
        with nc.Block() as block:

            @block.sync
            def _(sp):
                for i, m in enumerate((Wq, Wk, Wv)):
                    sp.dma_start(w[:, i, :, :], m.rearrange("(c p) n -> p c n", p=P)).then_inc(loaded, 16)
                for i, m in enumerate((bq, bk)):
                    sp.dma_start(bqk[:, CT * i:CT * (i + 1)], m.rearrange("(c p) -> p c", p=P), allow_slow_non_contiguous=True
                                 ).then_inc(loaded, 16)
                sp.dma_start(bvb[:, :], bv.rearrange("(a n) -> a n", a=1).to_broadcast([P, H])).then_inc(loaded, 16)
                sp.wait_ge(zeroed, 1)
                sp.dma_start(g.v_dram[0:HALF, :], zero[:, :]).then_inc(pads_out, 16)
                sp.dma_start(g.v_dram[HALF + T:TP, :], zero[:, :]).then_inc(pads_out, 16)
                with sp.Fori(0, NT // 2) as b:
                    for u in range(2):
                        t = 2 * b + u
                        sp.wait_ge(q_ready, t + 1)
                        sp.dma_start(g.q_dram[bass.ds(t * P, P), :], qrow[:, u, :]).then_inc(q_out[u], 16)
                        sp.wait_ge(v_ready, t + 1)
                        sp.dma_start(g.v_dram[bass.ds(t * P + HALF, P), :],
                                     vrow[:, u, :, :].rearrange("p h w -> p (h w)")).then_inc(v_out[u], 16)
                    sp.wait_ge(part3, 2 * b + 2)
                    for i in range(3):
                        sp.dma_start(
                            g.qk_dram[i, :, bass.ds(b * 2 * P, 2 * P)].rearrange("(m p) n -> p m n", p=P),
                            parts[:, i, :, bass.ds(b * 2 * P, 2 * P)]).then_inc(parts_out, 16)
                for s in (*q_out, *v_out):
                    sp.wait_ge(s, 16 * NT // 2)
                sp.wait_ge(parts_out, 16 * 3 * NT // 2)
                sp.wait_ge(pads_out, 32)

            @block.gpsimd
            def _(pool):
                pool.memset(heads[:, :, :], 1.0).then_inc(preset, 1)
                pool.wait_ge(preset, 1)
                pool.affine_select(out=heads[:, :, :], in_=heads[:, :, :], compare_op=ALU.is_ge, fill=0.0,
                                   base=0, pattern=[[P, CT], [-HD, NH]], channel_multiplier=1).then_inc(preset, 1)
                pool.wait_ge(preset, 2)
                pool.affine_select(out=heads[:, :, :], in_=heads[:, :, :], compare_op=ALU.is_ge, fill=0.0,
                                   base=HD - 1, pattern=[[-P, CT], [HD, NH]], channel_multiplier=-1).then_inc(preset, 1)
                pool.memset(vrow[:, :, :, :], 0.0).then_inc(preset, 1)
                pool.wait_ge(preset, 4)
                pool.memset(vrow[:, :, :, SUM:SUM + 1], 1.0).then_inc(preset, 1)
                pool.memset(zero[:, :], 0.0).then_inc(zeroed, 1)
                with pool.Fori(0, NT // 2) as b:
                    for u in range(2):
                        t = 2 * b + u
                        pool.wait_ge(qk_ready, t + 1)
                        pool.wait_ge(part1, t + 1)
                        pool.wait_ge(part2, 2 * b)
                        pool.wait_ge(part3, 2 * b)
                        pool.tensor_tensor(rest[:, u, :, :], qkf[:, u, :, :],
                                           parts[:, 0, :, bass.ds(t * P, P)], ALU.subtract).then_inc(rest1, 1)
                        pool.wait_ge(part2, t + 1)
                        pool.wait_ge(rest1, t + 1)
                        pool.tensor_tensor(parts[:, 2, :, bass.ds(t * P, P)], rest[:, u, :, :],
                                           parts[:, 1, :, bass.ds(t * P, P)], ALU.subtract).then_inc(part3, 1)

            @block.vector
            def _(dve):
                dve.wait_ge(loaded, 16 * NLOAD)
                dve.wait_ge(preset, 5)
                with dve.Fori(0, NT // 2) as b:
                    for u in range(2):
                        t = 2 * b + u
                        dve.wait_ge(turned, 2 * b)
                        dve.tensor_scalar(xn[:, u, :], g.x[:, t, :], g.mean[:, bass.ds(t, 1)],
                                          g.rstd[:, bass.ds(t, 1)], ALU.subtract,
                                          ALU.mult).then_inc(normed, 1)
                        dve.wait_ge(qk_done, t + 1)
                        dve.wait_ge(squared, 2 * b)
                        dve.wait_ge(rest1, 2 * b)
                        dve.wait_ge(qT_done, 2 * b)
                        dve.tensor_tensor(
                            qkf[:, u, :, :], psQK[:, u, :].rearrange("p (m n) -> p m n", n=P),
                            bqk[:, :].unsqueeze(2).to_broadcast([P, 2 * CT, P]), ALU.add).then_inc(qk_ready, 1)
                        dve.wait_ge(v_done, t + 1)
                        dve.wait_ge(v_out[u], 16 * b)
                        dve.tensor_tensor(
                            vrow[:, u, :, 0:HD], psV[:, u, :].rearrange("p (h d) -> p h d", d=HD),
                            bvb[:, :].rearrange("p (h d) -> p h d", d=HD), ALU.add).then_inc(v_ready, 1)
                        dve.wait_ge(norm_done, t + 1)
                        dve.tensor_copy(g.norms[:, bass.ds(t * P, P)], psN[:, u, 0:P]).then_inc(norms_copied, 1)

            @block.scalar
            def _(act):
                with act.Fori(0, NT // 2) as b:
                    for u in range(2):
                        t = 2 * b + u
                        act.wait_ge(turned, t + 1)
                        act.wait_ge(v_done, 2 * b)
                        act.activation(xnT[:, u, :, :].rearrange("p c n -> p (c n)"), psT[:, u, :],
                                       ACT.Copy).then_inc(xT_ready, 1)
                        act.wait_ge(qk_ready, t + 1)
                        act.activation(parts[:, 0, :, bass.ds(t * P, P)], qkf[:, u, :, :], ACT.Copy).then_inc(part1, 1)
                        act.wait_ge(norm_done, 2 * b)
                        act.activation(sq[:, u, :, :], qkf[:, u, 0:CT, :], ACT.Square).then_inc(squared, 1)
                        act.wait_ge(rest1, t + 1)
                        act.activation(parts[:, 1, :, bass.ds(t * P, P)], rest[:, u, :, :], ACT.Copy).then_inc(part2, 1)
                        act.wait_ge(qT_done, t + 1)
                        act.wait_ge(q_out[u], 16 * b)
                        act.activation(qrow[:, u, :], psR[:, u, :], ACT.Copy).then_inc(q_ready, 1)

            @block.tensor
            def _(pe):
                pe.wait_ge(loaded, 16 * NLOAD)
                pe.wait_ge(preset, 5)
                with pe.Fori(0, NT // 2) as b:
                    for u in range(2):
                        t = 2 * b + u
                        pe.wait_ge(normed, t + 1)
                        pe.wait_ge(xT_ready, 2 * b)
                        for c in range(CT):
                            mm = pe.transpose(psT[:, u, c * P:(c + 1) * P], xn[:, u, c * P:(c + 1) * P],
                                              g.ident[:, :])
                        mm.then_inc(turned, 1)
                        pe.wait_ge(xT_ready, t + 1)
                        pe.wait_ge(qk_ready, 2 * b)
                        for m in range(2 * CT):
                            for c in range(CT):
                                mm = pe.matmul(psQK[:, u, m * P:(m + 1) * P],
                                               w[:, m // CT, c, (m % CT) * P:(m % CT + 1) * P],
                                               xnT[:, u, c, :], start=(c == 0), stop=(c == CT - 1))
                        mm.then_inc(qk_done, 1)
                        pe.wait_ge(v_ready, 2 * b)
                        for c in range(CT):
                            mm = pe.matmul(psV[:, u, :], xnT[:, u, c, :], w[:, 2, c, :],
                                           start=(c == 0), stop=(c == CT - 1))
                        mm.then_inc(v_done, 1)
                        pe.wait_ge(squared, t + 1)
                        pe.wait_ge(norms_copied, 2 * b)
                        for c in range(CT):
                            mm = pe.matmul(psN[:, u, 0:P], heads[:, c, :], sq[:, u, c, :],
                                           start=(c == 0), stop=(c == CT - 1))
                        mm.then_inc(norm_done, 1)
                        pe.wait_ge(q_ready, 2 * b)
                        for c in range(CT):
                            mm = pe.transpose(psR[:, u, c * P:(c + 1) * P], qkf[:, u, c, :], g.ident[:, :])
                        mm.then_inc(qT_done, 1)

def pick_queries(nc, g):
    with ExitStack() as ctx:
        sem = lambda n: nc.alloc_semaphore(f"pick_{n}")
        sb = lambda n, s, d=F32: ctx.enter_context(nc.sbuf_tensor(f"pick_{n}", s, d))
        pb = lambda n, s, d=F32: ctx.enter_context(nc.psum_tensor(f"pick_{n}", s, d))
        top = sb("top", [NH, 8])
        idx = sb("idx", [NH, SLOTS], U32)
        idxf = sb("idxf", [NH, SLOTS])
        hrow = sb("hrow", [SLOTS, NH])
        gq = sb("gq", [SLOTS, NH, HD])
        gp = sb("gp", [P, 3, CT, SLOTS], BF16)
        gf = sb("gf", [P, CT, SLOTS])
        gr = sb("gr", [P, CT, SLOTS])
        psI = pb("psI", [SLOTS, 512])
        psQ = pb("psQ", [P, 512])
        (own, found, turned, hrow_ready, placed, gathered, q_turned, split, stored) = [sem(n) for n in (
            "own", "found", "turned", "hrow_ready", "placed", "gathered", "q_turned", "split", "stored")]
        with nc.Block() as block:

            @block.vector
            def _(dve):
                me = Tally(own)
                for r in range(SLOTS // 8):
                    me.mark(dve.max(top[:, :], g.norms[:, :]))
                    me.done(dve)
                    me.mark(dve.max_index(idx[:, 8 * r:8 * r + 8], top[:, :], g.norms[:, :]))
                    me.done(dve)
                    if r < SLOTS // 8 - 1:
                        me.mark(dve.match_replace(out=g.norms[:, :], in_to_replace=top[:, :],
                                                  in_values=g.norms[:, :], imm_value=-1.0))
                        me.done(dve)
                me.mark(dve.tensor_copy(idxf[:, :], idx[:, :]))
                me.done(dve)
                me.mark(dve.memset(idxf[:, SLOTS - 2:SLOTS - 1], 0.0))
                me.done(dve)
                dve.memset(idxf[:, SLOTS - 1:SLOTS], float(T - 1)).then_inc(found, 1)
                dve.wait_ge(turned, 1)
                dve.wait_ge(hrow_ready, 1)
                dve.scalar_tensor_tensor(out=g.places[:, :], in0=psI[:, 0:NH], scalar=float(NH),
                                         in1=hrow[:, :], op0=ALU.mult, op1=ALU.add).then_inc(placed, 1)
                dve.wait_ge(q_turned, 1)
                src = psQ[:, 0:CT * SLOTS].rearrange("p (c s) -> p c s", s=SLOTS)
                me.mark(dve.tensor_copy(gf[:, :, :], src))
                me.done(dve)
                me.mark(dve.tensor_copy(gp[:, 0, :, :], gf[:, :, :]))
                me.done(dve)
                me.mark(dve.tensor_tensor(gr[:, :, :], gf[:, :, :], gp[:, 0, :, :], ALU.subtract))
                me.done(dve)
                me.mark(dve.tensor_copy(gp[:, 1, :, :], gr[:, :, :]))
                me.done(dve)
                dve.tensor_tensor(gp[:, 2, :, :], gr[:, :, :], gp[:, 1, :, :], ALU.subtract).then_inc(split, 1)

            @block.gpsimd
            def _(pool):
                pool.iota(hrow[:, :], pattern=[[1, NH]], base=0, channel_multiplier=0,
                          allow_small_or_imprecise_dtypes=True).then_inc(hrow_ready, 1)
                pool.wait_ge(placed, 1)
                for h in range(NH):
                    pool.indirect_dma_start(
                        out=gq[:, h, :], out_offset=None,
                        in_=g.q_dram.rearrange("t (h d) -> (t h) d", d=HD),
                        in_offset=bass.IndirectOffsetOnAxis(ap=g.places[:, h:h + 1], axis=0)).then_inc(gathered, 16)

            @block.tensor
            def _(pe):
                pe.wait_ge(found, 1)
                pe.transpose(psI[:, 0:NH], idxf[:, :], g.ident[0:NH, 0:NH]).then_inc(turned, 1)
                pe.wait_ge(gathered, 16 * NH)
                rows = gq[:, :, :].rearrange("s h d -> s (h d)")
                for c in range(CT):
                    mm = pe.transpose(psQ[:, c * SLOTS:(c + 1) * SLOTS], rows[:, c * P:(c + 1) * P],
                                      g.ident[0:SLOTS, 0:SLOTS])
                mm.then_inc(q_turned, 1)

            @block.sync
            def _(sp):
                sp.wait_ge(split, 1)
                for i in range(3):
                    sp.dma_start(g.gq_dram[i, :, :].rearrange("(c p) s -> p c s", p=P),
                                 gp[:, i, :, :]).then_inc(stored, 16)
                sp.wait_ge(stored, 48)


def load_stack(sp, dst, source, which, width, cols, sem):
    for c, combo in enumerate(COMBOS):
        sp.dma_start(dst[c * HD:(c + 1) * HD, :, cols:cols + width],
                     source[combo[which], :, :, :].rearrange("h d n -> d h n")).then_inc(sem, 16)


def stack_constants(eng, kst, own):
    for s in range(2):
        for rows, cols, value in (((0, PADROW), (0, HALF), 0.0), ((0, PADROW), (HALF + T, TP), 0.0),
                                  ((PADROW, KALL), (0, TP), 1.0), ((PADROW, KMAX), (0, TP), 0.0),
                                  ((PADROW, KMAX), (0, HALF), PAD_SCORE),
                                  ((PADROW, KMAX), (HALF + T, TP), PAD_SCORE)):
            own.mark(eng.memset(kst[rows[0]:rows[1], s, :, cols[0]:cols[1]], value))
            own.done(eng)


NB = NT
PRE = 8
VR = 4


def before(n0, i):
    return n0 + (max(i, 0) if isinstance(i, int) else i)


def head_groups(eng, step, lag, each=None):
    with eng.Fori(0, NG // 2) as hp:
        for e in range(2):
            n0 = hp * (2 * NB) + e * NB
            if each is not None:
                each(hp, e, n0)
            for i in range(PRE):
                step(e, n0, i, i, [k for k in range(lag + 1) if k <= i])
            with eng.Fori(PRE // 4, NB // 4) as b:
                for j in range(4):
                    step(e, n0, b * 4 + j, j, list(range(lag + 1)))
            for i in range(NB, NB + lag):
                step(e, n0, i, i, [k for k in range(lag + 1) if k > i - NB])


def local_attention(nc, g):
    with ExitStack() as ctx:
        sem = lambda n: nc.alloc_semaphore(f"loc_{n}")
        sb = lambda n, s, d=F32: ctx.enter_context(nc.sbuf_tensor(f"loc_{n}", s, d))
        pb = lambda n, s, d=F32: ctx.enter_context(nc.psum_tensor(f"loc_{n}", s, d))
        kst = g.kst
        qst = sb("qst", [KALL, 2, HG, T], BF16)
        nmax = sb("nmax", [P, 2, HG])
        mrest = sb("mrest", [P, 2, HG])
        zero = sb("zero", [P, HG])
        mparts = sb("mparts", [P, 2, HG, 4], BF16)
        probs = sb("probs", [P, 2, HG, 2, P])
        vt = sb("vt", [P, VR, 2, HG * VW])
        oT = sb("oT", [P, 2, P])
        rden = sb("rden", [P, 2, HG])
        cx = sb("cx", [P, 2, HG, HD])
        psS = pb("psS", [P, 2, HG, 2 * P])
        psX = pb("psX", [P, HG, 2, P])
        psM = pb("psM", [P, HG * P])
        psO = pb("psO", [P, 4 * P])
        (own, preset, scored, maxed, mchain, split, rows_done, rows_copied, x_done, exp_done, pv_done,
         oT_copied, back, den_ready, cx_ready) = [sem(n) for n in (
             "own", "preset", "scored", "maxed", "mchain", "split", "rows_done", "rows_copied", "x_done",
             "exp_done", "pv_done", "oT_copied", "back", "den_ready", "cx_ready")]
        stacked = [sem(f"stacked{e}") for e in range(2)]
        v_in = [sem(f"v_in{s}") for s in range(VR)]
        cx_out = [sem(f"cx_out{s}") for s in range(2)]
        kq = g.qk_dram.rearrange("i (m h d) t -> i m h d t", m=2, d=HD)

        def turned(i, j):
            return psS[:, (j - 1) % 2, 0, 0:P].rearrange("p (h w) -> p h w", w=VW)

        with nc.Block() as block:

            @block.sync
            def _(sp):
                def stacks(e, h0):
                    load_stack(sp, qst[:, e, :, :], kq[:, 0, h0, :, :], 0, T, 0, stacked[e])
                    load_stack(sp, kst[:, e, :, :], kq[:, 1, h0, :, :], 1, T, HALF, stacked[e])

                def next_stacks(hp, e, n0):
                    sp.wait_ge(x_done, n0)
                    if e == 0:
                        stacks(1, bass.ds(hp * (2 * HG) + HG, HG))
                    else:
                        stacks(0, bass.ds(((hp + 1) % (NG // 2)) * (2 * HG), HG))
                    hg[0] = (hp * 2 + e) * HG

                hg = [0]

                def step(e, n0, i, j, live):
                    if 0 in live:
                        sp.wait_ge(pv_done, before(n0, i - 3))
                        sp.dma_start(vt[:, j % VR, :, :],
                                     g.v_dram[bass.ds(i * P, 2 * P), bass.ds(hg[0] * VW, HG * VW)]
                                     .rearrange("(k p) n -> p k n", p=P)).then_inc(v_in[j % VR], 16)
                    if 5 in live:
                        s = (j - 5) % 2
                        sp.wait_ge(cx_ready, n0 + i - 4)
                        sp.dma_start(g.c_dram[bass.ds((i - 5) * P, P), bass.ds(hg[0] * HD, HG * HD)],
                                     cx[:, s, :, :].rearrange("p h d -> p (h d)")).then_inc(cx_out[s], 16)
                stacks(0, slice(0, HG))
                head_groups(sp, step, 5, next_stacks)
                for s in cx_out:
                    sp.wait_ge(s, 16 * NG * NB // 2)
                sp.wait_ge(stacked[0], 16 * 12 * 3)
                sp.wait_ge(stacked[1], 16 * 12 * 2)

            @block.gpsimd
            def _(pool):
                me = Tally(own)
                me.mark(pool.memset(zero[:, :], 0.0))
                me.done(pool)
                for s in range(2):
                    me.mark(pool.memset(qst[PADROW:KALL, s, :, :], 1.0))
                    me.done(pool)
                    me.mark(pool.memset(mparts[:, s, :, :], 1.0))
                    me.done(pool)
                stack_constants(pool, kst, me)
                pool.sem_inc(preset, 1)

                def step(e, n0, i, j, live):
                    s = j % 2
                    pool.wait_ge(maxed, n0 + i + 1)
                    pool.wait_ge(rows_done, before(n0, i - 1))
                    at = (n0 + i) * 3
                    pool.tensor_tensor(mparts[:, s, :, 1], nmax[:, s, :], zero[:, :], ALU.add).then_inc(mchain, 1)
                    pool.wait_ge(mchain, at + 1)
                    pool.tensor_tensor(mrest[:, s, :], nmax[:, s, :], mparts[:, s, :, 1],
                                       ALU.subtract).then_inc(mchain, 1)
                    pool.wait_ge(mchain, at + 2)
                    pool.tensor_tensor(mparts[:, s, :, 2], mrest[:, s, :], zero[:, :], ALU.add).then_inc(mchain, 1)
                    pool.wait_ge(mchain, at + 3)
                    pool.tensor_tensor(mparts[:, s, :, 3], mrest[:, s, :], mparts[:, s, :, 2],
                                       ALU.subtract).then_inc(split, 1)
                head_groups(pool, step, 0)

            @block.vector
            def _(dve):
                def step(e, n0, i, j, live):
                    if 0 in live:
                        s = j % 2
                        dve.wait_ge(scored, n0 + i + 1)
                        dve.wait_ge(split, before(n0, i - 1))
                        dve.tensor_reduce(out=nmax[:, s, :], in_=psS[:, s, :, :], axis=AX.X, op=ALU.max,
                                          negate=True).then_inc(maxed, 1)
                    if 4 in live:
                        s = (j - 4) % 2
                        c = turned(i, j)
                        dve.wait_ge(back, n0 + i - 3)
                        dve.reciprocal(rden[:, s, :], c[:, :, SUM]).then_inc(den_ready, 1)
                        dve.wait_ge(den_ready, n0 + i - 3)
                        dve.wait_ge(cx_out[s], (n0 + i - 4 - s) * 8)
                        dve.tensor_tensor(cx[:, s, :, :], c[:, :, 0:HD],
                                          rden[:, s, :].unsqueeze(2).to_broadcast([P, HG, HD]),
                                          ALU.mult).then_inc(cx_ready, 1)
                head_groups(dve, step, 4)

            @block.scalar
            def _(act):
                def step(e, n0, i, j, live):
                    if 1 in live:
                        act.wait_ge(rows_done, n0 + i)
                        act.activation(qst[PADROW:KALL, e, :, bass.ds((i - 1) * P, P)],
                                       psM[PADROW:KALL, :].rearrange("p (h n) -> p h n", n=P),
                                       ACT.Copy).then_inc(rows_copied, 1)
                    if 2 in live:
                        s = (j - 2) % 2
                        act.wait_ge(x_done, n0 + i - 1)
                        act.wait_ge(pv_done, before(n0, i - 3))
                        act.activation(probs[:, s, :, :, :], psX[:, :, :, :], ACT.Exp,
                                       scale=HD ** -0.5).then_inc(exp_done, 1)
                    if 3 in live:
                        s = (j - 3) % 2
                        act.wait_ge(pv_done, n0 + i - 2)
                        act.wait_ge(back, before(n0, i - 4))
                        act.activation(oT[:, s, :], psO[:, 0:P], ACT.Copy).then_inc(oT_copied, 1)
                head_groups(act, step, 3)

            @block.tensor
            def _(pe):
                pe.wait_ge(preset, 1)

                def arrived(hp, e, n0):
                    pe.wait_ge(stacked[e], hp * (12 * 16) + 12 * 16)

                def step(e, n0, i, j, live):
                    if 0 in live:
                        s = j % 2
                        pe.wait_ge(maxed, before(n0, i - 1))
                        pe.wait_ge(cx_ready, before(n0, i - 4))
                        for h in range(HG):
                            mm = pe.matmul(psS[:, s, h, :], qst[0:KMAX, e, h, bass.ds(i * P, P)],
                                           kst[0:KMAX, e, h, bass.ds(i * P, 2 * P)], start=True, stop=True)
                        mm.then_inc(scored, 1)
                    if 1 in live:
                        s = (j - 1) % 2
                        pe.wait_ge(split, n0 + i)
                        pe.wait_ge(rows_copied, n0 + i - 1)
                        for h in range(HG):
                            mm = pe.matmul(psM[PADROW:KALL, h * P:(h + 1) * P], mparts[:, s, h, :],
                                           g.identb[:, :], start=True, stop=True)
                        mm.then_inc(rows_done, 1)
                    if 4 in live:
                        s = (j - 4) % 2
                        pe.wait_ge(oT_copied, n0 + i - 3)
                        pe.wait_ge(maxed, n0 + min(i, NB) if isinstance(i, int) else n0 + i)
                        pe.wait_ge(cx_ready, before(n0, i - 5))
                        pe.transpose(psS[:, (j - 1) % 2, 0, 0:P], oT[:, s, :], g.ident[:, :]).then_inc(back, 1)
                    if 2 in live:
                        pe.wait_ge(rows_copied, n0 + i - 1)
                        pe.wait_ge(exp_done, n0 + i - 2)
                        for h in range(HG):
                            for k in range(2):
                                mm = pe.matmul(psX[:, h, k, :],
                                               kst[0:KALL, e, h, bass.ds((i - 2) * P + k * P, P)],
                                               qst[0:KALL, e, h, bass.ds((i - 2) * P, P)],
                                               start=True, stop=True)
                        mm.then_inc(x_done, 1)
                    if 3 in live:
                        s = (j - 3) % 2
                        r = (j - 3) % VR
                        pe.wait_ge(exp_done, n0 + i - 2)
                        pe.wait_ge(v_in[r], (n0 + i - 3 - r) * (16 // VR) + 16)
                        pe.wait_ge(oT_copied, n0 + i - 3)
                        for k in range(2):
                            for h in range(HG):
                                mm = pe.matmul(psO[h * VW:(h + 1) * VW, 0:P],
                                               vt[:, r, k, h * VW:(h + 1) * VW],
                                               probs[:, s, h, k, :], start=(k == 0), stop=(k == 1),
                                               skip_group_check=True)
                        mm.then_inc(pv_done, 1)
                head_groups(pe, step, 4, arrived)


def global_attention(nc, g):
    PAIRS = HG // 2
    with ExitStack() as ctx:
        sem = lambda n: nc.alloc_semaphore(f"glo_{n}")
        sb = lambda n, s, d=F32: ctx.enter_context(nc.sbuf_tensor(f"glo_{n}", s, d))
        pb = lambda n, s, d=F32: ctx.enter_context(nc.psum_tensor(f"glo_{n}", s, d))
        kst = g.kst
        gst = sb("gst", [KALL, 2, HG, SLOTS], BF16)
        nmax = sb("nmax", [P, 2])
        mrest = sb("mrest", [P, 2])
        zero = sb("zero", [P, 1])
        mparts = sb("mparts", [P, 2, 4], BF16)
        probs = sb("probs", [P, 2, NT, SLOTS])
        vt = sb("vt", [P, 2, NT, HG * VW])
        oT = sb("oT", [P, P])
        rden = sb("rden", [SLOTS, HG])
        gcx = sb("gcx", [SLOTS, NH, HD])
        psS = pb("psS", [P, T])
        psX = pb("psX", [P, NT, SLOTS])
        psM = pb("psM", [P, 4 * P])
        psO = pb("psO", [P, 4 * P])
        (own, preset, scored, maxed, mchain, split, rows_done, rows_copied, x_done, exp_done, pv_done,
         oT_copied, back, den_ready, cx_ready, swapped, ends_out) = [sem(n) for n in (
             "own", "preset", "scored", "maxed", "mchain", "split", "rows_done", "rows_copied", "x_done",
             "exp_done", "pv_done", "oT_copied", "back", "den_ready", "cx_ready", "swapped", "ends_out")]
        stacked = [sem(f"stacked{e}") for e in range(2)]
        v_in = [sem(f"v_in{e}") for e in range(2)]
        g_in = [sem(f"g_in{e}") for e in range(2)]
        kq = g.qk_dram.rearrange("i (m h d) t -> i m h d t", m=2, d=HD)

        with nc.Block() as block:

            @block.sync
            def _(sp):
                def v_tiles(e, cols):
                    sp.dma_start(vt[:, e, :, :], g.v_dram[HALF:HALF + T, cols]
                                 .rearrange("(k p) n -> p k n", p=P)).then_inc(v_in[e], 16)
                v_tiles(0, slice(0, HG * VW))
                sp.wait_ge(preset, 1)
                gq = g.gq_dram.rearrange("i (h d) s -> i h d s", d=HD)
                load_stack(sp, gst[:, 0, :, :], gq[:, 0:HG, :, :], 0, SLOTS, 0, g_in[0])
                with sp.Fori(0, NG // 2) as hp:
                    for e in range(2):
                        hg = hp * 2 + e
                        sp.wait_ge(pv_done, hg * HG)
                        nxt = (hp * 2 + 1) if e == 0 else ((hp + 1) % (NG // 2)) * 2
                        load_stack(sp, kst[:, 1 - e, :, :], kq[:, 1, bass.ds(nxt * HG, HG), :, :], 1, T, HALF,
                                   stacked[1 - e])
                        load_stack(sp, gst[:, 1 - e, :, :], gq[:, bass.ds(nxt * HG, HG), :, :], 0, SLOTS, 0,
                                   g_in[1 - e])
                        v_tiles(1 - e, bass.ds(nxt * (HG * VW), HG * VW))
                sp.wait_ge(stacked[0], 16 * 6 * NG // 2)
                sp.wait_ge(g_in[0], 16 * 6 * (NG // 2 + 1))
                sp.wait_ge(v_in[0], 16 * (NG // 2 + 1))
                sp.wait_ge(swapped, 16 * NH)
                for s, t in ((SLOTS - 2, 0), (SLOTS - 1, T - 1)):
                    sp.dma_start(g.c_dram[t:t + 1, :], gcx[s:s + 1, :, :].rearrange("s h d -> s (h d)")
                                 ).then_inc(ends_out, 16)
                sp.wait_ge(ends_out, 32)

            @block.gpsimd
            def _(pool):
                pool.memset(zero[:, :], 0.0).then_inc(own, 1)
                pool.wait_ge(own, 1)
                pool.memset(oT[:, :], 0.0).then_inc(own, 1)
                pool.wait_ge(own, 2)
                pool.memset(gst[PADROW:KALL, :, :, :], 1.0).then_inc(own, 1)
                pool.wait_ge(own, 3)
                pool.memset(mparts[:, :, :], 1.0).then_inc(preset, 1)
                with pool.Fori(0, NG // 2) as hp:
                    for e in range(2):
                        for s in range(PAIRS):
                            n = hp * (2 * PAIRS) + e * PAIRS + s
                            pool.wait_ge(maxed, n + 1)
                            pool.wait_ge(rows_done, hp * (2 * PAIRS) + e * PAIRS)
                            pool.tensor_tensor(mparts[:, s, 1:2], nmax[:, s:s + 1], zero[:, :], ALU.add).then_inc(mchain, 1)
                            pool.wait_ge(mchain, n * 3 + 1)
                            pool.tensor_tensor(mrest[:, s:s + 1], nmax[:, s:s + 1], mparts[:, s, 1:2],
                                               ALU.subtract).then_inc(mchain, 1)
                            pool.wait_ge(mchain, n * 3 + 2)
                            pool.tensor_tensor(mparts[:, s, 2:3], mrest[:, s:s + 1], zero[:, :],
                                               ALU.add).then_inc(mchain, 1)
                            pool.wait_ge(mchain, n * 3 + 3)
                            pool.tensor_tensor(mparts[:, s, 3:4], mrest[:, s:s + 1], mparts[:, s, 2:3],
                                               ALU.subtract).then_inc(split, 1)
                pool.wait_ge(cx_ready, NG)
                for h in range(NH):
                    pool.indirect_dma_start(
                        out=g.c_dram.rearrange("t (h d) -> (t h) d", d=HD),
                        out_offset=bass.IndirectOffsetOnAxis(ap=g.places[0:SLOTS - 2, h:h + 1], axis=0),
                        in_=gcx[0:SLOTS - 2, h, :], in_offset=None).then_inc(swapped, 16)
                pool.wait_ge(swapped, 16 * NH)

            @block.vector
            def _(dve):
                with dve.Fori(0, NG // 2) as hp:
                    for e in range(2):
                        hg = hp * 2 + e
                        for s in range(PAIRS):
                            dve.wait_ge(scored, hg * PAIRS + s + 1)
                            dve.wait_ge(split, hg * PAIRS)
                            dve.tensor_reduce(out=nmax[:, s:s + 1], in_=psS[:, :], axis=AX.X, op=ALU.max,
                                              negate=True).then_inc(maxed, 1)
                        c = psM[0:SLOTS, 0:P].rearrange("p (h w) -> p h w", w=VW)
                        dve.wait_ge(back, hg + 1)
                        dve.reciprocal(rden[:, :], c[:, :, SUM]).then_inc(den_ready, 1)
                        dve.wait_ge(den_ready, hg + 1)
                        dve.tensor_tensor(gcx[:, bass.ds(hg * HG, HG), :], c[:, :, 0:HD],
                                          rden[:, :].unsqueeze(2).to_broadcast([SLOTS, HG, HD]),
                                          ALU.mult).then_inc(cx_ready, 1)

            @block.scalar
            def _(act):
                with act.Fori(0, NG // 2) as hp:
                    for e in range(2):
                        hg = hp * 2 + e
                        for s in range(PAIRS):
                            act.wait_ge(rows_done, hg * PAIRS + s + 1)
                            act.activation(gst[PADROW:KALL, e, 2 * s:2 * s + 2, :],
                                           psM[PADROW:KALL, 0:P].rearrange("p (h n) -> p h n", n=SLOTS),
                                           ACT.Copy).then_inc(rows_copied, 1)
                            for h in range(2 * s, 2 * s + 2):
                                act.wait_ge(x_done, hg * HG + h + 1)
                                act.wait_ge(pv_done, hg * HG + max(h - 1, 0))
                                act.activation(probs[:, h % 2, :, :], psX[:, :, :], ACT.Exp,
                                               scale=HD ** -0.5).then_inc(exp_done, 1)
                        act.wait_ge(pv_done, hg * HG + HG)
                        act.wait_ge(back, hg)
                        act.activation(oT[:, 0:SLOTS], psO[:, 0:SLOTS], ACT.Copy).then_inc(oT_copied, 1)

            @block.tensor
            def _(pe):
                pe.wait_ge(preset, 1)
                with pe.Fori(0, NG // 2) as hp:
                    for e in range(2):
                        hg = hp * 2 + e
                        if e:
                            pe.wait_ge(stacked[1], (hp + 1) * (16 * 6))
                        else:
                            pe.wait_ge(stacked[0], hp * (16 * 6))
                        pe.wait_ge(v_in[e], (hp + 1) * 16)
                        pe.wait_ge(g_in[e], (hp + 1) * (16 * 6))

                        def scores(s):
                            pe.wait_ge(maxed, hg * PAIRS + s)
                            for h in range(2):
                                for k in range(T // 512):
                                    mm = pe.matmul(psS[h * SLOTS:(h + 1) * SLOTS, k * 512:(k + 1) * 512],
                                                   gst[0:KMAX, e, 2 * s + h, :],
                                                   kst[0:KMAX, e, 2 * s + h, HALF + k * 512:HALF + (k + 1) * 512],
                                                   start=True, stop=True)
                            mm.then_inc(scored, 1)

                        def rows(s):
                            pe.wait_ge(split, hg * PAIRS + s + 1)
                            pe.wait_ge(rows_copied, hg * PAIRS + s)
                            pe.matmul(psM[PADROW:KALL, 0:P], mparts[:, s, :], g.identb[:, :],
                                      start=True, stop=True).then_inc(rows_done, 1)

                        def transposed(h):
                            pe.wait_ge(rows_copied, hg * PAIRS + h // 2 + 1)
                            pe.wait_ge(exp_done, hg * HG + h)
                            for k in range(NT):
                                mm = pe.matmul(psX[:, k, :], kst[0:KALL, e, h, HALF + k * P:HALF + (k + 1) * P],
                                               gst[0:KALL, e, h, :], start=True, stop=True)
                            mm.then_inc(x_done, 1)

                        def values(h):
                            pe.wait_ge(exp_done, hg * HG + h + 1)
                            pe.wait_ge(oT_copied, hg)
                            for k in range(NT):
                                mm = pe.matmul(psO[h * VW:(h + 1) * VW, 0:SLOTS], vt[:, e, k, h * VW:(h + 1) * VW],
                                               probs[:, h % 2, k, :], start=(k == 0), stop=(k == NT - 1))
                            mm.then_inc(pv_done, 1)

                        scores(0)
                        rows(0)
                        scores(1)
                        transposed(0)
                        transposed(1)
                        values(0)
                        rows(1)
                        transposed(2)
                        values(1)
                        transposed(3)
                        values(2)
                        values(3)
                        pe.wait_ge(oT_copied, hg + 1)
                        pe.wait_ge(cx_ready, hg)
                        pe.transpose(psM[:, 0:P], oT[:, :], g.ident[:, :]).then_inc(back, 1)

NE = 8
FI = 512
FT = FI // P
NS = NT + NE - 1


def take_attention(nc, g):
    with ExitStack() as ctx:
        y_in = nc.alloc_semaphore("att_y_in")
        with nc.Block() as block:
            @block.sync
            def _(sp):
                sp.dma_start(g.y[:, :, :], g.c_dram.rearrange("(t p) c -> p t c", p=P)).then_inc(y_in, 16)
                sp.wait_ge(y_in, 16)


def mixture(nc, g, router_w, gate_up, down, shared_gate, shared_up, shared_down):
    with ExitStack() as ctx:
        sem = lambda n: nc.alloc_semaphore(f"moe_{n}")
        sb = lambda n, s, d=F32: ctx.enter_context(nc.sbuf_tensor(f"moe_{n}", s, d))
        wgu = sb("wgu", [P, NE, CT, 2 * FI])
        wd = sb("wd", [P, NE, FT, H])
        sg = sb("sg", [P, CT, FI])
        su = sb("su", [P, CT, FI])
        sd = sb("sd", [P, FT, H])
        xnT = sb("xnT", [P, CT, T])
        xr = sb("xr", [P, NT, H])
        logits = sb("logits", [P, NT, NE])
        experts_in, shared_in, zeros_out = [sem(n) for n in ("experts_in", "shared_in", "zeros_out")]
        router(nc, g, router_w, gate_up, down, shared_gate, shared_up, shared_down, wgu, wd, sg, su, sd, xnT,
               xr, logits, experts_in, shared_in, zeros_out)
        experts(nc, g, wgu, wd, sg, su, sd, xnT, xr, logits, experts_in, shared_in, zeros_out)


def router(nc, g, router_w, gate_up, down, shared_gate, shared_up, shared_down, wgu, wd, sg, su, sd, xnT, xr,
           logits, experts_in, shared_in, zeros_out):
    with ExitStack() as ctx:
        sem = lambda n: nc.alloc_semaphore(f"rt_{n}")
        sb = lambda n, s, d=F32: ctx.enter_context(nc.sbuf_tensor(f"rt_{n}", s, d))
        pb = lambda n, s, d=F32: ctx.enter_context(nc.psum_tensor(f"rt_{n}", s, d))
        rw = sb("rw", [P, CT, NE])
        rows = sb("rows", [NE, H])
        xT = sb("xT", [P, 2, CT, P])
        xn = sb("xn", [P, 2, H])
        zero = sb("zero", [P, H])
        best = sb("best", [P, NT])
        e1 = sb("e1", [P, NT])
        d1 = sb("d1", [P, NT])
        score = sb("score", [P, NT])
        psT = [pb(f"psT{u}", [P, 512]) for u in range(2)]
        psL = [pb(f"psL{u}", [P, 512]) for u in range(2)]
        (rw_in, zeroed, rw_turned, rw_ready, normed, turned, xT_ready, all_T, logit_done, logit_ready, best_ready,
         e_ready, chain) = [sem(n) for n in (
             "rw_in", "zeroed", "rw_turned", "rw_ready", "normed", "turned", "xT_ready", "all_T", "logit_done",
             "logit_ready", "best_ready", "e_ready", "chain")]
        with nc.Block() as block:

            @block.sync
            def _(sp):
                sp.dma_start(rows[:, :], router_w).then_inc(rw_in, 16)
                sp.dma_start(sg[:, :, :], shared_gate.rearrange("(c p) n -> p c n", p=P)).then_inc(shared_in, 16)
                sp.dma_start(su[:, :, :], shared_up.rearrange("(c p) n -> p c n", p=P)).then_inc(shared_in, 16)
                sp.dma_start(sd[:, :, :], shared_down.rearrange("(c p) n -> p c n", p=P)).then_inc(shared_in, 16)
                sp.wait_ge(zeroed, 1)
                with sp.Fori(0, NS) as s:
                    sp.dma_start(g.xr_dram[bass.ds(s * P, P), :], zero[:, :]).then_inc(zeros_out, 16)
                for e in range(NE):
                    sp.dma_start(wgu[:, e, :, :], gate_up[e, :, :].rearrange("(c p) n -> p c n", p=P)
                                 ).then_inc(experts_in, 16)
                    sp.dma_start(wd[:, e, :, :], down[e, :, :].rearrange("(c p) n -> p c n", p=P)
                                 ).then_inc(experts_in, 16)
                sp.wait_ge(zeros_out, 16 * NS)

            @block.gpsimd
            def _(pool):
                pool.memset(zero[:, :], 0.0).then_inc(zeroed, 1)

            @block.vector
            def _(dve):
                dve.wait_ge(rw_turned, 1)
                dve.tensor_copy(rw[:, :, :], psL[0][:, 0:CT * NE].rearrange("p (c e) -> p c e", e=NE)).then_inc(rw_ready, 1)
                with dve.Fori(0, NT // 2) as b:
                    for u in range(2):
                        t = 2 * b + u
                        dve.wait_ge(turned, 2 * b)
                        dve.tensor_scalar(xn[:, u, :], g.x[:, t, :], g.mean[:, bass.ds(t, 1)],
                                          g.rstd[:, bass.ds(t, 1)], ALU.subtract, ALU.mult).then_inc(normed, 1)
                        dve.wait_ge(logit_done, t + 1)
                        dve.tensor_copy(logits[:, t, :], psL[u][:, 0:NE]).then_inc(logit_ready, 1)
                dve.wait_ge(logit_ready, NT)
                dve.tensor_reduce(out=best[:, :], in_=logits[:, :, :], axis=AX.X, op=ALU.max).then_inc(best_ready, 1)
                dve.wait_ge(e_ready, 1)
                dve.tensor_scalar(d1[:, :], e1[:, :], 1.0, None, ALU.add).then_inc(chain, 1)
                dve.wait_ge(chain, 1)
                dve.reciprocal(score[:, :], d1[:, :]).then_inc(chain, 1)
                dve.wait_ge(chain, 2)
                dve.tensor_tensor(score[:, :], score[:, :], g.rstd[:, :], ALU.mult).then_inc(chain, 1)
                dve.wait_ge(chain, 3)
                with dve.Fori(0, NT) as t:
                    dve.tensor_scalar(xr[:, t, :], g.x[:, t, :], g.mean[:, bass.ds(t, 1)],
                                      score[:, bass.ds(t, 1)], ALU.subtract, ALU.mult).then_inc(chain, 1)

            @block.scalar
            def _(act):
                with act.Fori(0, NT // 2) as b:
                    for u in range(2):
                        t = 2 * b + u
                        act.wait_ge(turned, t + 1)
                        act.wait_ge(logit_done, 2 * b)
                        act.activation(xT[:, u, :, :].rearrange("p c n -> p (c n)"), psT[u][:, 0:H],
                                       ACT.Copy).then_inc(xT_ready, 1)
                        act.activation(xnT[:, :, bass.ds(t * P, P)],
                                       psT[u][:, 0:H].rearrange("p (c n) -> p c n", n=P), ACT.Copy).then_inc(all_T, 1)
                act.wait_ge(best_ready, 1)
                act.activation(e1[:, :], best[:, :], ACT.Exp, scale=-1.0).then_inc(e_ready, 1)

            @block.tensor
            def _(pe):
                pe.wait_ge(rw_in, 16)
                for c in range(CT):
                    mm = pe.transpose(psL[0][:, c * NE:(c + 1) * NE], rows[:, c * P:(c + 1) * P],
                                      g.ident[0:NE, 0:NE])
                mm.then_inc(rw_turned, 1)
                pe.wait_ge(rw_ready, 1)
                with pe.Fori(0, NT // 2) as b:
                    for u in range(2):
                        t = 2 * b + u
                        pe.wait_ge(normed, t + 1)
                        pe.wait_ge(all_T, 2 * b)
                        for c in range(CT):
                            mm = pe.transpose(psT[u][:, c * P:(c + 1) * P], xn[:, u, c * P:(c + 1) * P],
                                              g.ident[:, :])
                        mm.then_inc(turned, 1)
                        pe.wait_ge(xT_ready, t + 1)
                        pe.wait_ge(logit_ready, 2 * b)
                        for c in range(CT):
                            mm = pe.matmul(psL[u][:, 0:NE], xT[:, u, c, :], rw[:, c, :],
                                           start=(c == 0), stop=(c == CT - 1))
                        mm.then_inc(logit_done, 1)


def experts(nc, g, wgu, wd, sg, su, sd, xnT, xr, logits, experts_in, shared_in, zeros_out):
    with ExitStack() as ctx:
        sem = lambda n: nc.alloc_semaphore(f"ex_{n}")
        sb = lambda n, s, d=F32: ctx.enter_context(nc.sbuf_tensor(f"ex_{n}", s, d))
        pb = lambda n, s, d=F32: ctx.enter_context(nc.psum_tensor(f"ex_{n}", s, d))
        sel = sb("sel", [P, NT, NE])
        pref = sb("pref", [P, NT, NE])
        code = sb("code", [P, NE])
        mx = sb("mx", [P, NT])
        upper = sb("upper", [P, P])
        ones = sb("ones", [P, P])
        cnt = sb("cnt", [P, NE])
        total = sb("total", [P, NE])
        steps = sb("steps", [P, NE, NT])
        tiles = sb("tiles", [P, NE])
        ends = sb("ends", [P, NE])
        starts = sb("starts", [P, NE])
        tileno = sb("tileno", [1, NS, NE])
        past = sb("past", [1, NS, NE])
        ownerf = sb("ownerf", [1, NS])
        owner = sb("owner", [1, NS], I32)
        slotf = sb("slotf", [P, NT])
        GW = 512
        NGR = T // GW
        silus = sb("silus", [P, 2, GW])
        hT = sb("hT", [P, FT, GW])
        xs = sb("xs", [P, 2, H])
        xsT = sb("xsT", [P, 2, CT, P])
        silur = silus
        hid = sb("hid", [P, 2, FI])
        hidT = sb("hidT", [P, 2, FT, P])
        ys = sb("ys", [P, 2, H])
        banks = [pb(f"bank{i}", [P, 512]) for i in range(8)]
        psRank, psCnt = banks[7], banks[6]
        (const, me, sel_ready, cnt_ready, ranked, counted, owner_ready, slot_ready, scattered, gu_done, silu_ready,
         h_ready, y_done, y_copied, xs_turned, xsT_ready, rgu_done, rsilu, hid_ready, hid_turned, hidT_ready,
         yr_done, ys_ready) = [sem(n) for n in (
             "const", "me", "sel_ready", "cnt_ready", "ranked", "counted", "owner_ready", "slot_ready", "scattered",
             "gu_done", "silu_ready", "h_ready", "y_done", "y_copied", "xs_turned", "xsT_ready", "rgu_done",
             "rsilu", "hid_ready", "hid_turned", "hidT_ready", "yr_done", "ys_ready")]
        xs_in = [sem(f"xs_in{u}") for u in range(2)]
        ys_out = [sem(f"ys_out{u}") for u in range(2)]

        def sorted_tiles(eng, step, lag, last_lag=None):
            PRE_S = 4
            END = NS - 1 - (NS - 1) % 2
            for s in range(PRE_S):
                step(s, s % 2, [k for k in range(lag + 1) if k <= s])
            with eng.Fori(PRE_S // 2, END // 2) as b:
                for u in range(2):
                    step(b * 2 + u, u, list(range(lag + 1)))
            for s in range(END, NS + lag):
                step(s, s % 2, [k for k in range(lag + 1) if 0 <= s - k < NS])

        with nc.Block() as block:

            @block.gpsimd
            def _(pool):
                n = 0
                for op in (
                    lambda: pool.memset(upper[:, :], 1.0),
                    lambda: pool.affine_select(out=upper[:, :], in_=upper[:, :], compare_op=ALU.is_gt, fill=0.0,
                                               base=0, pattern=[[1, P]], channel_multiplier=-1),
                    lambda: pool.memset(ones[:, :], 1.0),
                    lambda: pool.iota(code[:, :], pattern=[[-1, NE]], base=NE, channel_multiplier=0,
                                      allow_small_or_imprecise_dtypes=True),
                    lambda: pool.iota(steps[:, :, :], pattern=[[0, NE], [P, NT]], base=0, channel_multiplier=0,
                                      allow_small_or_imprecise_dtypes=True),
                    lambda: pool.iota(tileno[:, :, :], pattern=[[1, NS], [0, NE]], base=0, channel_multiplier=0,
                                      allow_small_or_imprecise_dtypes=True),
                ):
                    op().then_inc(const, 1)
                    n += 1
                    pool.wait_ge(const, n)
                pool.wait_ge(slot_ready, 1)
                pool.wait_ge(zeros_out, 16 * NS)
                for t in range(NT):
                    pool.indirect_dma_start(out=g.xr_dram,
                                            out_offset=bass.IndirectOffsetOnAxis(ap=g.slot[:, t:t + 1], axis=0),
                                            in_=xr[:, t, :], in_offset=None).then_inc(scattered, 16)
                pool.wait_ge(scattered, 16 * NT)

            @block.sync
            def _(sp):
                sp.wait_ge(scattered, 16 * NT)

                def step(s, u, live):
                    if 0 in live:
                        if not isinstance(s, int) or s >= 2:
                            sp.wait_ge(xs_turned, s - 1)
                        sp.dma_start(xs[:, u, :], g.xr_dram[bass.ds(s * P, P), :]).then_inc(xs_in[u], 16)
                    if 4 in live:
                        sp.wait_ge(ys_ready, s - 3)
                        sp.dma_start(g.yr_dram[bass.ds((s - 4) * P, P), :], ys[:, u, :]).then_inc(ys_out[u], 16)
                sorted_tiles(sp, step, 4)
                sp.wait_ge(ys_out[0], 16 * ((NS + 1) // 2))
                sp.wait_ge(ys_out[1], 16 * (NS // 2))

            @block.vector
            def _(dve):
                own = Tally(me)
                bc = [P, NT, NE]
                dve.wait_ge(const, 6)
                own.mark(dve.tensor_reduce(out=mx[:, :], in_=logits[:, :, :], axis=AX.X, op=ALU.max))
                own.done(dve)
                own.mark(dve.tensor_tensor(sel[:, :, :], logits[:, :, :], mx[:, :].unsqueeze(2).to_broadcast(bc),
                                           ALU.is_equal))
                own.done(dve)
                own.mark(dve.tensor_tensor(pref[:, :, :], sel[:, :, :], code[:, :].unsqueeze(1).to_broadcast(bc),
                                           ALU.mult))
                own.done(dve)
                own.mark(dve.tensor_reduce(out=mx[:, :], in_=pref[:, :, :], axis=AX.X, op=ALU.max))
                own.done(dve)
                dve.tensor_tensor(sel[:, :, :], pref[:, :, :], mx[:, :].unsqueeze(2).to_broadcast(bc),
                                  ALU.is_equal).then_inc(sel_ready, 1)
                dve.wait_ge(sel_ready, 1)
                dve.tensor_reduce(out=cnt[:, :], in_=sel[:, :, :].rearrange("p t e -> p e t"), axis=AX.X,
                                  op=ALU.add).then_inc(cnt_ready, 1)
                dve.wait_ge(counted, 1)
                own.mark(dve.tensor_copy(total[:, :], psCnt[:, 0:NE]))
                own.done(dve)
                own.mark(dve.tensor_tensor(steps[:, :, :], total[:, :].unsqueeze(2).to_broadcast([P, NE, NT]),
                                           steps[:, :, :], ALU.is_gt))
                own.done(dve)
                own.mark(dve.tensor_reduce(out=tiles[:, :], in_=steps[:, :, :], axis=AX.X, op=ALU.add))
                own.done(dve)
                own.mark(dve.tensor_tensor_scan(out=ends[:, :], data0=ones[:, 0:NE], data1=tiles[:, :], initial=0.0,
                                                op0=ALU.mult, op1=ALU.add))
                own.done(dve)
                own.mark(dve.tensor_tensor(starts[:, :], ends[:, :], tiles[:, :], ALU.subtract))
                own.done(dve)
                own.mark(dve.tensor_scalar(starts[:, :], starts[:, :], float(P), None, ALU.mult))
                own.done(dve)
                own.mark(dve.tensor_tensor(past[:, :, :], ends[0:1, :].unsqueeze(1).to_broadcast([1, NS, NE]),
                                           tileno[:, :, :], ALU.is_le))
                own.done(dve)
                own.mark(dve.tensor_reduce(out=ownerf[:, :], in_=past[:, :, :], axis=AX.X, op=ALU.add))
                own.done(dve)
                dve.tensor_scalar(owner[:, :], ownerf[:, :], float(NE - 1), None, ALU.min).then_inc(owner_ready, 1)
                dve.wait_ge(ranked, 1)
                own.mark(dve.tensor_tensor(pref[:, :, :], psRank[:, 0:NT * NE].rearrange("p (t e) -> p t e", e=NE),
                                           starts[:, :].unsqueeze(1).to_broadcast(bc), ALU.add))
                own.done(dve)
                own.mark(dve.tensor_tensor(pref[:, :, :], pref[:, :, :], sel[:, :, :], ALU.mult))
                own.done(dve)
                own.mark(dve.tensor_reduce(out=slotf[:, :], in_=pref[:, :, :], axis=AX.X, op=ALU.add))
                own.done(dve)
                dve.tensor_copy(g.slot[:, :], slotf[:, :]).then_inc(slot_ready, 1)
                with dve.Fori(0, NGR) as q:
                    for f in range(FT):
                        dve.wait_ge(silu_ready, q * FT + f + 1)
                        dve.wait_ge(y_done, q * 4)
                        dve.tensor_tensor(hT[:, f, :], silus[:, f % 2, :], banks[2 * (f % 2) + 1][:, :],
                                          ALU.mult).then_inc(h_ready, 1)
                    for k in range(4):
                        dve.wait_ge(y_done, q * 4 + k + 1)
                        dve.tensor_copy(g.y[:, q * 4 + k, :], banks[4 + k % 2][:, 0:H]).then_inc(y_copied, 1)

                def step(s, u, live):
                    if 1 in live:
                        v = 1 - u
                        dve.wait_ge(rsilu, s)
                        if not isinstance(s, int) or s >= 3:
                            dve.wait_ge(hid_turned, s - 2)
                        dve.tensor_tensor(hid[:, v, :], silur[:, v, :], banks[2 * v + 1][:, :],
                                          ALU.mult).then_inc(hid_ready, 1)
                    if 3 in live:
                        v = 1 - u
                        dve.wait_ge(yr_done, s - 2)
                        if not isinstance(s, int) or s >= 5:
                            dve.wait_ge(ys_out[v], (s - 3 - v) * 8)
                        dve.tensor_copy(ys[:, v, :], banks[6][:, 0:H]).then_inc(ys_ready, 1)
                sorted_tiles(dve, step, 3)

            @block.scalar
            def _(act):
                with act.Fori(0, NGR) as q:
                    for f in range(FT):
                        act.wait_ge(gu_done, q * FT + f + 1)
                        if f >= 2:
                            act.wait_ge(h_ready, q * FT + f - 1)
                        else:
                            act.wait_ge(h_ready, q * FT)
                        act.activation(silus[:, f % 2, :], banks[2 * (f % 2)][:, :], ACT.Silu).then_inc(silu_ready, 1)

                def step(s, u, live):
                    if 0 in live:
                        act.wait_ge(xs_turned, s + 1)
                        if not isinstance(s, int) or s >= 2:
                            act.wait_ge(rgu_done, s - 1)
                        act.activation(xsT[:, u, :, :].rearrange("p c n -> p (c n)"), banks[4][:, 0:H],
                                       ACT.Copy).then_inc(xsT_ready, 1)
                    if 2 in live:
                        act.wait_ge(hid_turned, s - 1)
                        if not isinstance(s, int) or s >= 4:
                            act.wait_ge(yr_done, s - 3)
                        act.activation(hidT[:, u, :, :].rearrange("p k n -> p (k n)"), banks[5][:, :],
                                       ACT.Copy).then_inc(hidT_ready, 1)
                    if 1 in live:
                        v = 1 - u
                        act.wait_ge(rgu_done, s)
                        if not isinstance(s, int) or s >= 3:
                            act.wait_ge(hid_ready, s - 2)
                        else:
                            act.wait_ge(h_ready, NGR * FT)
                        act.activation(silur[:, v, :], banks[2 * v][:, :], ACT.Silu).then_inc(rsilu, 1)
                sorted_tiles(act, step, 2)

            @block.tensor
            def _(pe):
                pe.wait_ge(const, 6)
                pe.wait_ge(sel_ready, 1)
                for e in range(1):
                    mm = pe.matmul(psRank[:, 0:NT * NE], upper[:, :], sel[:, :, :].rearrange("p t e -> p (t e)"),
                                   start=True, stop=False, skip_group_check=True)
                for t in range(NT - 1):
                    rest = NT - 1 - t
                    mm = pe.matmul(psRank[:, (t + 1) * NE:NT * NE], ones[:, :],
                                   sel[:, t, :].unsqueeze(1).to_broadcast([P, rest, NE]),
                                   start=False, stop=(t == NT - 2), skip_group_check=True)
                mm.then_inc(ranked, 1)
                pe.wait_ge(cnt_ready, 1)
                pe.matmul(psCnt[:, 0:NE], ones[:, :], cnt[:, :], start=True, stop=True).then_inc(counted, 1)
                pe.wait_ge(shared_in, 48)
                with pe.Fori(0, NGR) as q:
                    for f in range(FT):
                        pe.wait_ge(h_ready, q * FT + f - 1 if f >= 2 else q * FT)
                        for w, bank in ((sg, banks[2 * (f % 2)]), (su, banks[2 * (f % 2) + 1])):
                            for c in range(CT):
                                mm = pe.matmul(bank[:, :], w[:, c, f * P:(f + 1) * P],
                                               xnT[:, c, bass.ds(q * GW, GW)], start=(c == 0), stop=(c == CT - 1))
                        mm.then_inc(gu_done, 1)
                    pe.wait_ge(h_ready, q * FT + FT)
                    for k in range(4):
                        pe.wait_ge(y_copied, q * 4 + k - 1 if k >= 2 else q * 4)
                        for f in range(FT):
                            mm = pe.matmul(banks[4 + k % 2][:, 0:H], hT[:, f, k * P:(k + 1) * P], sd[:, f, :],
                                           start=(f == 0), stop=(f == FT - 1))
                        mm.then_inc(y_done, 1)
                pe.wait_ge(experts_in, 16 * 2 * NE)
                pe.wait_ge(owner_ready, 1)
                pe.wait_ge(slot_ready, 1)
                pe.wait_ge(y_copied, NT)

                def step(s, u, live):
                    if 0 in live:
                        pe.wait_ge(xs_in[u], (s - u) * 8 + 16)
                        if not isinstance(s, int) or s >= 1:
                            pe.wait_ge(xsT_ready, s)
                        for c in range(CT):
                            mm = pe.transpose(banks[4][:, c * P:(c + 1) * P], xs[:, u, c * P:(c + 1) * P],
                                              g.ident[:, :])
                        mm.then_inc(xs_turned, 1)
                    if 1 in live:
                        v = 1 - u
                        e = pe.value_load(owner[0:1, bass.ds(s - 1, 1)], min_val=0, max_val=NE - 1)
                        pe.wait_ge(xsT_ready, s)
                        if not isinstance(s, int) or s >= 3:
                            pe.wait_ge(hid_ready, s - 2)
                        for half in range(2):
                            for c in range(CT):
                                mm = pe.matmul(banks[2 * v + half][:, :], xsT[:, v, c, :],
                                               wgu[:, bass.ds(e, 1), c, half * FI:(half + 1) * FI]
                                               .rearrange("p e n -> p (e n)"), start=(c == 0), stop=(c == CT - 1))
                        mm.then_inc(rgu_done, 1)
                    if 2 in live:
                        pe.wait_ge(hid_ready, s - 1)
                        if not isinstance(s, int) or s >= 3:
                            pe.wait_ge(hidT_ready, s - 2)
                        for k in range(FT):
                            mm = pe.transpose(banks[5][:, k * P:(k + 1) * P], hid[:, u, k * P:(k + 1) * P],
                                              g.ident[:, :])
                        mm.then_inc(hid_turned, 1)
                    if 3 in live:
                        v = 1 - u
                        e = pe.value_load(owner[0:1, bass.ds(s - 3, 1)], min_val=0, max_val=NE - 1)
                        pe.wait_ge(hidT_ready, s - 2)
                        if not isinstance(s, int) or s >= 4:
                            pe.wait_ge(ys_ready, s - 3)
                        for k in range(FT):
                            mm = pe.matmul(banks[6][:, 0:H], hidT[:, v, k, :],
                                           wd[:, bass.ds(e, 1), k, :].rearrange("p e n -> p (e n)"),
                                           start=(k == 0), stop=(k == FT - 1))
                        mm.then_inc(yr_done, 1)
                sorted_tiles(pe, step, 3)


def gather_routed(nc, g):
    with ExitStack() as ctx:
        yg = ctx.enter_context(nc.sbuf_tensor("gr_yg", [P, NT, H], F32))
        gathered = [nc.alloc_semaphore(f"gr_in{t}") for t in range(NT)]
        added = nc.alloc_semaphore("gr_added")
        with nc.Block() as block:
            @block.gpsimd
            def _(pool):
                for t in range(NT):
                    pool.indirect_dma_start(out=yg[:, t, :], out_offset=None, in_=g.yr_dram,
                                            in_offset=bass.IndirectOffsetOnAxis(ap=g.slot[:, t:t + 1], axis=0)
                                            ).then_inc(gathered[t], 16)

            @block.vector
            def _(dve):
                for t in range(NT):
                    dve.wait_ge(gathered[t], 16)
                    dve.tensor_tensor(g.y[:, t, :], g.y[:, t, :], yg[:, t, :], ALU.add).then_inc(added, 1)

DI = 512
VH, VP = 64, 8
SG, SN = 8, 64
GV = VH // SG
KC = 4
XT = DI // P
CONV_T = 3 * XT
NC = NT
HT = T // 2
ATANH = 7


def flat(ap):
    return ap.rearrange("p t c -> p (t c)")


def project_state(nc, g, xc, z, alog, in_w, conv_w, conv_b, z_bias):
    ET = CONV_T + XT
    with ExitStack() as ctx:
        sem = lambda n: nc.alloc_semaphore(f"ps_{n}")
        sb = lambda n, s, d=F32: ctx.enter_context(nc.sbuf_tensor(f"ps_{n}", s, d))
        pb = lambda n, s, d=F32: ctx.enter_context(nc.psum_tensor(f"ps_{n}", s, d))
        xnT = flat(g.y[:, :, :]).rearrange("p (c n) -> p c n", c=CT)
        xn = sb("xn", [P, 2, H])
        wrow = sb("wrow", [P, 2, H])
        wT = sb("wT", [P, 2, CT, P])
        raw = sb("raw", [P, 2, KC - 1 + T])
        cw = sb("cw", [P, CONV_T, KC])
        cb = sb("cb", [P, CONV_T])
        zb = sb("zb", [P, XT])
        banks = [pb(f"bank{i}", [P, 512]) for i in range(8)]
        (const_in, x_out, preset, normed, turned, xT_ready, w_turned, w_ready, proj_done, raw_ready, tap0, conv,
         silu, evac) = [sem(n) for n in (
             "const_in", "x_out", "preset", "normed", "turned", "xT_ready", "w_turned", "w_ready", "proj_done",
             "raw_ready", "tap0", "conv", "silu", "evac")]
        w_in = [sem(f"w_in{u}") for u in range(2)]
        NQ = T // 512
        with nc.Block() as block:

            @block.sync
            def _(sp):
                sp.dma_start(cw[:, :, :], conv_w.rearrange("(m p) a k -> p m (a k)", p=P)).then_inc(const_in, 16)
                sp.dma_start(cb[:, :], conv_b.rearrange("(m p) -> p m", p=P),
                             allow_slow_non_contiguous=True).then_inc(const_in, 16)
                sp.dma_start(zb[:, :], z_bias.rearrange("(m p) -> p m", p=P),
                             allow_slow_non_contiguous=True).then_inc(const_in, 16)
                sp.dma_start(g.x_dram.rearrange("(t p) c -> p t c", p=P), g.x[:, :, :]).then_inc(x_out, 16)
                with sp.Fori(0, ET // 2) as b:
                    for u in range(2):
                        sp.wait_ge(w_turned, 2 * b)
                        sp.dma_start(wrow[:, u, :], in_w[bass.ds((2 * b + u) * P, P), :]).then_inc(w_in[u], 16)
                sp.wait_ge(w_turned, ET - 1)
                sp.dma_start(wrow[0:VH, 0, :], in_w[ET * P:ET * P + VH, :]).then_inc(w_in[0], 16)
                sp.wait_ge(x_out, 16)

            @block.gpsimd
            def _(pool):
                for u in range(2):
                    pool.memset(raw[:, u, 0:KC - 1], 0.0).then_inc(preset, 1)
                    pool.wait_ge(preset, u + 1)

            @block.vector
            def _(dve):
                with dve.Fori(0, NT // 2) as b:
                    for u in range(2):
                        t = 2 * b + u
                        dve.wait_ge(turned, 2 * b)
                        dve.tensor_scalar(xn[:, u, :], g.x[:, t, :], g.mean[:, bass.ds(t, 1)],
                                          g.rstd[:, bass.ds(t, 1)], ALU.subtract, ALU.mult).then_inc(normed, 1)
                with dve.Fori(0, CONV_T // 2) as b:
                    for u in range(2):
                        m = 2 * b + u
                        dve.wait_ge(raw_ready, (m + 1) * NQ)
                        dve.wait_ge(tap0, m + 1)
                        for k in range(1, KC):
                            dve.scalar_tensor_tensor(out=xc[:, m, :], in0=raw[:, u, k:k + T],
                                                     scalar=cw[:, m, k:k + 1], in1=xc[:, m, :],
                                                     op0=ALU.mult, op1=ALU.add).then_inc(conv, 1)
                            if k < KC - 1:
                                dve.wait_ge(conv, m * (KC - 1) + k)

            @block.scalar
            def _(act):
                with act.Fori(0, NT // 2) as b:
                    for u in range(2):
                        t = 2 * b + u
                        act.wait_ge(turned, t + 1)
                        act.activation(xnT[:, :, bass.ds(t * P, P)],
                                       banks[6 + u][:, 0:H].rearrange("p (c n) -> p c n", n=P),
                                       ACT.Copy).then_inc(xT_ready, 1)
                act.wait_ge(const_in, 48)
                act.wait_ge(preset, 2)

                def weights(m, u):
                    act.wait_ge(w_turned, m + 1)
                    act.wait_ge(proj_done, (m - 1) * NQ if not isinstance(m, int) or m >= 1 else 0)
                    act.activation(wT[:, u, :, :].rearrange("p c n -> p (c n)"), banks[4 + u][:, 0:H],
                                   ACT.Copy).then_inc(w_ready, 1)
                weights(0, 0)
                with act.Fori(0, CONV_T // 2) as b:
                    for u in range(2):
                        m = 2 * b + u
                        act.wait_ge(conv, 2 * b * (KC - 1))
                        act.wait_ge(tap0, 2 * b)
                        for q in range(NQ):
                            act.wait_ge(proj_done, m * NQ + q + 1)
                            act.activation(raw[:, u, KC - 1 + q * 512:KC - 1 + (q + 1) * 512], banks[q][:, :],
                                           ACT.Copy).then_inc(raw_ready, 1)
                            if q == 0:
                                weights(m + 1, 1 - u)
                        act.wait_ge(raw_ready, (m + 1) * NQ)
                        act.activation(xc[:, m, :], raw[:, u, 0:T], ACT.Copy, scale=cw[:, m, 0:1]).then_inc(tap0, 1)
                        if u == 1:
                            act.wait_ge(conv, (m * (KC - 1)))
                            act.activation(xc[:, m - 1, :], xc[:, m - 1, :], ACT.Silu,
                                           bias=cb[:, bass.ds(m - 1, 1)]).then_inc(silu, 1)
                            act.wait_ge(conv, (m + 1) * (KC - 1))
                            act.activation(xc[:, m, :], xc[:, m, :], ACT.Silu,
                                           bias=cb[:, bass.ds(m, 1)]).then_inc(silu, 1)
                for m in range(CONV_T, ET):
                    for q in range(NQ):
                        act.wait_ge(proj_done, m * NQ + q + 1)
                        act.activation(z[:, m - CONV_T, q * 512:(q + 1) * 512], banks[q][:, :], ACT.Silu,
                                       bias=zb[:, m - CONV_T:m - CONV_T + 1]).then_inc(evac, 1)
                        if q == 0 and m + 1 < ET:
                            weights(m + 1, (m + 1) % 2)
                act.wait_ge(w_turned, ET + 1)
                act.wait_ge(proj_done, ET * NQ)
                act.activation(wT[:, 0, :, 0:VH],
                               banks[4][:, 0:CT * VH].rearrange("p (c n) -> p c n", n=VH), ACT.Copy).then_inc(w_ready, 1)
                act.wait_ge(proj_done, ET * NQ + 1)
                for q in range(2):
                    act.activation(alog[:, q * 512:(q + 1) * 512], banks[q][:, :], ACT.Copy).then_inc(evac, 1)

            @block.tensor
            def _(pe):
                with pe.Fori(0, NT // 2) as b:
                    for u in range(2):
                        t = 2 * b + u
                        pe.wait_ge(normed, t + 1)
                        pe.wait_ge(xT_ready, 2 * b)
                        for c in range(CT):
                            mm = pe.transpose(banks[6 + u][:, c * P:(c + 1) * P], xn[:, u, c * P:(c + 1) * P],
                                              g.ident[:, :])
                        mm.then_inc(turned, 1)
                pe.wait_ge(xT_ready, NT)

                def turn_weights(m, u, count):
                    pe.wait_ge(w_in[u], count)
                    for c in range(CT):
                        mm = pe.transpose(banks[4 + u][:, c * P:(c + 1) * P], wrow[:, u, c * P:(c + 1) * P],
                                          g.ident[:, :])
                    mm.then_inc(w_turned, 1)

                def products(m, u, freed):
                    pe.wait_ge(w_ready, m + 1)
                    for q in range(NQ):
                        freed(q)
                        for c in range(CT):
                            mm = pe.matmul(banks[q][:, :], wT[:, u, c, :], xnT[:, c, q * 512:(q + 1) * 512],
                                           start=(c == 0), stop=(c == CT - 1))
                        mm.then_inc(proj_done, 1)
                turn_weights(0, 0, 16)
                with pe.Fori(0, CONV_T // 2) as b:
                    for u in range(2):
                        m = 2 * b + u
                        turn_weights(m + 1, 1 - u, (b + 1) * 16 + (16 if u else 0))
                        products(m, u, lambda q: pe.wait_ge(raw_ready, (m - 1) * NQ + q + 1) if u else
                                 pe.wait_ge(raw_ready, m * NQ))
                for m in range(CONV_T, ET):
                    u = m % 2
                    if m + 1 < ET:
                        turn_weights(m + 1, 1 - u, ((m + 1) // 2 + 1) * 16)
                    products(m, u, lambda q: (pe.wait_ge(raw_ready, CONV_T * NQ),
                                              pe.wait_ge(evac, max((m - CONV_T - 1) * NQ + q + 1, 0))))
                pe.wait_ge(w_in[0], 16 * (ET // 2 + 1))
                for c in range(CT):
                    mm = pe.transpose(banks[4][:, c * VH:(c + 1) * VH], wrow[0:VH, 0, c * P:(c + 1) * P],
                                      g.ident[0:VH, 0:VH])
                mm.then_inc(w_turned, 1)
                pe.wait_ge(w_ready, ET + 1)
                pe.wait_ge(evac, XT * NQ)
                for half in range(2):
                    for q in range(2):
                        for c in range(CT):
                            n0 = half * HT + q * 512
                            mm = pe.matmul(banks[q][half * VH:(half + 1) * VH, :], wT[:, 0, c, 0:VH],
                                           xnT[:, c, n0:n0 + 512], start=(c == 0), stop=(c == CT - 1),
                                           skip_group_check=True)
                mm.then_inc(proj_done, 1)


def decays(nc, g, alog, decT, D):
    with ExitStack() as ctx:
        sem = lambda n: nc.alloc_semaphore(f"dc_{n}")
        sb = lambda n, s, d=F32: ctx.enter_context(nc.sbuf_tensor(f"dc_{n}", s, d))
        pb = lambda n, s, d=F32: ctx.enter_context(nc.psum_tensor(f"dc_{n}", s, d))
        e = sb("e", [P, HT])
        s = sb("s", [P, HT])
        s2 = sb("s2", [P, HT])
        p = sb("p", [P, HT])
        dt = sb("dt", [P, HT])
        keep = sb("keep", [P, NC // 2, P])
        ac = sb("ac", [P, HT])
        dcol = sb("dcol", [P, 1])
        parts = sb("parts", [P, 3, HT], BF16)
        banks = [pb(f"bank{i}", [P, 512]) for i in range(2)]
        (own, d_in, keep_ready, abs_ready, e_ready, ac_ready, ea_ready, dec_arg, dec_ready, parts_ready, ddt_ready,
         turned, decT_ready, stored) = [sem(n) for n in (
             "own", "d_in", "keep_ready", "abs_ready", "e_ready", "ac_ready", "ea_ready", "dec_arg", "dec_ready",
             "parts_ready", "ddt_ready", "turned", "decT_ready", "stored")]
        ea = e
        with nc.Block() as block:

            @block.sync
            def _(sp):
                for half in range(2):
                    sp.dma_start(dcol[half * VH:(half + 1) * VH, :], D.rearrange("(h a) -> h a", a=1)).then_inc(d_in, 16)
                halves = lambda i: g.rep_dram[i, :, :].rearrange("h (a n) -> a h n", a=2)
                for what, i, ready in ((ddt_ready, 1, s), (ea_ready, 0, ea)):
                    sp.wait_ge(what, 1)
                    for half in range(2):
                        sp.dma_start(halves(i)[half, :, :], ready[half * VH:(half + 1) * VH, :]).then_inc(stored, 16)
                sp.wait_ge(parts_ready, 1)
                for i in range(3):
                    for half in range(2):
                        sp.dma_start(g.ac_dram[i, :, :].rearrange("h (a n) -> a h n", a=2)[half, :, :],
                                     parts[half * VH:(half + 1) * VH, i, :]).then_inc(stored, 16)
                sp.wait_ge(stored, 16 * 10)

            @block.gpsimd
            def _(pool):
                pool.memset(keep[:, :, :], 1.0).then_inc(keep_ready, 1)
                pool.wait_ge(keep_ready, 1)
                pool.memset(keep[:, :, 0:1], 0.0).then_inc(keep_ready, 1)

            @block.vector
            def _(dve):
                me = Tally(own)

                def run(ins):
                    me.mark(ins)
                    me.done(dve)
                dve.wait_ge(e_ready, 1)
                run(dve.tensor_scalar(s2[:, :], e[:, :], 2.0, None, ALU.add))
                run(dve.reciprocal(s2[:, :], s2[:, :]))
                run(dve.tensor_tensor(s[:, :], e[:, :], s2[:, :], ALU.mult))
                run(dve.tensor_tensor(s2[:, :], s[:, :], s[:, :], ALU.mult))
                run(dve.tensor_scalar(p[:, :], s2[:, :], 1.0 / (2 * ATANH + 1), None, ALU.mult))
                for k in range(ATANH - 1, 0, -1):
                    run(dve.scalar_tensor_tensor(out=p[:, :], in0=p[:, :], scalar=1.0 / (2 * k + 1), in1=s2[:, :],
                                                 op0=ALU.add, op1=ALU.mult))
                run(dve.scalar_tensor_tensor(out=p[:, :], in0=p[:, :], scalar=1.0, in1=s[:, :],
                                             op0=ALU.add, op1=ALU.mult))
                run(dve.tensor_scalar(s2[:, :], alog[:, :], 0.0, None, ALU.max))
                run(dve.scalar_tensor_tensor(out=dt[:, :], in0=p[:, :], scalar=2.0, in1=s2[:, :],
                                             op0=ALU.mult, op1=ALU.add))
                run(dve.tensor_scalar(s2[:, :], dt[:, :], -1.0, None, ALU.mult))
                dve.wait_ge(keep_ready, 2)
                dve.tensor_tensor_scan(out=ac[:, :], data0=keep[:, :, :].rearrange("p c n -> p (c n)"),
                                       data1=s2[:, :], initial=0.0, op0=ALU.mult, op1=ALU.add).then_inc(ac_ready, 1)
                dve.wait_ge(ac_ready, 1)
                ac3 = ac[:, :].rearrange("p (c n) -> p c n", n=P)
                dve.tensor_tensor(p[:, :].rearrange("p (c n) -> p c n", n=P),
                                  ac3[:, :, P - 1:P].to_broadcast([P, NC // 2, P]), ac3, ALU.subtract).then_inc(dec_arg, 1)
                run(dve.tensor_copy(parts[:, 0, :], ac[:, :]))
                run(dve.tensor_tensor(s2[:, :], ac[:, :], parts[:, 0, :], ALU.subtract))
                run(dve.tensor_copy(parts[:, 1, :], s2[:, :]))
                dve.tensor_tensor(parts[:, 2, :], s2[:, :], parts[:, 1, :], ALU.subtract).then_inc(parts_ready, 1)
                dve.wait_ge(d_in, 32)
                run(dve.reciprocal(dt[:, :], dt[:, :]))
                dve.tensor_scalar(s[:, :], dt[:, :], dcol[:, 0:1], None, ALU.mult).then_inc(ddt_ready, 1)
                for i in range(2):
                    dve.wait_ge(turned, i + 1)
                    dve.tensor_copy(decT[:, :, :].rearrange("p (a c) h -> p c a h", a=2)[:, 4 * i:4 * i + 4, :, :],
                                    banks[i][:, :].rearrange("p (c a h) -> p c a h", a=2, h=VH)
                                    ).then_inc(decT_ready, 1)

            @block.scalar
            def _(act):
                act.activation(e[:, :], alog[:, :], ACT.Abs).then_inc(abs_ready, 1)
                act.wait_ge(abs_ready, 1)
                act.activation(e[:, :], e[:, :], ACT.Exp, scale=-1.0).then_inc(e_ready, 1)
                act.wait_ge(ac_ready, 1)
                act.activation(ea[:, :], ac[:, :], ACT.Exp).then_inc(ea_ready, 1)
                act.wait_ge(dec_arg, 1)
                act.activation(p[:, :], p[:, :], ACT.Exp).then_inc(dec_ready, 1)

            @block.tensor
            def _(pe):
                pe.wait_ge(dec_ready, 1)
                for i in range(2):
                    for c in range(4):
                        mm = pe.transpose(banks[i][:, c * P:(c + 1) * P],
                                          p[:, (4 * i + c) * P:(4 * i + c + 1) * P], g.ident[:, :])
                    mm.then_inc(turned, 1)


def scan(nc, g, xc, z, decT):
    KD = 3 + 3 * GV
    with ExitStack() as ctx:
        sem = lambda n: nc.alloc_semaphore(f"sc_{n}")
        sb = lambda n, s, d=F32: ctx.enter_context(nc.sbuf_tensor(f"sc_{n}", s, d))
        pb = lambda n, s, d=F32: ctx.enter_context(nc.psum_tensor(f"sc_{n}", s, d))
        QW, WINDOW = 96, (0, 24, 40, 64)
        NQD = VH // 4
        xw, yw = flat(g.x[:, :, :]), flat(g.y[:, :, :])
        EX = yw.rearrange("p (r h n) -> p r h n", r=4, h=GV)
        Xm = xw[:, 0:2 * NQD * QW].rearrange("p (u n) -> p u n", u=2)
        rep = xw[:, 2 * NQD * QW:2 * NQD * QW + 2 * XT * P].rearrange("p (a i n) -> p a i n", a=2, i=XT)
        Xd = sb("Xd", [P, DI])
        tmp = sb("tmp", [P, XT * P])
        tmp2 = sb("tmp2", [P, XT * P])
        xr = sb("xr", [P, 2, XT, P])
        Br = sb("Br", [P, XT, P])
        Bz = sb("Bz", [P, XT, 2, P])
        Bt = sb("Bt", [P, SG * SN])
        CBm = sb("CBm", [P, 2, SG, P])
        mask = sb("mask", [P, P], BF16)
        ST = sb("ST", [P, XT, P])
        Sn = sb("Sn", [P, XT, P])
        dl = sb("dl", [KD, 2, SG, P], BF16)
        dm = sb("dm", [KD, 4, GV, P], BF16)
        dmi = tmp[0:GV, :].bitcast(BF16).rearrange("p (h n) -> p h n", h=GV)
        D0 = [pb(f"D{i}", [P, 2, 512]) for i in range(2)]
        W = [pb(f"W{i}", [P, 512]) for i in range(2)]
        Yo, Yd = pb("Yo", [P, XT, P]), pb("Yd", [P, XT, P])
        (own, preset, t_done, xm_ready, xd_ready, bt_ready, cb_done, cbm_ready, yo_done, st_done, st_ready, sT_done,
         s_ready, diff_done, exp_done, m_ready, yd_done, yo_used, summed, comb, dx_ready, out_ready,
         st_upd) = [sem(n) for n in (
             "own", "preset", "t_done", "xm_ready", "xd_ready", "bt_ready", "cb_done", "cbm_ready", "yo_done",
             "st_done", "st_ready", "sT_done", "s_ready", "diff_done", "exp_done", "m_ready", "yd_done", "yo_used",
             "summed", "comb", "dx_ready", "out_ready", "st_upd")]
        x_in = [sem(f"x_in{u}") for u in range(2)]
        dl_in = [sem(f"dl_in{u}") for u in range(2)]
        dm_in = [sem(f"dm_in{r}") for r in range(4)]
        b_in, bz_in, rep_in, ind_in = [sem(n) for n in ("b_in", "bz_in", "rep_in", "ind_in")]
        zeroed = sem("zeroed")
        turn = sem("turn")

        def chunks(eng, body):
            body(0, 0, False)
            with eng.Fori(0, (NC - 2) // 2) as b:
                body(b * 2 + 1, 1, False)
                body(b * 2 + 2, 0, False)
            body(NC - 1, (NC - 1) % 2, True)

        def passed(n):
            return max(n, 0) if isinstance(n, int) else n

        with nc.Block() as block:

            @block.sync
            def _(sp):
                def load_x(c, u):
                    cols = bass.ds(c * P, P)
                    sp.dma_start(xr[:, u, :, :], xc[:, 0:XT, cols]).then_inc(x_in[u], 16)
                    sp.dma_start(Br[:, :, :], xc[:, XT:2 * XT, cols]).then_inc(b_in, 16)
                    for k in range(2):
                        sp.dma_start(Bz[k * SN:(k + 1) * SN, :, k, :],
                                     xc[k * SN:(k + 1) * SN, XT:2 * XT, cols]).then_inc(bz_in, 16)

                def load_dl(c, u):
                    for i in range(3):
                        sp.dma_start(dl[3 + i * GV:3 + (i + 1) * GV, u, :, :],
                                     g.ac_dram[i, :, bass.ds(c * P, P)].rearrange("(s h) n -> h s n", h=GV)
                                     ).then_inc(dl_in[u], 16)

                def load_dm(c, s):
                    sp.dma_start(dm[0:3, s % 4, :, :], g.ac_dram[:, s * GV:(s + 1) * GV, bass.ds(c * P, P)]
                                 ).then_inc(dm_in[s % 4], 16)

                def load_rep(c):
                    for a in range(2):
                        for i in range(XT):
                            src = g.rep_dram[a, i * (VH // XT):(i + 1) * (VH // XT), bass.ds(c * P, P)]
                            sp.dma_start(rep[:, a, i, :],
                                         src.unsqueeze(1).to_broadcast([VH // XT, VP, P])).then_inc(rep_in, 16)

                sp.wait_ge(preset, 1)
                for i in range(3):
                    for r in range(4):
                        sp.dma_start(dm[3 + i * GV:3 + (i + 1) * GV, r, :, :], dmi).then_inc(ind_in, 16)
                load_x(0, 0)
                load_dl(0, 0)
                for s in range(4):
                    load_dm(0, s)
                load_rep(0)

                def body(c, u, last):
                    for s in range(SG):
                        if last and s >= 4:
                            continue
                        sp.wait_ge(diff_done, c * SG + s + 1)
                        sp.sem_inc(turn, 1)
                        if s < 4:
                            load_dm(c, s + 4)
                        else:
                            load_dm(c + 1, s - 4)
                        if s == 0 and not last:
                            sp.wait_ge(cb_done, c + 1)
                            sp.wait_ge(t_done, c + 1)
                            sp.wait_ge(dx_ready, passed(c))
                            sp.sem_inc(turn, 1)
                            load_x(c + 1, 1 - u)
                            load_dl(c + 1, 1 - u)
                        if s == 3 and not last:
                            sp.wait_ge(st_ready, c + 1)
                            sp.wait_ge(yo_used, c + 1)
                            sp.wait_ge(dx_ready, c + 1)
                            sp.sem_inc(turn, 1)
                            load_rep(c + 1)

                chunks(sp, body)

            @block.gpsimd
            def _(pool):
                n = 0
                for op in (
                    lambda: pool.memset(dmi, -1.0),
                    lambda: pool.affine_select(out=dmi, in_=dmi, compare_op=ALU.is_equal, fill=0.0,
                                               base=0, pattern=[[-1, GV], [0, P]], channel_multiplier=1),
                    lambda: pool.memset(mask[:, :], 0.0),
                    lambda: pool.affine_select(out=mask[:, :], in_=mask[:, :], compare_op=ALU.is_ge, fill=PAD_SCORE,
                                               base=0, pattern=[[1, P]], channel_multiplier=-1),
                ):
                    op().then_inc(own, 1)
                    n += 1
                    pool.wait_ge(own, n)
                pool.wait_ge(zeroed, 5)
                pool.sem_inc(preset, 1)

                def body(c, u, last):
                    pool.wait_ge(rep_in, (c + 1) * (16 * 2 * XT))
                    pool.wait_ge(x_in[u], (c - u) * 8 + 16)
                    pool.wait_ge(summed, passed(c))
                    pool.tensor_tensor(tmp2[:, :].rearrange("p (i n) -> p i n", n=P), xr[:, u, :, :],
                                       rep[:, 1, :, :], ALU.mult).then_inc(dx_ready, 1)
                    pool.wait_ge(comb, c + 1)
                    zc = z[:, :, bass.ds(c * P, P)]
                    pool.tensor_tensor(zc, zc, tmp[:, :].rearrange("p (i n) -> p i n", n=P),
                                       ALU.mult).then_inc(out_ready, 1)
                chunks(pool, body)

            @block.vector
            def _(dve):
                for op in (Xm, Bz[:, :, :, :], ST[:, :, :], Sn[:, :, :]):
                    dve.memset(op, 0.0).then_inc(zeroed, 1)
                dve.memset(dl[:, :, :, :], 1.0).then_inc(zeroed, 1)
                dve.wait_ge(preset, 1)

                def turned_x(c, u):
                    dve.wait_ge(t_done, c + 1)
                    dve.wait_ge(yd_done, passed((c - 1) * SG))
                    xm = Xm[:, u, :].rearrange("p (q n) -> p q n", q=NQD)
                    for k in range(2):
                        dve.tensor_copy(
                            xm[:, :, 56 * k:56 * k + 40].rearrange("p q (j w) -> p q j w", w=VP)[:, :, 0:5:4, :],
                            W[0][:, :].rearrange("p (q a j v) -> p q a j v", q=NQD, a=2, j=2)[:, :, k, :, :]
                        ).then_inc(xm_ready, 1)
                    dve.wait_ge(st_done, passed(c))
                    dve.tensor_tensor(Xd[:, :].rearrange("p (h v) -> p h v", v=VP),
                                      W[0][:, :].rearrange("p (h v) -> p h v", v=VP),
                                      decT[:, bass.ds(c, 1), :].rearrange("p c h -> p (c h)").unsqueeze(2)
                                      .to_broadcast([P, VH, VP]), ALU.mult).then_inc(xd_ready, 1)

                def products_out(c, u):
                    dve.wait_ge(cb_done, c + 1)
                    for k in range(2):
                        dve.tensor_copy(CBm[:, u, 4 * k:4 * k + 4, :], W[k][:, :].rearrange("p (s n) -> p s n", n=P)
                                        ).then_inc(cbm_ready, 1)

                turned_x(0, 0)
                products_out(0, 0)

                def body(c, u, last):
                    t3 = tmp[:, :].rearrange("p (i n) -> p i n", n=P)
                    dve.wait_ge(cbm_ready, 2 * c + 2)
                    for s in range(SG):
                        dve.wait_ge(exp_done, c * SG + s + 1)
                        dve.tensor_tensor(EX[:, s % 4, :, :], EX[:, s % 4, :, :],
                                          CBm[:, u, s, :].unsqueeze(1).to_broadcast([P, GV, P]),
                                          ALU.mult).then_inc(m_ready, 1)
                        if s == 0:
                            dve.wait_ge(st_done, c + 1)
                            dve.wait_ge(rep_in, (c + 1) * (16 * 2 * XT))
                            for i in range(XT):
                                for k in range(2):
                                    r = slice(k * SN, (k + 1) * SN)
                                    dve.scalar_tensor_tensor(
                                        out=ST[r, i, r], in0=ST[r, i, r], scalar=rep[r, 0, i, P - 1:P],
                                        in1=W[0][r, i * P + k * SN:i * P + (k + 1) * SN],
                                        op0=ALU.mult, op1=ALU.add).then_inc(st_upd, 1)
                            dve.wait_ge(st_upd, (c + 1) * (2 * XT))
                            dve.sem_inc(st_ready, 1)
                        if s == 1:
                            dve.wait_ge(yo_done, c + 1)
                            dve.wait_ge(out_ready, passed(c))
                            dve.tensor_tensor(t3, Yo[:, :, :], rep[:, 0, :, :], ALU.mult).then_inc(yo_used, 1)
                        if s == 2:
                            dve.wait_ge(yo_used, c + 1)
                            dve.wait_ge(dx_ready, c + 1)
                            dve.tensor_tensor(tmp[:, :], tmp[:, :], tmp2[:, :], ALU.add).then_inc(summed, 1)
                        if s == 4 and not last:
                            turned_x(c + 1, 1 - u)
                        if s == 6 and not last:
                            products_out(c + 1, 1 - u)
                    dve.wait_ge(summed, c + 1)
                    dve.wait_ge(yd_done, (c + 1) * SG)
                    dve.tensor_tensor(t3, t3, Yd[:, :, :], ALU.add).then_inc(comb, 1)
                chunks(dve, body)

            @block.scalar
            def _(act):
                def turned_b(c):
                    act.wait_ge(t_done, c + 1)
                    act.wait_ge(st_done, passed(c))
                    act.activation(Bt[:, :], W[1][:, :], ACT.Copy).then_inc(bt_ready, 1)
                turned_b(0)

                def body(c, u, last):
                    for s in range(SG):
                        act.wait_ge(diff_done, c * SG + s + 1)
                        act.wait_ge(yd_done, passed(c * SG + s - 3))
                        act.activation(EX[:, s % 4, :, :].rearrange("p h n -> p (h n)"),
                                       D0[s % 2][:, :, :].rearrange("p a n -> p (a n)"), ACT.Exp).then_inc(exp_done, 1)
                        if s == 3 and not last:
                            act.wait_ge(sT_done, c + 1)
                            act.wait_ge(yo_done, c + 1)
                            act.activation(Sn[:, :, :].rearrange("p i n -> p (i n)"), W[1][:, :],
                                           ACT.Copy).then_inc(s_ready, 1)
                        if s == 5 and not last:
                            turned_b(c + 1)
                chunks(act, body)

            @block.tensor
            def _(pe):
                pe.wait_ge(preset, 1)
                pe.wait_ge(ind_in, 16 * 12)

                def turn_xb(c, u):
                    pe.wait_ge(x_in[u], (c - u) * 8 + 16)
                    pe.wait_ge(b_in, (c + 1) * 16)
                    pe.wait_ge(st_ready, passed(c))
                    pe.wait_ge(s_ready, passed(c))
                    for a in range(2):
                        for i in range(XT):
                            mm = pe.transpose(W[a][:, i * P:(i + 1) * P], Br[:, i, :] if a else xr[:, u, i, :],
                                              g.ident[:, :])
                    mm.then_inc(t_done, 1)

                def diff(c, u, s):
                    if s == 0:
                        pe.wait_ge(dl_in[u], (c - u) * 24 + 48)
                    pe.wait_ge(dm_in[s % 4], (c * 2 + s // 4 + 1) * 16)
                    pe.wait_ge(exp_done, passed(c * SG + s - 1))
                    for k in range(2):
                        pe.matmul(D0[s % 2][:, k, :], g.identb[:, :],
                                  mask[:, :].unsqueeze(1).to_broadcast([P, 4, P]), start=True, stop=False)
                        mm = pe.matmul(D0[s % 2][:, k, :], dl[:, u, s, :],
                                       dm[:, s % 4, 4 * k:4 * k + 4, :], start=False, stop=True)
                    mm.then_inc(diff_done, 1)

                def products(c):
                    pe.wait_ge(xm_ready, 2 * c + 2)
                    pe.wait_ge(xd_ready, c + 1)
                    pe.wait_ge(bt_ready, c + 1)
                    pe.wait_ge(bz_in, (c + 1) * 32)
                    for s in range(SG):
                        mm = pe.matmul(W[s // 4][:, (s % 4) * P:(s % 4 + 1) * P], Bz[:, s // 2, s % 2, :],
                                       xc[:, 2 * XT + s // 2, bass.ds(c * P, P)], start=True, stop=True)
                    mm.then_inc(cb_done, 1)

                def from_state(c):
                    pe.wait_ge(yo_used, passed(c))
                    pe.wait_ge(s_ready, passed(c))
                    for i in range(XT):
                        mm = pe.matmul(Yo[:, i, :], Sn[:, i, :], xc[:, 2 * XT + i, bass.ds(c * P, P)],
                                       start=True, stop=True)
                    mm.then_inc(yo_done, 1)

                turn_xb(0, 0)
                diff(0, 0, 0)
                diff(0, 0, 1)
                products(0)
                from_state(0)

                def body(c, u, last):
                    pe.wait_ge(cbm_ready, 2 * c + 2)
                    for i in range(XT):
                        mm = pe.matmul(W[0][:, i * P:(i + 1) * P], Xd[:, i * P:(i + 1) * P],
                                       Bt[:, i * P:(i + 1) * P], start=True, stop=True)
                    mm.then_inc(st_done, 1)
                    for s in range(SG):
                        pe.wait_ge(m_ready, c * SG + s + 1)
                        if s == 0:
                            pe.wait_ge(comb, passed(c))
                        for j in range(4):
                            for k in range(2):
                                quad = 2 * s + k
                                r = (quad % 4) * 32
                                w0 = quad * QW + WINDOW[j]
                                mm = pe.matmul(Yd[r:r + 32, s // 2, :], Xm[:, u, w0:w0 + 32],
                                               EX[:, s % 4, 4 * k + j, :], start=(j == 0), stop=(j == 3),
                                               skip_group_check=True)
                        mm.then_inc(yd_done, 1)
                        if s + 2 < SG:
                            diff(c, u, s + 2)
                        elif not last:
                            diff(c + 1, 1 - u, s + 2 - SG)
                        if s == 1 and not last:
                            pe.wait_ge(st_ready, c + 1)
                            for i in range(XT):
                                mm = pe.transpose(W[1][:, i * P:(i + 1) * P], ST[:, i, :], g.ident[:, :])
                            mm.then_inc(sT_done, 1)
                        if s == 3 and not last:
                            turn_xb(c + 1, 1 - u)
                        if s == 4 and not last:
                            from_state(c + 1)
                        if s == 5 and not last:
                            products(c + 1)
                chunks(pe, body)


def project_out(nc, g, z, out_w):
    with ExitStack() as ctx:
        sem = lambda n: nc.alloc_semaphore(f"po_{n}")
        sb = lambda n, s, d=F32: ctx.enter_context(nc.sbuf_tensor(f"po_{n}", s, d))
        pb = lambda n, s, d=F32: ctx.enter_context(nc.psum_tensor(f"po_{n}", s, d))
        wrow = sb("wrow", [P, CT, DI])
        wT = sb("wT", [P, XT, H])
        zt = sb("zt", [P, 2, XT, P])
        banks = [pb(f"bank{i}", [P, 512]) for i in range(4)]
        w_in, x_in, turned, w_ready, y_done, y_copied = [sem(n) for n in (
            "w_in", "x_in", "turned", "w_ready", "y_done", "y_copied")]
        z_in = [sem(f"z_in{u}") for u in range(2)]
        with nc.Block() as block:

            @block.sync
            def _(sp):
                sp.dma_start(wrow[:, :, :], out_w.rearrange("(a p) n -> p a n", p=P)).then_inc(w_in, 16)
                sp.dma_start(g.x[:, :, :], g.x_dram.rearrange("(t p) c -> p t c", p=P)).then_inc(x_in, 16)
                with sp.Fori(0, NT // 2) as b:
                    for u in range(2):
                        sp.wait_ge(y_done, 2 * b)
                        sp.dma_start(zt[:, u, :, :], z[:, :, bass.ds((2 * b + u) * P, P)]).then_inc(z_in[u], 16)
                sp.wait_ge(x_in, 16)

            @block.vector
            def _(dve):
                for a in range(CT):
                    dve.wait_ge(turned, a + 1)
                    dve.tensor_copy(wT[:, :, a * P:(a + 1) * P],
                                    banks[2 + a][:, :].rearrange("p (k n) -> p k n", n=P)).then_inc(w_ready, 1)

            @block.scalar
            def _(act):
                with act.Fori(0, NT // 2) as b:
                    for u in range(2):
                        act.wait_ge(y_done, 2 * b + u + 1)
                        act.activation(g.y[:, 2 * b + u, :], banks[u][:, 0:H], ACT.Copy).then_inc(y_copied, 1)

            @block.tensor
            def _(pe):
                pe.wait_ge(w_in, 16)
                for a in range(CT):
                    for k in range(XT):
                        mm = pe.transpose(banks[2 + a][:, k * P:(k + 1) * P], wrow[:, a, k * P:(k + 1) * P],
                                          g.ident[:, :])
                    mm.then_inc(turned, 1)
                pe.wait_ge(w_ready, CT)
                with pe.Fori(0, NT // 2) as b:
                    for u in range(2):
                        pe.wait_ge(z_in[u], (b + 1) * 16)
                        pe.wait_ge(y_copied, 2 * b)
                        for k in range(XT):
                            mm = pe.matmul(banks[u][:, 0:H], zt[:, u, k, :], wT[:, k, :],
                                           start=(k == 0), stop=(k == XT - 1))
                        mm.then_inc(y_done, 1)


def state_space(nc, g, in_w, conv_w, conv_b, z_bias, D, out_w):
    with ExitStack() as ctx:
        z = ctx.enter_context(nc.sbuf_tensor("ss_z", [P, XT, T], F32))
        with ExitStack() as inner:
            xc = inner.enter_context(nc.sbuf_tensor("ss_xc", [P, CONV_T, T], F32))
            decT = inner.enter_context(nc.sbuf_tensor("ss_decT", [P, NC, VH], F32))
            with ExitStack() as a:
                alog = a.enter_context(nc.sbuf_tensor("ss_alog", [P, HT], F32))
                project_state(nc, g, xc, z, alog, in_w, conv_w, conv_b, z_bias)
                decays(nc, g, alog, decT, D)
            scan(nc, g, xc, z, decT)
        project_out(nc, g, z, out_w)

MLP = 2048
MT = MLP // P
BLK = 32
NJ = MLP // 512


def unpack(nc, g, w1T, w2T, mats):
    CODES = MLP * H // 2 // P
    with ExitStack() as ctx:
        sem = lambda n: nc.alloc_semaphore(f"up_{n}")
        sb = lambda n, s, d=F32: ctx.enter_context(nc.sbuf_tensor(f"up_{n}", s, d))
        pb = lambda n, s, d=F32: ctx.enter_context(nc.psum_tensor(f"up_{n}", s, d))
        codes = sb("codes", [P, 3, CODES], I32)
        scales = sb("scales", [P, 3, 2 * CODES // BLK])
        mag = sb("mag", [P, 2, CODES], I16)
        neg = sb("neg", [P, 2, CODES], I16)
        magf = sb("magf", [P, 2, CODES], BF16)
        sign = sb("sign", [P, 2, CODES], BF16)
        a = sb("a", [P, 2, CODES], BF16)
        b = sb("b", [P, 2, CODES], BF16)
        w = sb("w", [P, 2, 2 * CODES])
        banks = [pb(f"bank{i}", [P, 512]) for i in range(4)]
        (bits, magf_ready, sign_ready, chain, magf_used, sign_used, low, high, turned, evac) = [sem(n) for n in (
            "bits", "magf_ready", "sign_ready", "chain", "magf_used", "sign_used", "low", "high", "turned",
            "evac")]
        codes_in = [sem(f"codes_in{m}") for m in range(3)]
        NTURN = 2 * CODES // 512

        def scaled(eng, m, k, done):
            if m >= 2:
                eng.wait_ge(turned, NTURN * (m - 1))
            out = w[:, m % 2, :].rearrange("p (n i two) -> p n i two", i=BLK // 2, two=2)[:, :, :, k]
            eng.tensor_tensor(out, a[:, k, :].rearrange("p (n i) -> p n i", i=BLK // 2),
                              scales[:, m, :].unsqueeze(2).to_broadcast([P, 2 * CODES // BLK, BLK // 2]),
                              ALU.mult).then_inc(done, 1)

        with nc.Block() as block:

            @block.sync
            def _(sp):
                for m, (codes_d, scales_d) in enumerate(mats):
                    sp.dma_start(codes[:, m, :].rearrange("p (a n) -> p a n", n=codes_d.shape[1]),
                                 codes_d.rearrange("(a p) n -> p a n", p=P)).then_inc(codes_in[m], 16)
                    sp.dma_start(scales[:, m, :].rearrange("p (a n) -> p a n", n=scales_d.shape[1]),
                                 scales_d.rearrange("(a p) n -> p a n", p=P)).then_inc(codes_in[m], 16)

            @block.vector
            def _(dve):
                me = Tally(chain)

                def run(ins):
                    me.mark(ins)
                    me.done(dve)

                def take_bits(m):
                    dve.wait_ge(codes_in[m], 32)
                    src = codes[:, m, :].bitcast(I16).rearrange("p (n two) -> p n two", two=2)[:, :, 0]
                    for out, bit in ((mag, 7), (neg, 8)):
                        dve.tensor_scalar(out[:, 0, :], src, bit, None, ALU.bitwise_and).then_inc(bits, 1)
                        dve.tensor_scalar(out[:, 1, :], src, 4, bit, ALU.logical_shift_right,
                                          ALU.bitwise_and).then_inc(bits, 1)
                take_bits(0)
                for m in range(3):
                    dve.wait_ge(magf_ready, m + 1)
                    dve.wait_ge(sign_ready, m + 1)
                    if m < 2:
                        take_bits(m + 1)
                    if m:
                        dve.wait_ge(high, m)
                        dve.wait_ge(low, m)
                    run(dve.tensor_scalar(a[:, :, :], magf[:, :, :], -4.0, 0.0, ALU.add, ALU.max))
                    run(dve.tensor_scalar(b[:, :, :], magf[:, :, :], -6.0, 0.0, ALU.add, ALU.max))
                    run(dve.tensor_tensor(a[:, :, :], a[:, :, :], magf[:, :, :], ALU.add))
                    dve.sem_inc(magf_used, 1)
                    run(dve.tensor_tensor(a[:, :, :], a[:, :, :], b[:, :, :], ALU.add))
                    run(dve.tensor_tensor(a[:, :, :], a[:, :, :], b[:, :, :], ALU.add))
                    dve.tensor_tensor(a[:, :, :], a[:, :, :], sign[:, :, :], ALU.mult).then_inc(sign_used, 1)
                    dve.wait_ge(sign_used, m + 1)
                    scaled(dve, m, 0, low)

            @block.gpsimd
            def _(pool):
                for m in range(3):
                    pool.wait_ge(codes_in[m], 32)
                    pool.wait_ge(sign_used, m + 1)
                    scaled(pool, m, 1, high)

            def turns():
                for m in range(3):
                    for n in range(NTURN):
                        if m < 2:
                            cols = [((2 * n + i) * H + c * P) for c in range(CT) for i in range(2)]
                            out = w1T[:, m, :, 2 * n * P:(2 * n + 2) * P]
                        else:
                            cols = [(c * MLP + (2 * n + i) * P) for i in range(2) for c in range(CT)]
                            out = w2T[:, 2 * n:2 * n + 2, :]
                        yield m, n, cols, out

            @block.tensor
            def _(pe):
                for q, (m, n, cols, _) in enumerate(turns()):
                    if n == 0:
                        pe.wait_ge(low, m + 1)
                        pe.wait_ge(high, m + 1)
                    if q >= 4:
                        pe.wait_ge(evac, q - 3)
                    for i, c in enumerate(cols):
                        mm = pe.transpose(banks[q % 4][:, i * P:(i + 1) * P], w[:, m % 2, c:c + P], g.ident[:, :])
                    mm.then_inc(turned, 1)

            @block.scalar
            def _(act):
                def as_floats(m):
                    act.wait_ge(bits, 4 * m + 4)
                    if m:
                        act.wait_ge(magf_used, m)
                    act.activation(magf[:, :, :], mag[:, :, :], ACT.Copy).then_inc(magf_ready, 1)
                    if m:
                        act.wait_ge(sign_used, m)
                    act.activation(sign[:, :, :], neg[:, :, :], ACT.Copy, bias=0.5, scale=-0.125
                                   ).then_inc(sign_ready, 1)

                as_floats(0)
                for q, (m, n, cols, out) in enumerate(turns()):
                    if n == 0 and m < 2:
                        as_floats(m + 1)
                    act.wait_ge(turned, q + 1)
                    act.activation(out, banks[q % 4][:, :].rearrange("p (a n) -> p a n", a=2), ACT.Copy).then_inc(evac, 1)


def feed_forward(nc, g, w1T, w2T):
    with ExitStack() as ctx:
        sem = lambda n: nc.alloc_semaphore(f"ff_{n}")
        sb = lambda n, s, d=F32: ctx.enter_context(nc.sbuf_tensor(f"ff_{n}", s, d))
        pb = lambda n, s, d=F32: ctx.enter_context(nc.psum_tensor(f"ff_{n}", s, d))
        xn = sb("xn", [P, 2, H])
        xT = sb("xT", [P, 2, CT, P])
        gelu = sb("gelu", [P, 2, 512])
        hid = sb("hid", [P, 2, 512])
        hidT = sb("hidT", [P, 2, 4, P])
        G = [pb(f"G{i}", [P, 512]) for i in range(2)]
        U = [pb(f"U{i}", [P, 512]) for i in range(2)]
        TH = [pb(f"TH{i}", [P, 512]) for i in range(2)]
        O, X = pb("O", [P, 512]), pb("X", [P, 512])
        normed, turned, xT_ready, gu_done, gelu_ready, h_ready, h_turned, hT_ready, d_done, y_ready = [
            sem(n) for n in ("normed", "turned", "xT_ready", "gu_done", "gelu_ready", "h_ready", "h_turned",
                             "hT_ready", "d_done", "y_ready")]

        def slices(eng, tile, step, lag):
            for j in range(8):
                if j % 4 == 0:
                    tile(j // 4, j // 4)
                step(j // 4, j, j, [k for k in range(lag + 1) if k <= j])
            with eng.Fori(1, NT // 2) as b:
                for j in range(8):
                    if j % 4 == 0:
                        tile(b * 2 + j // 4, j // 4)
                    step(b * 2 + j // 4, b * 8 + j, j, list(range(lag + 1)))
            for j in range(lag):
                step(NT, 4 * NT + j, j, [k for k in range(lag + 1) if k > j])

        with nc.Block() as block:

            @block.vector
            def _(dve):
                def tile(t, u):
                    if not isinstance(t, int) or t >= 2:
                        dve.wait_ge(turned, t - 1)
                    dve.tensor_scalar(xn[:, u, :], g.x[:, t, :], g.mean[:, bass.ds(t, 1)],
                                      g.rstd[:, bass.ds(t, 1)], ALU.subtract, ALU.mult).then_inc(normed, 1)

                def step(t, n, j, live):
                    if 0 in live:
                        s = j % 2
                        dve.wait_ge(gelu_ready, n + 1)
                        if not isinstance(n, int) or n >= 2:
                            dve.wait_ge(h_turned, n - 1)
                        dve.tensor_tensor(hid[:, s, :], gelu[:, s, :], U[s][:, :], ALU.mult).then_inc(h_ready, 1)
                slices(dve, tile, step, 0)

            @block.scalar
            def _(act):
                def tile(t, u):
                    act.wait_ge(turned, t + 1)
                    if not isinstance(t, int) or t >= 2:
                        act.wait_ge(gu_done, t * 4 - 4)
                    act.activation(xT[:, u, :, :].rearrange("p c n -> p (c n)"), X[:, 0:H],
                                   ACT.Copy).then_inc(xT_ready, 1)

                def step(t, n, j, live):
                    if 0 in live:
                        s = j % 2
                        act.wait_ge(gu_done, n + 1)
                        if not isinstance(n, int) or n >= 2:
                            act.wait_ge(h_ready, n - 1)
                        act.activation(gelu[:, s, :], G[s][:, :], ACT.Gelu_apprx_tanh).then_inc(gelu_ready, 1)
                    if 1 in live:
                        s = (j - 1) % 2
                        act.wait_ge(h_turned, n)
                        if not isinstance(n, int) or n >= 3:
                            act.wait_ge(d_done, n - 2)
                        act.activation(hidT[:, s, :, :].rearrange("p k n -> p (k n)"), TH[s][:, :],
                                       ACT.Copy).then_inc(hT_ready, 1)
                    if 2 in live and j % 4 == 1:
                        act.wait_ge(d_done, n - 1)
                        act.activation(g.y[:, t - 1, :], O[:, 0:H], ACT.Copy).then_inc(y_ready, 1)

                def guarded(t, n, j, live):
                    if isinstance(n, int) and n < 4:
                        live = [k for k in live if k < 2]
                    step(t, n, j, live)
                slices(act, tile, guarded, 2)

            @block.tensor
            def _(pe):
                def tile(t, u):
                    pe.wait_ge(normed, t + 1)
                    if not isinstance(t, int) or t >= 1:
                        pe.wait_ge(xT_ready, t)
                    for c in range(CT):
                        mm = pe.transpose(X[:, c * P:(c + 1) * P], xn[:, u, c * P:(c + 1) * P], g.ident[:, :])
                    mm.then_inc(turned, 1)

                def step(t, n, j, live):
                    if 0 in live:
                        s, u = j % 2, (j // 4) % 2
                        pe.wait_ge(xT_ready, t + 1)
                        if not isinstance(n, int) or n >= 2:
                            pe.wait_ge(h_ready, n - 1)
                        for i, bank in enumerate((G[s], U[s])):
                            for c in range(CT):
                                mm = pe.matmul(bank[:, :], xT[:, u, c, :],
                                               w1T[:, i, c, (j % 4) * 512:(j % 4 + 1) * 512],
                                               start=(c == 0), stop=(c == CT - 1))
                        mm.then_inc(gu_done, 1)
                    if 1 in live:
                        s = (j - 1) % 2
                        pe.wait_ge(h_ready, n)
                        if not isinstance(n, int) or n >= 3:
                            pe.wait_ge(hT_ready, n - 2)
                        for k in range(4):
                            mm = pe.transpose(TH[s][:, k * P:(k + 1) * P], hid[:, s, k * P:(k + 1) * P],
                                              g.ident[:, :])
                        mm.then_inc(h_turned, 1)
                    if 2 in live:
                        s, jj = j % 2, (j - 2) % 4
                        pe.wait_ge(hT_ready, n - 1)
                        if jj == 0:
                            pe.wait_ge(y_ready, t)
                        for k in range(4):
                            mm = pe.matmul(O[:, 0:H], hidT[:, s, k, :], w2T[:, jj * 4 + k, :],
                                           start=(jj == 0 and k == 0), stop=(jj == 3 and k == 3))
                        mm.then_inc(d_done, 1)
                slices(pe, tile, step, 2)


def mlp4(nc, g, gate, gate_s, up, up_s, down, down_s):
    with ExitStack() as ctx:
        w1T = ctx.enter_context(nc.sbuf_tensor("m4_w1T", [P, 2, CT, MLP], F32))
        w2T = ctx.enter_context(nc.sbuf_tensor("m4_w2T", [P, MT, H], F32))
        unpack(nc, g, w1T, w2T, ((gate, gate_s), (up, up_s), (down, down_s)))
        feed_forward(nc, g, w1T, w2T)


def build_program(nc, hidden, Wq, bq, Wk, bk, Wv, bv, router_w, gate_up, down, shared_gate, shared_up, shared_down,
                  in_w, conv_w, conv_b, z_bias, D, out_w, gate4, gate4_s, up4, up4_s, down4, down4_s, out):
    g = Shared()
    dram = lambda n, s, d=F32: nc.dram_tensor(f"rest_{n}", s, d, kind="Internal").ap()
    g.q_dram, g.v_dram = dram("q", (T, H)), dram("v", (TP, NH * VW))
    g.qk_dram, g.gq_dram = dram("qk", (3, 2 * H, T), BF16), dram("gq", (3, H, SLOTS), BF16)
    g.c_dram, g.x_dram = dram("c", (T, H)), dram("x", (T, H))
    g.xr_dram, g.yr_dram = dram("xr", (NS * P, H)), dram("yr", (NS * P, H))
    g.ac_dram, g.rep_dram = dram("ac", (3, VH, T), BF16), dram("rep", (2, VH, T))
    with ExitStack() as ctx:
        sb = lambda n, s, d=F32: ctx.enter_context(nc.sbuf_tensor(n, s, d))
        g.x, g.y = sb("x", [P, NT, H]), sb("y", [P, NT, H])
        g.ident, g.identb = sb("ident", [P, P]), sb("identb", [P, P], BF16)
        g.mean, g.rstd = sb("mean", [P, NT]), sb("rstd", [P, NT])
        g.slot = sb("slot", [P, NT], U32)
        with nc.cleanup_on_exit(), ExitStack() as att:
            constants(nc, g, hidden)
            residual_and_stats(nc, g, None, True, "ln0")
            g.norms = att.enter_context(nc.sbuf_tensor("norms", [NH, T], F32))
            g.places = att.enter_context(nc.sbuf_tensor("places", [SLOTS, NH], U32))
            project(nc, g, Wq, bq, Wk, bk, Wv, bv)
            pick_queries(nc, g)
            g.kst = att.enter_context(nc.sbuf_tensor("kst", [KALL, 2, HG, TP], BF16))
            local_attention(nc, g)
            global_attention(nc, g)
        with nc.cleanup_on_exit():
            take_attention(nc, g)
            residual_and_stats(nc, g, g.y, False, "ln1")
            mixture(nc, g, router_w, gate_up, down, shared_gate, shared_up, shared_down)
            gather_routed(nc, g)
        with nc.cleanup_on_exit():
            residual_and_stats(nc, g, g.y, False, "ln2")
            state_space(nc, g, in_w, conv_w, conv_b, z_bias, D, out_w)
        with nc.cleanup_on_exit():
            residual_and_stats(nc, g, g.y, False, "ln3")
            mlp4(nc, g, gate4, gate4_s, up4, up4_s, down4, down4_s)
            residual_and_stats(nc, g, g.y, False, "ln4", out)


INPUTS = ['L0_attn_hidden_states', 'L0_attn_Wq', 'L0_attn_bq', 'L0_attn_Wk', 'L0_attn_bk', 'L0_attn_Wv',
          'L0_attn_bv', 'L0_ffn_router_w', 'L0_ffn_gate_up_proj', 'L0_ffn_down_proj', 'L0_ffn_shared_gate_w',
          'L0_ffn_shared_up_w', 'L0_ffn_shared_down_w', 'L1_attn_in_proj_w', 'L1_attn_conv1d_weight',
          'L1_attn_conv1d_bias', 'L1_attn_z_bias', 'L1_attn_D', 'L1_attn_out_proj_w', 'L1_ffn_gate_W_packed',
          'L1_ffn_gate_scales', 'L1_ffn_up_W_packed', 'L1_ffn_up_scales', 'L1_ffn_down_W_packed',
          'L1_ffn_down_scales']


def kernel(**inputs):
    import numpy as np
    import concourse.bacc as bacc
    from concourse.bass_utils import run_bass_kernel_spmd

    nc = bacc.Bacc("TRN2", target_bir_lowering=False, num_devices=1)
    arrays, args = {}, []
    for name in INPUTS:
        a = np.ascontiguousarray(inputs[name])
        arrays[f"in_{name}"] = a
        args.append(nc.dram_tensor(f"in_{name}", a.shape, mybir.dt.from_np(a.dtype), kind="ExternalInput").ap())
    out = nc.dram_tensor("out_0", (1, T, H), F32, kind="ExternalOutput").ap()
    build_program(nc, *args, out)
    r = run_bass_kernel_spmd(nc, [arrays], core_ids=[0])
    return r.results[0]["out_0"]
```

```python
import concourse.bass as bass
import numpy as np
from concourse import mybir
from contextlib import ExitStack

F32 = mybir.dt.float32
BF16 = mybir.dt.bfloat16
I32 = mybir.dt.int32
U32 = mybir.dt.uint32
I16 = mybir.dt.int16
ALU = mybir.AluOpType
ACT = mybir.ActivationFunctionType
AX = mybir.AxisListType

P = 128
T = 2048
NT = T // P
H = 256
CT = H // P
EPS = 1e-5

NH, HD = 16, 16
HG = 4
NG = NH // HG
HALF = 64
TP = T + 2 * HALF
SLOTS = 64
VW = 32
SUM = HD
COMBOS = [(0, 0), (0, 1), (0, 2), (1, 0), (1, 1), (2, 0)]
KS = len(COMBOS) * HD
PADROW = KS
KMAX, KALL = KS + 1, P
MW = KALL - KS
PAD_SCORE = -1e30
ONES = float(np.array([0x3F803F80], np.uint32).view(np.float32)[0])


class Shared:
    pass


class Tally:

    def __init__(self, sem):
        self.sem, self.n = sem, 0

    def mark(self, ins):
        ins.then_inc(self.sem, 1)
        self.n = self.n + 1
        return self.n

    def done(self, eng):
        eng.wait_ge(self.sem, self.n)


def residual_and_stats(nc, g, y, first, name, out=None, source=None, routed=False, counted=False):
    with ExitStack() as ctx:
        sem = lambda n: nc.alloc_semaphore(f"{name}_{n}")
        sb = lambda n, s, d=F32: ctx.enter_context(nc.sbuf_tensor(f"{name}_{n}", s, d))
        stats = g.stats
        mv = sb("mv", [P, NT, 2])
        ve = sb("ve", [P, NT])
        sd = sb("sd", [P, NT])
        shift = sb("shift", [P, NT])
        chain, y_var, y_sd, y_scale, y_norm, x_new, x_var, x_sd, stored = [
            sem(n) for n in ("chain", "y_var", "y_sd", "y_scale", "y_norm", "x_new", "x_var", "x_sd", "stored")]
        QT = NT // 4
        if source is not None:
            y_in = [sem(f"y_in{q}") for q in range(4)]
        if routed:
            yg = sb("yg", [P, NT, H])
            gathered = [sem(f"gathered{t}") for t in range(NT)]
            y_added = sem("y_added")
        with nc.Block() as block:

            if routed:
                @block.gpsimd
                def _(pool):
                    for t in range(NT):
                        pool.indirect_dma_start(out=yg[:, t, :], out_offset=None, in_=g.yr_dram,
                                                in_offset=bass.IndirectOffsetOnAxis(ap=g.slot[:, t:t + 1], axis=0)
                                                ).then_inc(gathered[t], 16)

            if source is not None:
                @block.sync
                def _(sp):
                    for q in range(4):
                        sp.dma_start(y[:, q * QT:(q + 1) * QT, :],
                                     source.rearrange("(t p) c -> p t c", p=P)[:, q * QT:(q + 1) * QT, :]
                                     ).then_inc(y_in[q], 16)

            @block.vector
            def _(dve):
                own = Tally(chain)

                def finish(var_sem, sd_sem):
                    own.done(dve)
                    for t in range(NT):
                        own.mark(dve.bn_aggr(mv[:, t, :], stats[:, t, :]))
                    own.done(dve)
                    dve.tensor_scalar(ve[:, :], mv[:, :, 1], EPS, None, ALU.add).then_inc(var_sem, 1)
                    own.mark(dve.tensor_copy(g.mean[:, :], mv[:, :, 0]))
                    dve.wait_ge(sd_sem, 1)
                    own.mark(dve.reciprocal(g.rstd[:, :], sd[:, :]))
                    own.done(dve)

                if not first:
                    if routed:
                        for t in range(NT):
                            dve.wait_ge(gathered[t], 16)
                            dve.tensor_tensor(y[:, t, :], y[:, t, :], yg[:, t, :], ALU.add).then_inc(y_added, 1)
                            if t:
                                dve.wait_ge(y_added, t)
                                dve.bn_stats(stats[:, t - 1, :], y[:, t - 1, :]).then_inc(chain, 1)
                        dve.wait_ge(y_added, NT)
                        dve.bn_stats(stats[:, NT - 1, :], y[:, NT - 1, :]).then_inc(chain, 1)
                    elif source is not None:
                        for t in range(NT):
                            dve.wait_ge(y_in[t // QT], 16)
                            dve.bn_stats(stats[:, t, :], y[:, t, :]).then_inc(chain, 1)
                    if not counted:
                        own.n = NT
                    finish(y_var, y_sd)
                    dve.scalar_tensor_tensor(out=shift[:, :], in0=g.mean[:, :], scalar=-1.0, in1=g.rstd[:, :],
                                             op0=ALU.mult, op1=ALU.mult).then_inc(y_scale, 1)
                    with dve.Fori(0, NT // 4) as b:
                        for t in range(4):
                            dve.wait_ge(y_norm, b * 4 + t + 1)
                            dve.tensor_tensor(g.x[:, b * 4 + t, :], g.x[:, b * 4 + t, :], y[:, b * 4 + t, :],
                                              ALU.add).then_inc(x_new, 1)
                        if out is None:
                            dve.wait_ge(x_new, b * 4 + 4)
                            for t in range(4):
                                dve.bn_stats(stats[:, b * 4 + t, :], g.x[:, b * 4 + t, :]).then_inc(chain, 1)
                else:
                    with dve.Fori(0, NT // 4) as b:
                        for t in range(4):
                            dve.bn_stats(stats[:, b * 4 + t, :], g.x[:, b * 4 + t, :]).then_inc(chain, 1)
                if out is None:
                    own.n += NT
                    finish(x_var, x_sd)

            if out is not None:
                @block.sync
                def _(sp):
                    for q in range(4):
                        sp.wait_ge(x_new, (q + 1) * NT // 4)
                        sp.dma_start(out.rearrange("a (t p) c -> p (a t) c", p=P)[:, q * NT // 4:(q + 1) * NT // 4, :],
                                     g.x[:, q * NT // 4:(q + 1) * NT // 4, :]).then_inc(stored, 16)
                    sp.wait_ge(stored, 64)

            @block.scalar
            def _(act):
                if not first:
                    act.wait_ge(y_var, 1)
                    act.activation(sd[:, :], ve[:, :], ACT.Sqrt).then_inc(y_sd, 1)
                    act.wait_ge(y_scale, 1)
                    with act.Fori(0, NT // 4) as b:
                        for u in range(4):
                            t = b * 4 + u
                            act.activation(y[:, t, :], y[:, t, :], ACT.Identity, bias=shift[:, bass.ds(t, 1)],
                                           scale=g.rstd[:, bass.ds(t, 1)]).then_inc(y_norm, 1)
                if out is None:
                    act.wait_ge(x_var, 1)
                    act.activation(sd[:, :], ve[:, :], ACT.Sqrt).then_inc(x_sd, 1)


def constants(nc, g, hidden):
    zeroed, made, loaded, rows = [nc.alloc_semaphore(f"const_{n}") for n in ("zeroed", "made", "loaded", "rows")]
    with nc.Block() as block:
        @block.vector
        def _(dve):
            k2 = g.kst.bitcast(F32)
            n = 0
            for r0, r1, e, cols, value in ((PADROW, KALL, slice(0, 2), (0, TP), ONES),
                                           (PADROW, KMAX, 0, (0, TP), 0.0),
                                           (0, PADROW, slice(0, 2), (0, HALF), 0.0),
                                           (0, PADROW, slice(0, 2), (HALF + T, TP), 0.0)):
                dve.memset(k2[r0:r1, e, :, cols[0] // 2:cols[1] // 2], value).then_inc(rows, 1)
                n += 1
                dve.wait_ge(rows, n)
            dve.wait_ge(made, 4)
            for cols in ((0, HALF), (HALF + T, TP)):
                dve.memset(g.kst[PADROW:KMAX, :, :, cols[0]:cols[1]], PAD_SCORE).then_inc(rows, 1)
                n += 1
                dve.wait_ge(rows, n)

        @block.gpsimd
        def _(pool):
            pool.memset(g.ident[:, :], 0.0).then_inc(zeroed, 1)
            pool.wait_ge(zeroed, 1)
            pool.affine_select(out=g.ident[:, :], in_=g.ident[:, :], compare_op=ALU.not_equal,
                               fill=1.0, base=0, pattern=[[-1, P]],
                               channel_multiplier=1).then_inc(made, 1)
            pool.wait_ge(made, 1)
            pool.tensor_copy(g.identb[:, :], g.ident[:, :]).then_inc(made, 1)
            pool.wait_ge(made, 2)
            pool.memset(g.qst.bitcast(F32)[PADROW:KALL, :, :, :], ONES).then_inc(made, 1)
            pool.wait_ge(made, 3)
            pool.wait_ge(rows, 1)
            pool.memset(g.kst.bitcast(F32)[PADROW:KMAX, 1, :, :], 0.0).then_inc(made, 1)

        @block.sync
        def _(sp):
            sp.dma_start(g.x[:, :, :], hidden.rearrange("a (t p) c -> p (a t) c", p=P)).then_inc(loaded, 16)
            sp.wait_ge(loaded, 16)


def tiles(n):
    return max(n, 0) if isinstance(n, int) else n


def pipelined(eng, step):
    for i in range(4):
        step(i, [k for k in range(3) if k <= i], i % 2)
    with eng.Fori(2, NT // 2) as b:
        for u in range(2):
            step(b * 2 + u, [0, 1, 2], u)
    for i in range(NT, NT + 2):
        step(i, list(range(i - NT + 1, 3)), i - NT)


def project(nc, g, Wq, bq, Wk, bk, Wv, bv):
    with ExitStack() as ctx:
        sem = lambda n: nc.alloc_semaphore(f"proj_{n}")
        sb = lambda n, s, d=F32: ctx.enter_context(nc.sbuf_tensor(f"proj_{n}", s, d))
        pb = lambda n, s, d=F32: ctx.enter_context(nc.psum_tensor(f"proj_{n}", s, d))
        w = sb("w", [P, 3, CT, H])
        bqk = sb("bqk", [P, 2 * CT])
        bvb = sb("bvb", [P, H])
        heads = sb("heads", [P, CT, NH])
        xn = sb("xn", [P, 2, H])
        xnT = sb("xnT", [P, 2, CT, P])
        qkf = sb("qkf", [P, 2, 2 * CT, P])
        rest = sb("rest", [P, 2, 2 * CT, P])
        parts = sb("parts", [P, 3, 2 * CT, T], BF16)
        sq = sb("sq", [P, 2, CT, P])
        vrow = sb("vrow", [P, 2, NH, VW])
        qrow = sb("qrow", [P, 2, H])
        zero = sb("zero", [HALF, NH * VW])
        psT = pb("psT", [P, 2, 512])
        psQK = pb("psQK", [P, 2, 2 * CT * P])
        psV = pb("psV", [P, 2, 512])
        psRN = pb("psRN", [P, 2, 512])
        psR, psN = psRN[:, :, 0:H], psRN[0:NH, :, H:H + P]
        (loaded, preset, normed, turned, xT_ready, qk_done, v_done, qk_ready, part1, rest1, part2,
         part3, squared, norm_done, norms_copied, v_ready, qT_done, q_ready, zeroed) = [sem(n) for n in (
             "loaded", "preset", "normed", "turned", "xT_ready", "qk_done", "v_done", "qk_ready",
             "part1", "rest1", "part2", "part3", "squared", "norm_done", "norms_copied", "v_ready",
             "qT_done", "q_ready", "zeroed")]
        parts_out = sem("parts_out")
        v_out = [sem(f"v_out{u}") for u in range(2)]
        q_out = [sem(f"q_out{u}") for u in range(2)]
        pads_out = sem("pads_out")
        NLOAD = 3 + 2 + 1
        with nc.Block() as block:

            @block.sync
            def _(sp):
                for i, m in enumerate((Wq, Wk, Wv)):
                    sp.dma_start(w[:, i, :, :], m.rearrange("(c p) n -> p c n", p=P)).then_inc(loaded, 16)
                for i, m in enumerate((bq, bk)):
                    sp.dma_start(bqk[:, CT * i:CT * (i + 1)], m.rearrange("(c p) -> p c", p=P),
                                 allow_slow_non_contiguous=True).then_inc(loaded, 16)
                sp.dma_start(bvb[:, :], bv.rearrange("(a n) -> a n", a=1).to_broadcast([P, H])).then_inc(loaded, 16)
                sp.wait_ge(zeroed, 1)
                sp.dma_start(g.v_dram[0:HALF, :], zero[:, :]).then_inc(pads_out, 16)
                sp.dma_start(g.v_dram[HALF + T:TP, :], zero[:, :]).then_inc(pads_out, 16)
                with sp.Fori(0, NT // 2) as b:
                    for u in range(2):
                        t = 2 * b + u
                        sp.wait_ge(q_ready, t + 1)
                        sp.dma_start(g.q_dram[bass.ds(t * P, P), :], qrow[:, u, :]).then_inc(q_out[u], 16)
                        sp.wait_ge(v_ready, t + 1)
                        sp.dma_start(g.v_dram[bass.ds(t * P + HALF, P), :],
                                     vrow[:, u, :, :].rearrange("p h w -> p (h w)")).then_inc(v_out[u], 16)
                    sp.wait_ge(part3, 2 * b + 2)
                    for i in range(3):
                        sp.dma_start(
                            g.qk_dram[i, :, bass.ds(b * 2 * P, 2 * P)].rearrange("(m p) n -> p m n", p=P),
                            parts[:, i, :, bass.ds(b * 2 * P, 2 * P)]).then_inc(parts_out, 16)
                for s in (*q_out, *v_out):
                    sp.wait_ge(s, 16 * NT // 2)
                sp.wait_ge(parts_out, 16 * 3 * NT // 2)
                sp.wait_ge(pads_out, 32)

            @block.gpsimd
            def _(pool):
                pool.memset(heads[:, :, :], 1.0).then_inc(preset, 1)
                pool.wait_ge(preset, 1)
                pool.affine_select(out=heads[:, :, :], in_=heads[:, :, :], compare_op=ALU.is_ge, fill=0.0,
                                   base=0, pattern=[[P, CT], [-HD, NH]], channel_multiplier=1).then_inc(preset, 1)
                pool.wait_ge(preset, 2)
                pool.affine_select(out=heads[:, :, :], in_=heads[:, :, :], compare_op=ALU.is_ge, fill=0.0,
                                   base=HD - 1, pattern=[[-P, CT], [HD, NH]], channel_multiplier=-1).then_inc(preset, 1)
                pool.memset(vrow[:, :, :, :], 0.0).then_inc(preset, 1)
                pool.wait_ge(preset, 4)
                pool.memset(vrow[:, :, :, SUM:SUM + 1], 1.0).then_inc(preset, 1)
                pool.memset(zero[:, :], 0.0).then_inc(zeroed, 1)
                with pool.Fori(0, NT // 2) as b:
                    for u in range(2):
                        t = 2 * b + u
                        pool.wait_ge(qk_ready, t + 1)
                        pool.wait_ge(part1, t + 1)
                        pool.wait_ge(part2, 2 * b)
                        pool.wait_ge(part3, 2 * b)
                        pool.tensor_tensor(rest[:, u, :, :], qkf[:, u, :, :],
                                           parts[:, 0, :, bass.ds(t * P, P)], ALU.subtract).then_inc(rest1, 1)
                        pool.wait_ge(part2, t + 1)
                        pool.wait_ge(rest1, t + 1)
                        pool.tensor_tensor(parts[:, 2, :, bass.ds(t * P, P)], rest[:, u, :, :],
                                           parts[:, 1, :, bass.ds(t * P, P)], ALU.subtract).then_inc(part3, 1)

            @block.vector
            def _(dve):
                dve.wait_ge(loaded, 16 * NLOAD)
                dve.wait_ge(preset, 5)

                def step(i, live, u):
                    if 0 in live:
                        dve.wait_ge(turned, tiles(i - 1))
                        dve.tensor_scalar(xn[:, u, :], g.x[:, i, :], g.mean[:, bass.ds(i, 1)],
                                          g.rstd[:, bass.ds(i, 1)], ALU.subtract,
                                          ALU.mult).then_inc(normed, 1)
                    if 1 in live:
                        t, v = i - 1, 1 - u
                        dve.wait_ge(qk_done, t + 1)
                        dve.wait_ge(squared, tiles(t - 1))
                        dve.wait_ge(rest1, tiles(t - 1))
                        dve.wait_ge(qT_done, tiles(t - 1))
                        dve.tensor_tensor(
                            qkf[:, v, :, :], psQK[:, v, :].rearrange("p (m n) -> p m n", n=P),
                            bqk[:, :].unsqueeze(2).to_broadcast([P, 2 * CT, P]), ALU.add).then_inc(qk_ready, 1)
                        dve.wait_ge(v_done, t + 1)
                        dve.wait_ge(v_out[v], tiles(t - v) * 8)
                        dve.tensor_tensor(
                            vrow[:, v, :, 0:HD], psV[:, v, 0:H].rearrange("p (h d) -> p h d", d=HD),
                            bvb[:, :].rearrange("p (h d) -> p h d", d=HD), ALU.add).then_inc(v_ready, 1)
                    if 2 in live:
                        t = i - 2
                        dve.wait_ge(qT_done, t + 1)
                        dve.wait_ge(q_out[u], tiles(t - u) * 8)
                        dve.tensor_copy(qrow[:, u, :], psR[:, u, :]).then_inc(q_ready, 1)
                        dve.tensor_copy(g.norms[:, bass.ds(t * P, P)], psN[:, u, :]).then_inc(norms_copied, 1)
                pipelined(dve, step)

            @block.scalar
            def _(act):
                def step(i, live, u):
                    if 0 in live:
                        act.wait_ge(turned, i + 1)
                        act.wait_ge(v_done, tiles(i - 1))
                        act.activation(xnT[:, u, :, :].rearrange("p c n -> p (c n)"), psT[:, u, 0:H],
                                       ACT.Copy).then_inc(xT_ready, 1)
                    if 1 in live:
                        t, v = i - 1, 1 - u
                        act.wait_ge(qk_ready, t + 1)
                        act.activation(parts[:, 0, :, bass.ds(t * P, P)], qkf[:, v, :, :], ACT.Copy).then_inc(part1, 1)
                        act.wait_ge(norm_done, tiles(t - 1))
                        act.activation(sq[:, v, :, :], qkf[:, v, 0:CT, :], ACT.Square).then_inc(squared, 1)
                        act.wait_ge(rest1, t + 1)
                        act.activation(parts[:, 1, :, bass.ds(t * P, P)], rest[:, v, :, :], ACT.Copy).then_inc(part2, 1)
                pipelined(act, step)

            @block.tensor
            def _(pe):
                pe.wait_ge(loaded, 16 * NLOAD)
                pe.wait_ge(preset, 5)

                def step(i, live, u):
                    if 0 in live:
                        pe.wait_ge(normed, i + 1)
                        pe.wait_ge(xT_ready, tiles(i - 1))
                        for c in range(CT):
                            mm = pe.transpose(psT[:, u, c * P:(c + 1) * P], xn[:, u, c * P:(c + 1) * P],
                                              g.ident[:, :])
                        mm.then_inc(turned, 1)
                    if 1 in live:
                        t, v = i - 1, 1 - u
                        pe.wait_ge(xT_ready, t + 1)
                        pe.wait_ge(qk_ready, tiles(t - 1))
                        for m in range(2 * CT):
                            for c in range(CT):
                                mm = pe.matmul(psQK[:, v, m * P:(m + 1) * P],
                                               w[:, m // CT, c, (m % CT) * P:(m % CT + 1) * P],
                                               xnT[:, v, c, :], start=(c == 0), stop=(c == CT - 1))
                        mm.then_inc(qk_done, 1)
                        pe.wait_ge(v_ready, tiles(t - 1))
                        for c in range(CT):
                            mm = pe.matmul(psV[:, v, 0:H], xnT[:, v, c, :], w[:, 2, c, :],
                                           start=(c == 0), stop=(c == CT - 1))
                        mm.then_inc(v_done, 1)
                    if 2 in live:
                        t = i - 2
                        pe.wait_ge(squared, t + 1)
                        pe.wait_ge(norms_copied, tiles(t - 1))
                        pe.wait_ge(q_ready, tiles(t - 1))
                        for c in range(CT):
                            mm = pe.matmul(psN[:, u, :], heads[:, c, :], sq[:, u, c, :],
                                           start=(c == 0), stop=(c == CT - 1))
                        mm.then_inc(norm_done, 1)
                        for c in range(CT):
                            mm = pe.transpose(psR[:, u, c * P:(c + 1) * P], qkf[:, u, c, :], g.ident[:, :])
                        mm.then_inc(qT_done, 1)
                pipelined(pe, step)

def pick_queries(nc, g):
    with ExitStack() as ctx:
        sem = lambda n: nc.alloc_semaphore(f"pick_{n}")
        sb = lambda n, s, d=F32: ctx.enter_context(nc.sbuf_tensor(f"pick_{n}", s, d))
        pb = lambda n, s, d=F32: ctx.enter_context(nc.psum_tensor(f"pick_{n}", s, d))
        hrow = sb("hrow", [SLOTS, NH])
        gq = sb("gq", [SLOTS, NH, HD])
        gp = sb("gp", [P, 3, CT, SLOTS], BF16)
        gf = sb("gf", [P, CT, SLOTS])
        gr = sb("gr", [P, CT, SLOTS])
        psI = pb("psI", [SLOTS, 512])
        psQ = pb("psQ", [P, 512])
        (own, found, turned, hrow_ready, placed, gathered, q_turned, split, stored) = [sem(n) for n in (
            "own", "found", "turned", "hrow_ready", "placed", "gathered", "q_turned", "split", "stored")]
        with nc.Block() as block:

            @block.vector
            def _(dve):
                me = Tally(own)
                me.mark(dve.memset(g.idxf[:, SLOTS - 2:SLOTS - 1], 0.0))
                me.done(dve)
                dve.memset(g.idxf[:, SLOTS - 1:SLOTS], float(T - 1)).then_inc(found, 1)
                dve.wait_ge(turned, 1)
                dve.wait_ge(hrow_ready, 1)
                dve.scalar_tensor_tensor(out=g.places[:, :], in0=psI[:, 0:NH], scalar=float(NH),
                                         in1=hrow[:, :], op0=ALU.mult, op1=ALU.add).then_inc(placed, 1)
                dve.wait_ge(q_turned, 1)
                src = psQ[:, 0:CT * SLOTS].rearrange("p (c s) -> p c s", s=SLOTS)
                me.mark(dve.tensor_copy(gf[:, :, :], src))
                me.done(dve)
                me.mark(dve.tensor_copy(gp[:, 0, :, :], gf[:, :, :]))
                me.done(dve)
                me.mark(dve.tensor_tensor(gr[:, :, :], gf[:, :, :], gp[:, 0, :, :], ALU.subtract))
                me.done(dve)
                me.mark(dve.tensor_copy(gp[:, 1, :, :], gr[:, :, :]))
                me.done(dve)
                dve.tensor_tensor(gp[:, 2, :, :], gr[:, :, :], gp[:, 1, :, :], ALU.subtract).then_inc(split, 1)

            @block.gpsimd
            def _(pool):
                pool.iota(hrow[:, :], pattern=[[1, NH]], base=0, channel_multiplier=0,
                          allow_small_or_imprecise_dtypes=True).then_inc(hrow_ready, 1)
                pool.wait_ge(placed, 1)
                for h in range(NH):
                    pool.indirect_dma_start(
                        out=gq[:, h, :], out_offset=None,
                        in_=g.q_dram.rearrange("t (h d) -> (t h) d", d=HD),
                        in_offset=bass.IndirectOffsetOnAxis(ap=g.places[:, h:h + 1], axis=0)).then_inc(gathered, 16)

            @block.tensor
            def _(pe):
                pe.wait_ge(found, 1)
                pe.transpose(psI[:, 0:NH], g.idxf[:, :], g.ident[0:NH, 0:NH]).then_inc(turned, 1)
                pe.wait_ge(gathered, 16 * NH)
                rows = gq[:, :, :].rearrange("s h d -> s (h d)")
                for c in range(CT):
                    mm = pe.transpose(psQ[:, c * SLOTS:(c + 1) * SLOTS], rows[:, c * P:(c + 1) * P],
                                      g.ident[0:SLOTS, 0:SLOTS])
                mm.then_inc(q_turned, 1)

            @block.sync
            def _(sp):
                sp.wait_ge(split, 1)
                for i in range(3):
                    sp.dma_start(g.gq_dram[i, :, :].rearrange("(c p) s -> p c s", p=P),
                                 gp[:, i, :, :]).then_inc(stored, 16)
                sp.wait_ge(stored, 48)


def load_stack(sp, dst, source, which, width, cols, sem):
    for c, combo in enumerate(COMBOS):
        sp.dma_start(dst[c * HD:(c + 1) * HD, :, cols:cols + width],
                     source[combo[which], :, :, :].rearrange("h d n -> d h n")).then_inc(sem, 16)


NB = NT
PRE = 8
VR = 4


def before(n0, i):
    return n0 + (max(i, 0) if isinstance(i, int) else i)


def head_groups(eng, step, lag, each=None):
    with eng.Fori(0, NG // 2) as hp:
        for e in range(2):
            n0 = hp * (2 * NB) + e * NB
            if each is not None:
                each(hp, e, n0)
            for i in range(PRE):
                step(e, n0, i, i, [k for k in range(lag + 1) if k <= i])
            with eng.Fori(PRE // 4, NB // 4) as b:
                for j in range(4):
                    step(e, n0, b * 4 + j, j, list(range(lag + 1)))
            for i in range(NB, NB + lag):
                step(e, n0, i, i, [k for k in range(lag + 1) if k > i - NB])


def local_attention(nc, g):
    with ExitStack() as ctx:
        sem = lambda n: nc.alloc_semaphore(f"loc_{n}")
        sb = lambda n, s, d=F32: ctx.enter_context(nc.sbuf_tensor(f"loc_{n}", s, d))
        pb = lambda n, s, d=F32: ctx.enter_context(nc.psum_tensor(f"loc_{n}", s, d))
        kst = g.kst
        qst = g.qst
        top = sb("top", [NH, 8])
        place8 = sb("place8", [NH, 8], U32)
        nmax = sb("nmax", [P, 2, HG])
        zero = sb("zero", [P, HG])
        mparts = sb("mparts", [P, 2, HG, MW], BF16)
        probs = sb("probs", [P, 2, HG, 2, P])
        vt = sb("vt", [P, VR, 2, HG * VW])
        oT = sb("oT", [P, 2, P])
        rden = sb("rden", [P, 2, HG])
        cx = sb("cx", [P, 2, HG, HD])
        psS = pb("psS", [P, 2, HG, 2 * P])
        psX = pb("psX", [P, HG, 2, P])
        psM = pb("psM", [P, HG * P])
        psO = pb("psO", [P, 4 * P])
        (own, preset, scored, maxed, mchain, split, rows_done, rows_copied, x_done, exp_done, pv_done,
         oT_copied, back, den_ready, cx_ready) = [sem(n) for n in (
             "own", "preset", "scored", "maxed", "mchain", "split", "rows_done", "rows_copied", "x_done",
             "exp_done", "pv_done", "oT_copied", "back", "den_ready", "cx_ready")]
        search_step, search_turn = sem("search_step"), sem("search_turn")
        stacked = [sem(f"stacked{e}") for e in range(2)]
        v_in = [sem(f"v_in{s}") for s in range(VR)]
        cx_out = [sem(f"cx_out{s}") for s in range(2)]
        kq = g.qk_dram.rearrange("i (m h d) t -> i m h d t", m=2, d=HD)

        def turned(i, j):
            return psS[:, (j - 1) % 2, 0, 0:P].rearrange("p (h w) -> p h w", w=VW)

        with nc.Block() as block:

            @block.sync
            def _(sp):
                def stacks(e, h0):
                    load_stack(sp, qst[:, e, :, :], kq[:, 0, h0, :, :], 0, T, 0, stacked[e])
                    load_stack(sp, kst[:, e, :, :], kq[:, 1, h0, :, :], 1, T, HALF, stacked[e])

                def next_stacks(hp, e, n0):
                    sp.wait_ge(x_done, n0)
                    if e == 0:
                        stacks(1, bass.ds(hp * (2 * HG) + HG, HG))
                    else:
                        stacks(0, bass.ds(((hp + 1) % (NG // 2)) * (2 * HG), HG))
                    hg[0] = (hp * 2 + e) * HG

                hg = [0]

                def step(e, n0, i, j, live):
                    if 0 in live:
                        sp.wait_ge(pv_done, before(n0, i - 3))
                        sp.dma_start(vt[:, j % VR, :, :],
                                     g.v_dram[bass.ds(i * P, 2 * P), bass.ds(hg[0] * VW, HG * VW)]
                                     .rearrange("(k p) n -> p k n", p=P)).then_inc(v_in[j % VR], 16)
                    if 5 in live:
                        s = (j - 5) % 2
                        sp.wait_ge(cx_ready, n0 + i - 4)
                        sp.dma_start(g.c_dram[bass.ds((i - 5) * P, P), bass.ds(hg[0] * HD, HG * HD)],
                                     cx[:, s, :, :].rearrange("p h d -> p (h d)")).then_inc(cx_out[s], 16)
                stacks(0, slice(0, HG))
                head_groups(sp, step, 5, next_stacks)
                for s in cx_out:
                    sp.wait_ge(s, 16 * NG * NB // 2)
                sp.wait_ge(stacked[0], 16 * 12 * 3)
                sp.wait_ge(stacked[1], 16 * 12 * 2)

            @block.gpsimd
            def _(pool):
                me = Tally(own)
                me.mark(pool.memset(zero[:, :], 0.0))
                me.done(pool)
                me.mark(pool.memset(mparts[:, :, :, :], 0.0))
                me.done(pool)
                me.mark(pool.memset(mparts[:, :, :, 0:1], 1.0))
                me.done(pool)
                pool.sem_inc(preset, 1)

                def step(e, n0, i, j, live):
                    s = j % 2
                    pool.wait_ge(maxed, n0 + i + 1)
                    pool.wait_ge(rows_done, before(n0, i - 1))
                    pool.tensor_tensor(mparts[:, s, :, 1], nmax[:, s, :], zero[:, :], ALU.add).then_inc(mchain, 1)
                    pool.wait_ge(mchain, n0 + i + 1)
                    pool.tensor_tensor(mparts[:, s, :, 2], nmax[:, s, :], mparts[:, s, :, 1],
                                       ALU.subtract).then_inc(split, 1)
                head_groups(pool, step, 0)

            @block.vector
            def _(dve):
                group = {}

                def search(i):
                    if not isinstance(i, int) or i not in range(1, 7):
                        return
                    r, part = divmod(i - 1, 3)
                    at = group["n"] * 8 + r * 4
                    if part == 0:
                        dve.wait_ge(search_step, at)
                        dve.sem_inc(search_turn, 1)
                        dve.max(top[:, :], g.norms[:, :]).then_inc(search_step, 1)
                    elif part == 1:
                        dve.wait_ge(search_step, at + 1)
                        dve.sem_inc(search_turn, 1)
                        dve.max_index(place8[:, :], top[:, :], g.norms[:, :]).then_inc(search_step, 1)
                    else:
                        dve.wait_ge(search_step, at + 2)
                        dve.tensor_copy(g.idxf[:, bass.ds(group["n"] * 16 + r * 8, 8)], place8[:, :]
                                        ).then_inc(search_step, 1)
                        dve.match_replace(out=g.norms[:, :], in_to_replace=top[:, :],
                                          in_values=g.norms[:, :], imm_value=-1.0).then_inc(search_step, 1)

                def begin(hp, e, n0):
                    group["n"] = hp * 2 + e

                def step(e, n0, i, j, live):
                    if 4 in live:
                        s = (j - 4) % 2
                        c = turned(i, j)
                        dve.wait_ge(back, n0 + i - 3)
                        dve.reciprocal(rden[:, s, :], c[:, :, SUM]).then_inc(den_ready, 1)
                        dve.wait_ge(den_ready, n0 + i - 3)
                        dve.wait_ge(cx_out[s], (n0 + i - 4 - s) * 8)
                        dve.tensor_tensor(cx[:, s, :, :], c[:, :, 0:HD],
                                          rden[:, s, :].unsqueeze(2).to_broadcast([P, HG, HD]),
                                          ALU.mult).then_inc(cx_ready, 1)
                    if 0 in live:
                        s = j % 2
                        dve.wait_ge(scored, n0 + i + 1)
                        dve.wait_ge(split, before(n0, i - 1))
                        dve.tensor_reduce(out=nmax[:, s, :], in_=psS[:, s, :, :], axis=AX.X, op=ALU.max,
                                          negate=True).then_inc(maxed, 1)
                    search(i)
                head_groups(dve, step, 4, begin)

            @block.scalar
            def _(act):
                def step(e, n0, i, j, live):
                    if 1 in live:
                        act.wait_ge(rows_done, n0 + i)
                        act.activation(qst[PADROW:KALL, e, :, bass.ds((i - 1) * P, P)],
                                       psM[PADROW:KALL, :].rearrange("p (h n) -> p h n", n=P),
                                       ACT.Copy).then_inc(rows_copied, 1)
                    if 2 in live:
                        s = (j - 2) % 2
                        act.wait_ge(x_done, n0 + i - 1)
                        act.wait_ge(pv_done, before(n0, i - 3))
                        act.activation(probs[:, s, :, :, :], psX[:, :, :, :], ACT.Exp,
                                       scale=HD ** -0.5).then_inc(exp_done, 1)
                    if 3 in live:
                        s = (j - 3) % 2
                        act.wait_ge(pv_done, n0 + i - 2)
                        act.wait_ge(back, before(n0, i - 4))
                        act.activation(oT[:, s, :], psO[:, 0:P], ACT.Copy).then_inc(oT_copied, 1)
                head_groups(act, step, 3)

            @block.tensor
            def _(pe):
                pe.wait_ge(preset, 1)

                def arrived(hp, e, n0):
                    pe.wait_ge(stacked[e], hp * (12 * 16) + 12 * 16)

                def step(e, n0, i, j, live):
                    if 0 in live:
                        s = j % 2
                        pe.wait_ge(maxed, before(n0, i - 1))
                        pe.wait_ge(cx_ready, before(n0, i - 4))
                        for h in range(HG):
                            mm = pe.matmul(psS[:, s, h, :], qst[0:KMAX, e, h, bass.ds(i * P, P)],
                                           kst[0:KMAX, e, h, bass.ds(i * P, 2 * P)], start=True, stop=True)
                        mm.then_inc(scored, 1)
                    if 4 in live:
                        s = (j - 4) % 2
                        pe.wait_ge(oT_copied, n0 + i - 3)
                        pe.wait_ge(maxed, n0 + min(i, NB) if isinstance(i, int) else n0 + i)
                        pe.wait_ge(cx_ready, before(n0, i - 5))
                        pe.transpose(psS[:, (j - 1) % 2, 0, 0:P], oT[:, s, :], g.ident[:, :]).then_inc(back, 1)
                    if 1 in live:
                        s = (j - 1) % 2
                        pe.wait_ge(split, n0 + i)
                        pe.wait_ge(rows_copied, n0 + i - 1)
                        for h in range(HG):
                            mm = pe.matmul(psM[PADROW:KALL, h * P:(h + 1) * P], mparts[:, s, h, :],
                                           g.identb[:, :], start=True, stop=True)
                        mm.then_inc(rows_done, 1)
                    if 2 in live:
                        pe.wait_ge(rows_copied, n0 + i - 1)
                        pe.wait_ge(exp_done, n0 + i - 2)
                        for h in range(HG):
                            for k in range(2):
                                mm = pe.matmul(psX[:, h, k, :],
                                               kst[0:KALL, e, h, bass.ds((i - 2) * P + k * P, P)],
                                               qst[0:KALL, e, h, bass.ds((i - 2) * P, P)],
                                               start=True, stop=True)
                        mm.then_inc(x_done, 1)
                    if 3 in live:
                        s = (j - 3) % 2
                        r = (j - 3) % VR
                        pe.wait_ge(exp_done, n0 + i - 2)
                        pe.wait_ge(v_in[r], (n0 + i - 3 - r) * (16 // VR) + 16)
                        pe.wait_ge(oT_copied, n0 + i - 3)
                        for k in range(2):
                            for h in range(HG):
                                mm = pe.matmul(psO[h * VW:(h + 1) * VW, 0:P],
                                               vt[:, r, k, h * VW:(h + 1) * VW],
                                               probs[:, s, h, k, :], start=(k == 0), stop=(k == 1),
                                               skip_group_check=True)
                        mm.then_inc(pv_done, 1)
                head_groups(pe, step, 4, arrived)


def global_attention(nc, g):
    PAIRS = HG // 2
    with ExitStack() as ctx:
        sem = lambda n: nc.alloc_semaphore(f"glo_{n}")
        sb = lambda n, s, d=F32: ctx.enter_context(nc.sbuf_tensor(f"glo_{n}", s, d))
        pb = lambda n, s, d=F32: ctx.enter_context(nc.psum_tensor(f"glo_{n}", s, d))
        kst = g.kst
        gst = sb("gst", [KALL, 2, HG, SLOTS], BF16)
        nmax = sb("nmax", [P, 2])
        zero = sb("zero", [P, 1])
        mparts = sb("mparts", [P, 2, MW], BF16)
        probs = sb("probs", [P, 2, NT, SLOTS])
        vt = sb("vt", [P, 2, NT, HG * VW])
        oT = sb("oT", [P, P])
        rden = sb("rden", [SLOTS, HG])
        gcx = sb("gcx", [SLOTS, 2, HG, HD])
        place = sb("place", [SLOTS, 2, HG], U32)
        psS = pb("psS", [P, T])
        psX = pb("psX", [P, NT, SLOTS])
        psM = pb("psM", [P, 4 * P])
        psO = pb("psO", [P, 4 * P])
        (own, preset, scored, maxed, mchain, split, rows_done, rows_copied, x_done, exp_done, pv_done,
         oT_copied, back, den_ready, cx_ready) = [sem(n) for n in (
             "own", "preset", "scored", "maxed", "mchain", "split", "rows_done", "rows_copied", "x_done",
             "exp_done", "pv_done", "oT_copied", "back", "den_ready", "cx_ready")]
        placed = sem("placed")
        turned_pool = sem("turned_pool")
        turn = sem("turn")
        swapped = [sem(f"swapped{e}") for e in range(2)]
        ends_out = [sem(f"ends_out{e}") for e in range(2)]
        stacked = [sem(f"stacked{e}") for e in range(2)]
        v_in = [sem(f"v_in{e}") for e in range(2)]
        g_in = [sem(f"g_in{e}") for e in range(2)]
        kq = g.qk_dram.rearrange("i (m h d) t -> i m h d t", m=2, d=HD)

        with nc.Block() as block:

            @block.sync
            def _(sp):
                def v_tiles(e, cols):
                    sp.dma_start(vt[:, e, :, :], g.v_dram[HALF:HALF + T, cols]
                                 .rearrange("(k p) n -> p k n", p=P)).then_inc(v_in[e], 16)
                v_tiles(0, slice(0, HG * VW))
                sp.wait_ge(preset, 1)
                gq = g.gq_dram.rearrange("i (h d) s -> i h d s", d=HD)
                load_stack(sp, gst[:, 0, :, :], gq[:, 0:HG, :, :], 0, SLOTS, 0, g_in[0])
                with sp.Fori(0, NG // 2) as hp:
                    for e in range(2):
                        hg = hp * 2 + e
                        sp.wait_ge(pv_done, hg * HG)
                        nxt = (hp * 2 + 1) if e == 0 else ((hp + 1) % (NG // 2)) * 2
                        load_stack(sp, kst[:, 1 - e, :, :], kq[:, 1, bass.ds(nxt * HG, HG), :, :], 1, T, HALF,
                                   stacked[1 - e])
                        load_stack(sp, gst[:, 1 - e, :, :], gq[:, bass.ds(nxt * HG, HG), :, :], 0, SLOTS, 0,
                                   g_in[1 - e])
                        v_tiles(1 - e, bass.ds(nxt * (HG * VW), HG * VW))
                        sp.wait_ge(swapped[e], (hp + 1) * (16 * HG))
                        sp.sem_inc(turn, 1)
                        for s, t in ((SLOTS - 2, 0), (SLOTS - 1, T - 1)):
                            sp.dma_start(g.c_dram[t:t + 1, bass.ds(hg * (HG * HD), HG * HD)],
                                         gcx[s:s + 1, e, :, :].rearrange("s h d -> s (h d)")
                                         ).then_inc(ends_out[e], 16)
                sp.wait_ge(stacked[0], 16 * 6 * NG // 2)
                sp.wait_ge(g_in[0], 16 * 6 * (NG // 2 + 1))
                sp.wait_ge(v_in[0], 16 * (NG // 2 + 1))
                for e in range(2):
                    sp.wait_ge(ends_out[e], 16 * 2 * (NG // 2))

            @block.gpsimd
            def _(pool):
                pool.memset(zero[:, :], 0.0).then_inc(own, 1)
                pool.wait_ge(own, 1)
                pool.memset(oT[:, :], 0.0).then_inc(own, 1)
                pool.wait_ge(own, 2)
                pool.memset(gst[PADROW:KALL, :, :, :], 1.0).then_inc(own, 1)
                pool.wait_ge(own, 3)
                pool.memset(mparts[:, :, :], 0.0).then_inc(own, 1)
                pool.wait_ge(own, 4)
                pool.memset(mparts[:, :, 0:1], 1.0).then_inc(preset, 1)
                with pool.Fori(0, NG // 2) as hp:
                    for e in range(2):
                        hg = hp * 2 + e
                        for s in range(PAIRS):
                            n = hp * (2 * PAIRS) + e * PAIRS + s
                            pool.wait_ge(maxed, n + 1)
                            pool.wait_ge(rows_done, hp * (2 * PAIRS) + e * PAIRS)
                            pool.tensor_tensor(mparts[:, s, 1:2], nmax[:, s:s + 1], zero[:, :],
                                               ALU.add).then_inc(mchain, 1)
                            pool.wait_ge(mchain, n + 1)
                            pool.tensor_tensor(mparts[:, s, 2:3], nmax[:, s:s + 1], mparts[:, s, 1:2],
                                               ALU.subtract).then_inc(split, 1)
                        pool.wait_ge(placed, hg + 1)
                        pool.wait_ge(cx_ready, hg + 1)
                        pool.sem_inc(turned_pool, 1)
                        for h in range(HG):
                            pool.indirect_dma_start(
                                out=g.c_dram.rearrange("t (h d) -> (t h) d", d=HD),
                                out_offset=bass.IndirectOffsetOnAxis(ap=place[0:SLOTS - 2, e, h:h + 1], axis=0),
                                in_=gcx[0:SLOTS - 2, e, h, :], in_offset=None).then_inc(swapped[e], 16)

            @block.vector
            def _(dve):
                with dve.Fori(0, NG // 2) as hp:
                    for e in range(2):
                        hg = hp * 2 + e
                        for s in range(PAIRS):
                            dve.wait_ge(scored, hg * PAIRS + s + 1)
                            dve.wait_ge(split, hg * PAIRS)
                            dve.tensor_reduce(out=nmax[:, s:s + 1], in_=psS[:, :], axis=AX.X, op=ALU.max,
                                              negate=True).then_inc(maxed, 1)
                        c = psM[0:SLOTS, 0:P].rearrange("p (h w) -> p h w", w=VW)
                        dve.wait_ge(back, hg + 1)
                        dve.reciprocal(rden[:, :], c[:, :, SUM]).then_inc(den_ready, 1)
                        dve.wait_ge(den_ready, hg + 1)
                        dve.wait_ge(swapped[e], hp * (16 * HG))
                        dve.wait_ge(ends_out[e], hp * (16 * 2))
                        dve.tensor_copy(place[:, e, :], g.places[:, bass.ds(hg * HG, HG)]).then_inc(placed, 1)
                        dve.tensor_tensor(gcx[:, e, :, :], c[:, :, 0:HD],
                                          rden[:, :].unsqueeze(2).to_broadcast([SLOTS, HG, HD]),
                                          ALU.mult).then_inc(cx_ready, 1)

            @block.scalar
            def _(act):
                with act.Fori(0, NG // 2) as hp:
                    for e in range(2):
                        hg = hp * 2 + e
                        for s in range(PAIRS):
                            act.wait_ge(rows_done, hg * PAIRS + s + 1)
                            act.activation(gst[PADROW:KALL, e, 2 * s:2 * s + 2, :],
                                           psM[PADROW:KALL, 0:P].rearrange("p (h n) -> p h n", n=SLOTS),
                                           ACT.Copy).then_inc(rows_copied, 1)
                            for h in range(2 * s, 2 * s + 2):
                                act.wait_ge(x_done, hg * HG + h + 1)
                                act.wait_ge(pv_done, hg * HG + max(h - 1, 0))
                                act.activation(probs[:, h % 2, :, :], psX[:, :, :], ACT.Exp,
                                               scale=HD ** -0.5).then_inc(exp_done, 1)
                        act.wait_ge(pv_done, hg * HG + HG)
                        act.wait_ge(back, hg)
                        act.activation(oT[:, 0:SLOTS], psO[:, 0:SLOTS], ACT.Copy).then_inc(oT_copied, 1)

            @block.tensor
            def _(pe):
                pe.wait_ge(preset, 1)
                with pe.Fori(0, NG // 2) as hp:
                    for e in range(2):
                        hg = hp * 2 + e
                        if e:
                            pe.wait_ge(stacked[1], (hp + 1) * (16 * 6))
                        else:
                            pe.wait_ge(stacked[0], hp * (16 * 6))
                        pe.wait_ge(v_in[e], (hp + 1) * 16)
                        pe.wait_ge(g_in[e], (hp + 1) * (16 * 6))

                        def scores(s):
                            pe.wait_ge(maxed, hg * PAIRS + s)
                            for h in range(2):
                                for k in range(T // 512):
                                    mm = pe.matmul(psS[h * SLOTS:(h + 1) * SLOTS, k * 512:(k + 1) * 512],
                                                   gst[0:KMAX, e, 2 * s + h, :],
                                                   kst[0:KMAX, e, 2 * s + h, HALF + k * 512:HALF + (k + 1) * 512],
                                                   start=True, stop=True)
                            mm.then_inc(scored, 1)

                        def rows(s):
                            pe.wait_ge(split, hg * PAIRS + s + 1)
                            pe.wait_ge(rows_copied, hg * PAIRS + s)
                            pe.matmul(psM[PADROW:KALL, 0:P], mparts[:, s, :], g.identb[:, :],
                                      start=True, stop=True).then_inc(rows_done, 1)

                        def transposed(h):
                            pe.wait_ge(rows_copied, hg * PAIRS + h // 2 + 1)
                            pe.wait_ge(exp_done, hg * HG + h)
                            for k in range(NT):
                                mm = pe.matmul(psX[:, k, :], kst[0:KALL, e, h, HALF + k * P:HALF + (k + 1) * P],
                                               gst[0:KALL, e, h, :], start=True, stop=True)
                            mm.then_inc(x_done, 1)

                        def values(h):
                            pe.wait_ge(exp_done, hg * HG + h + 1)
                            pe.wait_ge(oT_copied, hg)
                            for k in range(NT):
                                mm = pe.matmul(psO[h * VW:(h + 1) * VW, 0:SLOTS], vt[:, e, k, h * VW:(h + 1) * VW],
                                               probs[:, h % 2, k, :], start=(k == 0), stop=(k == NT - 1))
                            mm.then_inc(pv_done, 1)

                        scores(0)
                        scores(1)
                        rows(0)
                        transposed(0)
                        transposed(1)
                        values(0)
                        rows(1)
                        transposed(2)
                        values(1)
                        transposed(3)
                        values(2)
                        values(3)
                        pe.wait_ge(oT_copied, hg + 1)
                        pe.wait_ge(cx_ready, hg)
                        pe.transpose(psM[:, 0:P], oT[:, :], g.ident[:, :]).then_inc(back, 1)

NE = 8
FI = 512
FT = FI // P
NS = NT + NE - 1


def mixture(nc, g, router_w, gate_up, down, shared_gate, shared_up, shared_down):
    with ExitStack() as ctx:
        sem = lambda n: nc.alloc_semaphore(f"moe_{n}")
        sb = lambda n, s, d=F32: ctx.enter_context(nc.sbuf_tensor(f"moe_{n}", s, d))
        wgu = sb("wgu", [P, NE, CT, 2 * FI])
        wd = sb("wd", [P, NE, FT, H])
        sg = sb("sg", [P, CT, FI])
        su = sb("su", [P, CT, FI])
        sd = sb("sd", [P, FT, H])
        xnT = sb("xnT", [P, CT, T])
        xr = sb("xr", [P, NT, H])
        logits = sb("logits", [P, NT, NE])
        experts_in, shared_in, zeros_out = [sem(n) for n in ("experts_in", "shared_in", "zeros_out")]
        router(nc, g, router_w, gate_up, down, shared_gate, shared_up, shared_down, wgu, wd, sg, su, sd, xnT,
               xr, logits, experts_in, shared_in, zeros_out)
        experts(nc, g, wgu, wd, sg, su, sd, xnT, xr, logits, experts_in, shared_in, zeros_out)


def router(nc, g, router_w, gate_up, down, shared_gate, shared_up, shared_down, wgu, wd, sg, su, sd, xnT, xr,
           logits, experts_in, shared_in, zeros_out):
    with ExitStack() as ctx:
        sem = lambda n: nc.alloc_semaphore(f"rt_{n}")
        sb = lambda n, s, d=F32: ctx.enter_context(nc.sbuf_tensor(f"rt_{n}", s, d))
        pb = lambda n, s, d=F32: ctx.enter_context(nc.psum_tensor(f"rt_{n}", s, d))
        rw = sb("rw", [P, CT, NE])
        rows = sb("rows", [NE, H])
        xT = sb("xT", [P, 2, CT, P])
        xn = sb("xn", [P, 2, H])
        zero = sb("zero", [P, H])
        best = sb("best", [P, NT])
        e1 = sb("e1", [P, NT])
        d1 = sb("d1", [P, NT])
        score = sb("score", [P, NT])
        psT = [pb(f"psT{u}", [P, 512]) for u in range(2)]
        psL = [pb(f"psL{u}", [P, 512]) for u in range(2)]
        (rw_in, zeroed, rw_turned, rw_ready, normed, turned, xT_ready, all_T, logit_done, logit_ready, best_ready,
         e_ready, chain) = [sem(n) for n in (
             "rw_in", "zeroed", "rw_turned", "rw_ready", "normed", "turned", "xT_ready", "all_T", "logit_done",
             "logit_ready", "best_ready", "e_ready", "chain")]
        with nc.Block() as block:

            @block.sync
            def _(sp):
                sp.dma_start(rows[:, :], router_w).then_inc(rw_in, 16)
                sp.dma_start(sg[:, :, :], shared_gate.rearrange("(c p) n -> p c n", p=P)).then_inc(shared_in, 16)
                sp.dma_start(su[:, :, :], shared_up.rearrange("(c p) n -> p c n", p=P)).then_inc(shared_in, 16)
                sp.dma_start(sd[:, :, :], shared_down.rearrange("(c p) n -> p c n", p=P)).then_inc(shared_in, 16)
                sp.wait_ge(zeroed, 1)
                with sp.Fori(0, NS) as s:
                    sp.dma_start(g.xr_dram[bass.ds(s * P, P), :], zero[:, :]).then_inc(zeros_out, 16)
                for e in range(NE):
                    sp.dma_start(wgu[:, e, :, :], gate_up[e, :, :].rearrange("(c p) n -> p c n", p=P)
                                 ).then_inc(experts_in, 16)
                    sp.dma_start(wd[:, e, :, :], down[e, :, :].rearrange("(c p) n -> p c n", p=P)
                                 ).then_inc(experts_in, 16)
                sp.wait_ge(zeros_out, 16 * NS)

            @block.gpsimd
            def _(pool):
                pool.memset(zero[:, :], 0.0).then_inc(zeroed, 1)

            @block.vector
            def _(dve):
                dve.wait_ge(rw_turned, 1)
                dve.tensor_copy(rw[:, :, :], psL[0][:, 0:CT * NE].rearrange("p (c e) -> p c e", e=NE)
                                ).then_inc(rw_ready, 1)
                def step(i, live, u):
                    if 0 in live:
                        dve.wait_ge(turned, tiles(i - 1))
                        dve.tensor_scalar(xn[:, u, :], g.x[:, i, :], g.mean[:, bass.ds(i, 1)],
                                          g.rstd[:, bass.ds(i, 1)], ALU.subtract, ALU.mult).then_inc(normed, 1)
                    if 2 in live:
                        dve.wait_ge(logit_done, i - 1)
                        dve.tensor_copy(logits[:, i - 2, :], psL[u][:, 0:NE]).then_inc(logit_ready, 1)
                pipelined(dve, step)
                dve.wait_ge(logit_ready, NT)
                dve.tensor_reduce(out=best[:, :], in_=logits[:, :, :], axis=AX.X, op=ALU.max).then_inc(best_ready, 1)
                dve.wait_ge(e_ready, 1)
                dve.tensor_scalar(d1[:, :], e1[:, :], 1.0, None, ALU.add).then_inc(chain, 1)
                dve.wait_ge(chain, 1)
                dve.reciprocal(score[:, :], d1[:, :]).then_inc(chain, 1)
                dve.wait_ge(chain, 2)
                dve.tensor_tensor(score[:, :], score[:, :], g.rstd[:, :], ALU.mult).then_inc(chain, 1)
                dve.wait_ge(chain, 3)
                with dve.Fori(0, NT // 4) as b:
                    for u in range(4):
                        t = b * 4 + u
                        dve.tensor_scalar(xr[:, t, :], g.x[:, t, :], g.mean[:, bass.ds(t, 1)],
                                          score[:, bass.ds(t, 1)], ALU.subtract, ALU.mult).then_inc(chain, 1)

            @block.scalar
            def _(act):
                def step(i, live, u):
                    if 0 in live:
                        act.wait_ge(turned, i + 1)
                        act.wait_ge(logit_done, tiles(i - 1))
                        act.activation(xT[:, u, :, :].rearrange("p c n -> p (c n)"), psT[u][:, 0:H],
                                       ACT.Copy).then_inc(xT_ready, 1)
                        act.activation(xnT[:, :, bass.ds(i * P, P)],
                                       psT[u][:, 0:H].rearrange("p (c n) -> p c n", n=P), ACT.Copy).then_inc(all_T, 1)
                pipelined(act, step)
                act.wait_ge(best_ready, 1)
                act.activation(e1[:, :], best[:, :], ACT.Exp, scale=-1.0).then_inc(e_ready, 1)

            @block.tensor
            def _(pe):
                pe.wait_ge(rw_in, 16)
                for c in range(CT):
                    mm = pe.transpose(psL[0][:, c * NE:(c + 1) * NE], rows[:, c * P:(c + 1) * P],
                                      g.ident[0:NE, 0:NE])
                mm.then_inc(rw_turned, 1)
                pe.wait_ge(rw_ready, 1)
                def step(i, live, u):
                    if 0 in live:
                        pe.wait_ge(normed, i + 1)
                        pe.wait_ge(all_T, tiles(i - 1))
                        for c in range(CT):
                            mm = pe.transpose(psT[u][:, c * P:(c + 1) * P], xn[:, u, c * P:(c + 1) * P],
                                              g.ident[:, :])
                        mm.then_inc(turned, 1)
                    if 1 in live:
                        t, v = i - 1, 1 - u
                        pe.wait_ge(xT_ready, t + 1)
                        pe.wait_ge(logit_ready, tiles(t - 1))
                        for c in range(CT):
                            mm = pe.matmul(psL[v][:, 0:NE], xT[:, v, c, :], rw[:, c, :],
                                           start=(c == 0), stop=(c == CT - 1))
                        mm.then_inc(logit_done, 1)
                pipelined(pe, step)


def experts(nc, g, wgu, wd, sg, su, sd, xnT, xr, logits, experts_in, shared_in, zeros_out):
    with ExitStack() as ctx:
        sem = lambda n: nc.alloc_semaphore(f"ex_{n}")
        sb = lambda n, s, d=F32: ctx.enter_context(nc.sbuf_tensor(f"ex_{n}", s, d))
        pb = lambda n, s, d=F32: ctx.enter_context(nc.psum_tensor(f"ex_{n}", s, d))
        sel = sb("sel", [P, NT, NE])
        pref = sb("pref", [P, NT, NE])
        code = sb("code", [P, NE])
        mx = sb("mx", [P, NT])
        upper = sb("upper", [P, P])
        ones = sb("ones", [P, P])
        cnt = sb("cnt", [P, NE])
        total = sb("total", [P, NE])
        steps = sb("steps", [P, NE, NT])
        tiles = sb("tiles", [P, NE])
        ends = sb("ends", [P, NE])
        starts = sb("starts", [P, NE])
        tileno = sb("tileno", [1, NS, NE])
        past = sb("past", [1, NS, NE])
        ownerf = sb("ownerf", [1, NS])
        owner = sb("owner", [1, NS], I32)
        slotf = sb("slotf", [P, NT])
        GW = 512
        NGR = T // GW
        silus = sb("silus", [P, 2, GW])
        hT = sb("hT", [P, FT, GW])
        xs = sb("xs", [P, 2, H])
        xsT = sb("xsT", [P, 2, CT, P])
        silur = silus
        hid = sb("hid", [P, 2, FI])
        hidT = sb("hidT", [P, 2, FT, P])
        ys = sb("ys", [P, 2, H])
        banks = [pb(f"bank{i}", [P, 512]) for i in range(8)]
        psRank, psCnt = banks[7], banks[6]
        (const, me, sel_ready, cnt_ready, ranked, counted, owner_ready, slot_ready, scattered, gu_done, silu_ready,
         h_ready, y_done, y_copied, xs_turned, xsT_ready, rgu_done, rsilu, hid_ready, hid_turned, hidT_ready,
         yr_done, ys_ready) = [sem(n) for n in (
             "const", "me", "sel_ready", "cnt_ready", "ranked", "counted", "owner_ready", "slot_ready", "scattered",
             "gu_done", "silu_ready", "h_ready", "y_done", "y_copied", "xs_turned", "xsT_ready", "rgu_done",
             "rsilu", "hid_ready", "hid_turned", "hidT_ready", "yr_done", "ys_ready")]
        xs_in = [sem(f"xs_in{u}") for u in range(2)]
        ys_out = [sem(f"ys_out{u}") for u in range(2)]

        def sorted_tiles(eng, step, lag):
            PRE_S = 4
            END = NS - 1 - (NS - 1) % 2
            for s in range(PRE_S):
                step(s, s % 2, [k for k in range(lag + 1) if k <= s])
            with eng.Fori(PRE_S // 2, END // 2) as b:
                for u in range(2):
                    step(b * 2 + u, u, list(range(lag + 1)))
            for s in range(END, NS + lag):
                step(s, s % 2, [k for k in range(lag + 1) if 0 <= s - k < NS])

        with nc.Block() as block:

            @block.gpsimd
            def _(pool):
                n = 0
                for op in (
                    lambda: pool.memset(upper[:, :], 1.0),
                    lambda: pool.affine_select(out=upper[:, :], in_=upper[:, :], compare_op=ALU.is_gt, fill=0.0,
                                               base=0, pattern=[[1, P]], channel_multiplier=-1),
                    lambda: pool.memset(ones[:, :], 1.0),
                    lambda: pool.iota(code[:, :], pattern=[[-1, NE]], base=NE, channel_multiplier=0,
                                      allow_small_or_imprecise_dtypes=True),
                    lambda: pool.iota(steps[:, :, :], pattern=[[0, NE], [P, NT]], base=0, channel_multiplier=0,
                                      allow_small_or_imprecise_dtypes=True),
                    lambda: pool.iota(tileno[:, :, :], pattern=[[1, NS], [0, NE]], base=0, channel_multiplier=0,
                                      allow_small_or_imprecise_dtypes=True),
                ):
                    op().then_inc(const, 1)
                    n += 1
                    pool.wait_ge(const, n)
                pool.wait_ge(slot_ready, 1)
                pool.wait_ge(zeros_out, 16 * NS)
                for t in range(NT):
                    pool.indirect_dma_start(out=g.xr_dram,
                                            out_offset=bass.IndirectOffsetOnAxis(ap=g.slot[:, t:t + 1], axis=0),
                                            in_=xr[:, t, :], in_offset=None).then_inc(scattered, 16)
                pool.wait_ge(scattered, 16 * NT)

            @block.sync
            def _(sp):
                sp.wait_ge(scattered, 16 * NT)

                def step(s, u, live):
                    if 0 in live:
                        if not isinstance(s, int) or s >= 2:
                            sp.wait_ge(xs_turned, s - 1)
                        sp.dma_start(xs[:, u, :], g.xr_dram[bass.ds(s * P, P), :]).then_inc(xs_in[u], 16)
                    if 4 in live:
                        sp.wait_ge(ys_ready, s - 3)
                        sp.dma_start(g.yr_dram[bass.ds((s - 4) * P, P), :], ys[:, u, :]).then_inc(ys_out[u], 16)
                sorted_tiles(sp, step, 4)
                sp.wait_ge(ys_out[0], 16 * ((NS + 1) // 2))
                sp.wait_ge(ys_out[1], 16 * (NS // 2))

            @block.vector
            def _(dve):
                own = Tally(me)
                bc = [P, NT, NE]
                dve.wait_ge(const, 6)
                own.mark(dve.tensor_reduce(out=mx[:, :], in_=logits[:, :, :], axis=AX.X, op=ALU.max))
                own.done(dve)
                own.mark(dve.tensor_tensor(sel[:, :, :], logits[:, :, :], mx[:, :].unsqueeze(2).to_broadcast(bc),
                                           ALU.is_equal))
                own.done(dve)
                own.mark(dve.tensor_tensor(pref[:, :, :], sel[:, :, :], code[:, :].unsqueeze(1).to_broadcast(bc),
                                           ALU.mult))
                own.done(dve)
                own.mark(dve.tensor_reduce(out=mx[:, :], in_=pref[:, :, :], axis=AX.X, op=ALU.max))
                own.done(dve)
                dve.tensor_tensor(sel[:, :, :], pref[:, :, :], mx[:, :].unsqueeze(2).to_broadcast(bc),
                                  ALU.is_equal).then_inc(sel_ready, 1)
                dve.wait_ge(sel_ready, 1)
                dve.tensor_reduce(out=cnt[:, :], in_=sel[:, :, :].rearrange("p t e -> p e t"), axis=AX.X,
                                  op=ALU.add).then_inc(cnt_ready, 1)
                dve.wait_ge(counted, 1)
                own.mark(dve.tensor_copy(total[:, :], psCnt[:, 0:NE]))
                own.done(dve)
                own.mark(dve.tensor_tensor(steps[:, :, :], total[:, :].unsqueeze(2).to_broadcast([P, NE, NT]),
                                           steps[:, :, :], ALU.is_gt))
                own.done(dve)
                own.mark(dve.tensor_reduce(out=tiles[:, :], in_=steps[:, :, :], axis=AX.X, op=ALU.add))
                own.done(dve)
                own.mark(dve.tensor_tensor_scan(out=ends[:, :], data0=ones[:, 0:NE], data1=tiles[:, :], initial=0.0,
                                                op0=ALU.mult, op1=ALU.add))
                own.done(dve)
                own.mark(dve.tensor_tensor(starts[:, :], ends[:, :], tiles[:, :], ALU.subtract))
                own.done(dve)
                own.mark(dve.tensor_scalar(starts[:, :], starts[:, :], float(P), None, ALU.mult))
                own.done(dve)
                own.mark(dve.tensor_tensor(past[:, :, :], ends[0:1, :].unsqueeze(1).to_broadcast([1, NS, NE]),
                                           tileno[:, :, :], ALU.is_le))
                own.done(dve)
                own.mark(dve.tensor_reduce(out=ownerf[:, :], in_=past[:, :, :], axis=AX.X, op=ALU.add))
                own.done(dve)
                dve.tensor_scalar(owner[:, :], ownerf[:, :], float(NE - 1), None, ALU.min).then_inc(owner_ready, 1)
                dve.wait_ge(ranked, 1)
                own.mark(dve.tensor_tensor(pref[:, :, :], psRank[:, 0:NT * NE].rearrange("p (t e) -> p t e", e=NE),
                                           starts[:, :].unsqueeze(1).to_broadcast(bc), ALU.add))
                own.done(dve)
                own.mark(dve.tensor_tensor(pref[:, :, :], pref[:, :, :], sel[:, :, :], ALU.mult))
                own.done(dve)
                own.mark(dve.tensor_reduce(out=slotf[:, :], in_=pref[:, :, :], axis=AX.X, op=ALU.add))
                own.done(dve)
                dve.tensor_copy(g.slot[:, :], slotf[:, :]).then_inc(slot_ready, 1)
                with dve.Fori(0, NGR) as q:
                    for f in range(FT):
                        dve.wait_ge(silu_ready, q * FT + f + 1)
                        dve.wait_ge(y_done, q * 4)
                        dve.tensor_tensor(hT[:, f, :], silus[:, f % 2, :], banks[2 * (f % 2) + 1][:, :],
                                          ALU.mult).then_inc(h_ready, 1)
                    for k in range(4):
                        dve.wait_ge(y_done, q * 4 + k + 1)
                        dve.tensor_copy(g.y[:, q * 4 + k, :], banks[4 + k % 2][:, 0:H]).then_inc(y_copied, 1)

                def step(s, u, live):
                    if 1 in live:
                        v = 1 - u
                        dve.wait_ge(rsilu, s)
                        if not isinstance(s, int) or s >= 3:
                            dve.wait_ge(hid_turned, s - 2)
                        dve.tensor_tensor(hid[:, v, :], silur[:, v, :], banks[2 * v + 1][:, :],
                                          ALU.mult).then_inc(hid_ready, 1)
                    if 3 in live:
                        v = 1 - u
                        dve.wait_ge(yr_done, s - 2)
                        if not isinstance(s, int) or s >= 5:
                            dve.wait_ge(ys_out[v], (s - 3 - v) * 8)
                        dve.tensor_copy(ys[:, v, :], banks[6][:, 0:H]).then_inc(ys_ready, 1)
                sorted_tiles(dve, step, 3)

            @block.scalar
            def _(act):
                with act.Fori(0, NGR) as q:
                    for f in range(FT):
                        act.wait_ge(gu_done, q * FT + f + 1)
                        if f >= 2:
                            act.wait_ge(h_ready, q * FT + f - 1)
                        else:
                            act.wait_ge(h_ready, q * FT)
                        act.activation(silus[:, f % 2, :], banks[2 * (f % 2)][:, :], ACT.Silu).then_inc(silu_ready, 1)

                def step(s, u, live):
                    if 0 in live:
                        act.wait_ge(xs_turned, s + 1)
                        if not isinstance(s, int) or s >= 2:
                            act.wait_ge(rgu_done, s - 1)
                        act.activation(xsT[:, u, :, :].rearrange("p c n -> p (c n)"), banks[4][:, 0:H],
                                       ACT.Copy).then_inc(xsT_ready, 1)
                    if 2 in live:
                        act.wait_ge(hid_turned, s - 1)
                        if not isinstance(s, int) or s >= 4:
                            act.wait_ge(yr_done, s - 3)
                        act.activation(hidT[:, u, :, :].rearrange("p k n -> p (k n)"), banks[5][:, :],
                                       ACT.Copy).then_inc(hidT_ready, 1)
                    if 1 in live:
                        v = 1 - u
                        act.wait_ge(rgu_done, s)
                        if not isinstance(s, int) or s >= 3:
                            act.wait_ge(hid_ready, s - 2)
                        else:
                            act.wait_ge(h_ready, NGR * FT)
                        act.activation(silur[:, v, :], banks[2 * v][:, :], ACT.Silu).then_inc(rsilu, 1)
                sorted_tiles(act, step, 2)

            @block.tensor
            def _(pe):
                pe.wait_ge(const, 6)
                pe.wait_ge(sel_ready, 1)
                pe.matmul(psRank[:, 0:NT * NE], upper[:, :], sel[:, :, :].rearrange("p t e -> p (t e)"),
                          start=True, stop=False, skip_group_check=True)
                for t in range(NT - 1):
                    rest = NT - 1 - t
                    mm = pe.matmul(psRank[:, (t + 1) * NE:NT * NE], ones[:, :],
                                   sel[:, t, :].unsqueeze(1).to_broadcast([P, rest, NE]),
                                   start=False, stop=(t == NT - 2), skip_group_check=True)
                mm.then_inc(ranked, 1)
                pe.wait_ge(cnt_ready, 1)
                pe.matmul(psCnt[:, 0:NE], ones[:, :], cnt[:, :], start=True, stop=True).then_inc(counted, 1)
                pe.wait_ge(shared_in, 48)
                with pe.Fori(0, NGR) as q:
                    for f in range(FT):
                        pe.wait_ge(h_ready, q * FT + f - 1 if f >= 2 else q * FT)
                        for w, bank in ((sg, banks[2 * (f % 2)]), (su, banks[2 * (f % 2) + 1])):
                            for c in range(CT):
                                mm = pe.matmul(bank[:, :], w[:, c, f * P:(f + 1) * P],
                                               xnT[:, c, bass.ds(q * GW, GW)], start=(c == 0), stop=(c == CT - 1))
                        mm.then_inc(gu_done, 1)
                    pe.wait_ge(h_ready, q * FT + FT)
                    for k in range(4):
                        pe.wait_ge(y_copied, q * 4 + k - 1 if k >= 2 else q * 4)
                        for f in range(FT):
                            mm = pe.matmul(banks[4 + k % 2][:, 0:H], hT[:, f, k * P:(k + 1) * P], sd[:, f, :],
                                           start=(f == 0), stop=(f == FT - 1))
                        mm.then_inc(y_done, 1)
                pe.wait_ge(experts_in, 16 * 2 * NE)
                pe.wait_ge(owner_ready, 1)
                pe.wait_ge(slot_ready, 1)
                pe.wait_ge(y_copied, NT)

                def step(s, u, live):
                    if 0 in live:
                        pe.wait_ge(xs_in[u], (s - u) * 8 + 16)
                        if not isinstance(s, int) or s >= 1:
                            pe.wait_ge(xsT_ready, s)
                        for c in range(CT):
                            mm = pe.transpose(banks[4][:, c * P:(c + 1) * P], xs[:, u, c * P:(c + 1) * P],
                                              g.ident[:, :])
                        mm.then_inc(xs_turned, 1)
                    if 1 in live:
                        v = 1 - u
                        e = pe.value_load(owner[0:1, bass.ds(s - 1, 1)], min_val=0, max_val=NE - 1)
                        pe.wait_ge(xsT_ready, s)
                        if not isinstance(s, int) or s >= 3:
                            pe.wait_ge(hid_ready, s - 2)
                        for half in range(2):
                            for c in range(CT):
                                mm = pe.matmul(banks[2 * v + half][:, :], xsT[:, v, c, :],
                                               wgu[:, bass.ds(e, 1), c, half * FI:(half + 1) * FI]
                                               .rearrange("p e n -> p (e n)"), start=(c == 0), stop=(c == CT - 1))
                        mm.then_inc(rgu_done, 1)
                    if 2 in live:
                        pe.wait_ge(hid_ready, s - 1)
                        if not isinstance(s, int) or s >= 3:
                            pe.wait_ge(hidT_ready, s - 2)
                        for k in range(FT):
                            mm = pe.transpose(banks[5][:, k * P:(k + 1) * P], hid[:, u, k * P:(k + 1) * P],
                                              g.ident[:, :])
                        mm.then_inc(hid_turned, 1)
                    if 3 in live:
                        v = 1 - u
                        e = pe.value_load(owner[0:1, bass.ds(s - 3, 1)], min_val=0, max_val=NE - 1)
                        pe.wait_ge(hidT_ready, s - 2)
                        if not isinstance(s, int) or s >= 4:
                            pe.wait_ge(ys_ready, s - 3)
                        for k in range(FT):
                            mm = pe.matmul(banks[6][:, 0:H], hidT[:, v, k, :],
                                           wd[:, bass.ds(e, 1), k, :].rearrange("p e n -> p (e n)"),
                                           start=(k == 0), stop=(k == FT - 1))
                        mm.then_inc(yr_done, 1)
                sorted_tiles(pe, step, 3)

DI = 512
VH, VP = 64, 8
SG, SN = 8, 64
GV = VH // SG
KC = 4
XT = DI // P
CONV_T = 3 * XT
NC = NT
HT = T // 2
ATANH = 7


def flat(ap):
    return ap.rearrange("p t c -> p (t c)")


def project_state(nc, g, xc, z, alog, in_w, conv_w, conv_b, z_bias):
    ET = CONV_T + XT
    with ExitStack() as ctx:
        sem = lambda n: nc.alloc_semaphore(f"ps_{n}")
        sb = lambda n, s, d=F32: ctx.enter_context(nc.sbuf_tensor(f"ps_{n}", s, d))
        pb = lambda n, s, d=F32: ctx.enter_context(nc.psum_tensor(f"ps_{n}", s, d))
        xnT = flat(g.y[:, :, :]).rearrange("p (c n) -> p c n", c=CT)
        xn = sb("xn", [P, 2, H])
        wrow = sb("wrow", [P, 2, H])
        wT = sb("wT", [P, 2, CT, P])
        raw = sb("raw", [P, 2, KC - 1 + T])
        cw = sb("cw", [P, CONV_T, KC])
        cb = sb("cb", [P, CONV_T])
        zb = sb("zb", [P, XT])
        banks = [pb(f"bank{i}", [P, 512]) for i in range(8)]
        (const_in, x_out, preset, normed, turned, xT_ready, w_turned, w_ready, proj_done, raw_ready, tap0, conv,
         silu, evac) = [sem(n) for n in (
             "const_in", "x_out", "preset", "normed", "turned", "xT_ready", "w_turned", "w_ready", "proj_done",
             "raw_ready", "tap0", "conv", "silu", "evac")]
        w_in = [sem(f"w_in{u}") for u in range(2)]
        NQ = T // 512
        with nc.Block() as block:

            @block.sync
            def _(sp):
                sp.dma_start(cw[:, :, :], conv_w.rearrange("(m p) a k -> p m (a k)", p=P)).then_inc(const_in, 16)
                sp.dma_start(cb[:, :], conv_b.rearrange("(m p) -> p m", p=P),
                             allow_slow_non_contiguous=True).then_inc(const_in, 16)
                sp.dma_start(zb[:, :], z_bias.rearrange("(m p) -> p m", p=P),
                             allow_slow_non_contiguous=True).then_inc(const_in, 16)
                sp.dma_start(g.x_dram.rearrange("(t p) c -> p t c", p=P), g.x[:, :, :]).then_inc(x_out, 16)
                with sp.Fori(0, ET // 2) as b:
                    for u in range(2):
                        sp.wait_ge(w_turned, 2 * b)
                        sp.dma_start(wrow[:, u, :], in_w[bass.ds((2 * b + u) * P, P), :]).then_inc(w_in[u], 16)
                sp.wait_ge(w_turned, ET - 1)
                sp.dma_start(wrow[0:VH, 0, :], in_w[ET * P:ET * P + VH, :]).then_inc(w_in[0], 16)
                sp.wait_ge(x_out, 16)

            @block.gpsimd
            def _(pool):
                for u in range(2):
                    pool.memset(raw[:, u, 0:KC - 1], 0.0).then_inc(preset, 1)
                    pool.wait_ge(preset, u + 1)

            @block.vector
            def _(dve):
                with dve.Fori(0, NT // 2) as b:
                    for u in range(2):
                        t = 2 * b + u
                        dve.wait_ge(turned, 2 * b)
                        dve.tensor_scalar(xn[:, u, :], g.x[:, t, :], g.mean[:, bass.ds(t, 1)],
                                          g.rstd[:, bass.ds(t, 1)], ALU.subtract, ALU.mult).then_inc(normed, 1)
                with dve.Fori(0, CONV_T // 2) as b:
                    for u in range(2):
                        m = 2 * b + u
                        dve.wait_ge(raw_ready, (m + 1) * NQ)
                        dve.wait_ge(tap0, m + 1)
                        for k in range(1, KC):
                            dve.scalar_tensor_tensor(out=xc[:, m, :], in0=raw[:, u, k:k + T],
                                                     scalar=cw[:, m, k:k + 1], in1=xc[:, m, :],
                                                     op0=ALU.mult, op1=ALU.add).then_inc(conv, 1)
                            if k < KC - 1:
                                dve.wait_ge(conv, m * (KC - 1) + k)

            @block.scalar
            def _(act):
                with act.Fori(0, NT // 2) as b:
                    for u in range(2):
                        t = 2 * b + u
                        act.wait_ge(turned, t + 1)
                        act.activation(xnT[:, :, bass.ds(t * P, P)],
                                       banks[6 + u][:, 0:H].rearrange("p (c n) -> p c n", n=P),
                                       ACT.Copy).then_inc(xT_ready, 1)
                act.wait_ge(const_in, 48)
                act.wait_ge(preset, 2)

                def weights(m, u):
                    act.wait_ge(w_turned, m + 1)
                    act.wait_ge(proj_done, (m - 1) * NQ if not isinstance(m, int) or m >= 1 else 0)
                    act.activation(wT[:, u, :, :].rearrange("p c n -> p (c n)"), banks[4 + u][:, 0:H],
                                   ACT.Copy).then_inc(w_ready, 1)
                weights(0, 0)

                def silu_of(m):
                    act.wait_ge(conv, (m + 1) * (KC - 1))
                    act.activation(xc[:, m, :], xc[:, m, :], ACT.Silu, bias=cb[:, bass.ds(m, 1)]).then_inc(silu, 1)

                def tile(m, u):
                    if not isinstance(m, int) or m >= 2:
                        act.wait_ge(conv, (m - 1) * (KC - 1))
                        act.wait_ge(tap0, m - 1)
                    for q in range(NQ):
                        act.wait_ge(proj_done, m * NQ + q + 1)
                        act.activation(raw[:, u, KC - 1 + q * 512:KC - 1 + (q + 1) * 512], banks[q][:, :],
                                       ACT.Copy).then_inc(raw_ready, 1)
                        if q == 0:
                            weights(m + 1, 1 - u)
                    act.wait_ge(raw_ready, (m + 1) * NQ)
                    act.activation(xc[:, m, :], raw[:, u, 0:T], ACT.Copy, scale=cw[:, m, 0:1]).then_inc(tap0, 1)
                tile(0, 0)
                tile(1, 1)
                with act.Fori(1, CONV_T // 2) as b:
                    tile(b * 2, 0)
                    tile(b * 2 + 1, 1)
                for m in range(CONV_T, ET):
                    for q in range(NQ):
                        act.wait_ge(proj_done, m * NQ + q + 1)
                        act.activation(z[:, m - CONV_T, q * 512:(q + 1) * 512], banks[q][:, :], ACT.Silu,
                                       bias=zb[:, m - CONV_T:m - CONV_T + 1]).then_inc(evac, 1)
                        if q == 0 and m + 1 < ET:
                            weights(m + 1, (m + 1) % 2)
                        if (m - CONV_T) * NQ + q < CONV_T:
                            silu_of((m - CONV_T) * NQ + q)
                act.wait_ge(w_turned, ET + 1)
                act.wait_ge(proj_done, ET * NQ)
                act.activation(wT[:, 0, :, 0:VH],
                               banks[4][:, 0:CT * VH].rearrange("p (c n) -> p c n", n=VH),
                               ACT.Copy).then_inc(w_ready, 1)
                act.wait_ge(proj_done, ET * NQ + 1)
                for q in range(2):
                    act.activation(alog[:, q * 512:(q + 1) * 512], banks[q][:, :], ACT.Copy).then_inc(evac, 1)

            @block.tensor
            def _(pe):
                with pe.Fori(0, NT // 2) as b:
                    for u in range(2):
                        t = 2 * b + u
                        pe.wait_ge(normed, t + 1)
                        pe.wait_ge(xT_ready, 2 * b)
                        for c in range(CT):
                            mm = pe.transpose(banks[6 + u][:, c * P:(c + 1) * P], xn[:, u, c * P:(c + 1) * P],
                                              g.ident[:, :])
                        mm.then_inc(turned, 1)
                pe.wait_ge(xT_ready, NT)

                def turn_weights(m, u, count):
                    pe.wait_ge(w_in[u], count)
                    for c in range(CT):
                        mm = pe.transpose(banks[4 + u][:, c * P:(c + 1) * P], wrow[:, u, c * P:(c + 1) * P],
                                          g.ident[:, :])
                    mm.then_inc(w_turned, 1)

                def products(m, u, freed):
                    pe.wait_ge(w_ready, m + 1)
                    for q in range(NQ):
                        freed(q)
                        for c in range(CT):
                            mm = pe.matmul(banks[q][:, :], wT[:, u, c, :], xnT[:, c, q * 512:(q + 1) * 512],
                                           start=(c == 0), stop=(c == CT - 1))
                        mm.then_inc(proj_done, 1)
                turn_weights(0, 0, 16)

                def tile(m, u, arrived):
                    turn_weights(m + 1, 1 - u, arrived)
                    products(m, u, lambda q: None if isinstance(m, int) and m == 0 else
                             pe.wait_ge(raw_ready, (m - 1) * NQ + q + 1))
                tile(0, 0, 16)
                tile(1, 1, 32)
                with pe.Fori(1, CONV_T // 2) as b:
                    tile(b * 2, 0, (b + 1) * 16)
                    tile(b * 2 + 1, 1, (b + 2) * 16)
                for m in range(CONV_T, ET):
                    u = m % 2
                    if m + 1 < ET:
                        turn_weights(m + 1, 1 - u, ((m + 1) // 2 + 1) * 16)
                    products(m, u, lambda q: (pe.wait_ge(raw_ready, CONV_T * NQ),
                                              pe.wait_ge(evac, max((m - CONV_T - 1) * NQ + q + 1, 0))))
                pe.wait_ge(w_in[0], 16 * (ET // 2 + 1))
                for c in range(CT):
                    mm = pe.transpose(banks[4][:, c * VH:(c + 1) * VH], wrow[0:VH, 0, c * P:(c + 1) * P],
                                      g.ident[0:VH, 0:VH])
                mm.then_inc(w_turned, 1)
                pe.wait_ge(w_ready, ET + 1)
                pe.wait_ge(evac, XT * NQ)
                for half in range(2):
                    for q in range(2):
                        for c in range(CT):
                            n0 = half * HT + q * 512
                            mm = pe.matmul(banks[q][half * VH:(half + 1) * VH, :], wT[:, 0, c, 0:VH],
                                           xnT[:, c, n0:n0 + 512], start=(c == 0), stop=(c == CT - 1),
                                           skip_group_check=True)
                mm.then_inc(proj_done, 1)


def decays(nc, g, alog, decT, D):
    with ExitStack() as ctx:
        sem = lambda n: nc.alloc_semaphore(f"dc_{n}")
        sb = lambda n, s, d=F32: ctx.enter_context(nc.sbuf_tensor(f"dc_{n}", s, d))
        pb = lambda n, s, d=F32: ctx.enter_context(nc.psum_tensor(f"dc_{n}", s, d))
        e = sb("e", [P, HT])
        s = sb("s", [P, HT])
        s2 = sb("s2", [P, HT])
        p = sb("p", [P, HT])
        dt = sb("dt", [P, HT])
        keep = sb("keep", [P, NC // 2, P])
        ac = sb("ac", [P, HT])
        dcol = sb("dcol", [P, 1])
        parts = sb("parts", [P, 3, HT], BF16)
        banks = [pb(f"bank{i}", [P, 512]) for i in range(2)]
        (own, d_in, keep_ready, abs_ready, e_ready, ac_ready, ea_ready, dec_arg, dec_ready, parts_ready, ddt_ready,
         turned, decT_ready, stored) = [sem(n) for n in (
             "own", "d_in", "keep_ready", "abs_ready", "e_ready", "ac_ready", "ea_ready", "dec_arg", "dec_ready",
             "parts_ready", "ddt_ready", "turned", "decT_ready", "stored")]
        ea = e
        dt_ready = sem("dt_ready")
        with nc.Block() as block:

            @block.sync
            def _(sp):
                for half in range(2):
                    sp.dma_start(dcol[half * VH:(half + 1) * VH, :], D.rearrange("(h a) -> h a", a=1)
                                 ).then_inc(d_in, 16)
                halves = lambda i: g.rep_dram[i, :, :].rearrange("h (a n) -> a h n", a=2)
                for what, i, ready in ((ea_ready, 0, ea), (ddt_ready, 1, s)):
                    sp.wait_ge(what, 1)
                    for half in range(2):
                        sp.dma_start(halves(i)[half, :, :], ready[half * VH:(half + 1) * VH, :]).then_inc(stored, 16)
                sp.wait_ge(parts_ready, 1)
                for i in range(3):
                    for half in range(2):
                        sp.dma_start(g.ac_dram[i, :, :].rearrange("h (a n) -> a h n", a=2)[half, :, :],
                                     parts[half * VH:(half + 1) * VH, i, :]).then_inc(stored, 16)
                sp.wait_ge(stored, 16 * 10)

            @block.gpsimd
            def _(pool):
                pool.memset(keep[:, :, :], 1.0).then_inc(keep_ready, 1)
                pool.wait_ge(keep_ready, 1)
                pool.memset(keep[:, :, 0:1], 0.0).then_inc(keep_ready, 1)

            @block.vector
            def _(dve):
                me = Tally(own)

                def run(ins):
                    me.mark(ins)
                    me.done(dve)
                dve.wait_ge(e_ready, 1)
                run(dve.tensor_scalar(s2[:, :], e[:, :], 2.0, None, ALU.add))
                run(dve.reciprocal(s2[:, :], s2[:, :]))
                run(dve.tensor_tensor(s[:, :], e[:, :], s2[:, :], ALU.mult))
                run(dve.tensor_tensor(s2[:, :], s[:, :], s[:, :], ALU.mult))
                run(dve.tensor_scalar(p[:, :], s2[:, :], 1.0 / (2 * ATANH + 1), None, ALU.mult))
                for k in range(ATANH - 1, 0, -1):
                    run(dve.scalar_tensor_tensor(out=p[:, :], in0=p[:, :], scalar=1.0 / (2 * k + 1), in1=s2[:, :],
                                                 op0=ALU.add, op1=ALU.mult))
                run(dve.scalar_tensor_tensor(out=p[:, :], in0=p[:, :], scalar=1.0, in1=s[:, :],
                                             op0=ALU.add, op1=ALU.mult))
                run(dve.tensor_scalar(s2[:, :], alog[:, :], 0.0, None, ALU.max))
                dve.scalar_tensor_tensor(out=dt[:, :], in0=p[:, :], scalar=2.0, in1=s2[:, :],
                                         op0=ALU.mult, op1=ALU.add).then_inc(dt_ready, 1)
                dve.wait_ge(dt_ready, 1)
                run(dve.tensor_scalar(s2[:, :], dt[:, :], -1.0, None, ALU.mult))
                dve.wait_ge(keep_ready, 2)
                dve.tensor_tensor_scan(out=ac[:, :], data0=keep[:, :, :].rearrange("p c n -> p (c n)"),
                                       data1=s2[:, :], initial=0.0, op0=ALU.mult, op1=ALU.add).then_inc(ac_ready, 1)
                dve.wait_ge(ac_ready, 1)
                ac3 = ac[:, :].rearrange("p (c n) -> p c n", n=P)
                dve.tensor_tensor(p[:, :].rearrange("p (c n) -> p c n", n=P),
                                  ac3[:, :, P - 1:P].to_broadcast([P, NC // 2, P]), ac3,
                                  ALU.subtract).then_inc(dec_arg, 1)
                run(dve.tensor_copy(parts[:, 0, :], ac[:, :]))
                run(dve.tensor_tensor(s2[:, :], ac[:, :], parts[:, 0, :], ALU.subtract))
                run(dve.tensor_copy(parts[:, 1, :], s2[:, :]))
                dve.tensor_tensor(parts[:, 2, :], s2[:, :], parts[:, 1, :], ALU.subtract).then_inc(parts_ready, 1)
                dve.wait_ge(d_in, 32)
                run(dve.reciprocal(dt[:, :], dt[:, :]))
                dve.tensor_scalar(s[:, :], dt[:, :], dcol[:, 0:1], None, ALU.mult).then_inc(ddt_ready, 1)
                for i in range(2):
                    dve.wait_ge(turned, i + 1)
                    dve.tensor_copy(decT[:, :, :].rearrange("p (a c) h -> p c a h", a=2)[:, 4 * i:4 * i + 4, :, :],
                                    banks[i][:, :].rearrange("p (c a h) -> p c a h", a=2, h=VH)
                                    ).then_inc(decT_ready, 1)

            @block.scalar
            def _(act):
                act.activation(e[:, :], alog[:, :], ACT.Abs).then_inc(abs_ready, 1)
                act.wait_ge(abs_ready, 1)
                act.activation(e[:, :], e[:, :], ACT.Exp, scale=-1.0).then_inc(e_ready, 1)
                act.wait_ge(ac_ready, 1)
                act.activation(ea[:, :], ac[:, :], ACT.Exp).then_inc(ea_ready, 1)
                act.wait_ge(dec_arg, 1)
                act.activation(p[:, :], p[:, :], ACT.Exp).then_inc(dec_ready, 1)

            @block.tensor
            def _(pe):
                pe.wait_ge(dec_ready, 1)
                for i in range(2):
                    for c in range(4):
                        mm = pe.transpose(banks[i][:, c * P:(c + 1) * P],
                                          p[:, (4 * i + c) * P:(4 * i + c + 1) * P], g.ident[:, :])
                    mm.then_inc(turned, 1)


def scan(nc, g, xc, z, decT):
    KD = 3 + 3 * GV
    with ExitStack() as ctx:
        sem = lambda n: nc.alloc_semaphore(f"sc_{n}")
        sb = lambda n, s, d=F32: ctx.enter_context(nc.sbuf_tensor(f"sc_{n}", s, d))
        pb = lambda n, s, d=F32: ctx.enter_context(nc.psum_tensor(f"sc_{n}", s, d))
        QW, WINDOW = 96, (0, 24, 40, 64)
        NQD = VH // 4
        xw, yw = flat(g.x[:, :, :]), flat(g.y[:, :, :])
        EX = yw.rearrange("p (r h n) -> p r h n", r=4, h=GV)
        Xm = xw[:, 0:2 * NQD * QW].rearrange("p (u n) -> p u n", u=2)
        rep = xw[:, 2 * NQD * QW:2 * NQD * QW + 2 * XT * P].rearrange("p (a i n) -> p a i n", a=2, i=XT)
        Xd = sb("Xd", [P, DI])
        tmp = sb("tmp", [P, XT * P])
        tmp2 = sb("tmp2", [P, XT * P])
        xr = sb("xr", [P, 2, XT, P])
        Br = sb("Br", [P, XT, P])
        Bz = sb("Bz", [P, XT, 2, P])
        Bt = sb("Bt", [P, SG * SN])
        CBm = sb("CBm", [P, 2, SG, P])
        mask = sb("mask", [P, P], BF16)
        ST = sb("ST", [P, XT, P])
        Sn = sb("Sn", [P, XT, P])
        dl = sb("dl", [KD, 2, SG, P], BF16)
        dm = sb("dm", [KD, 4, GV, P], BF16)
        dmi = tmp[0:GV, :].bitcast(BF16).rearrange("p (h n) -> p h n", h=GV)
        D0 = [pb(f"D{i}", [P, 2, 512]) for i in range(2)]
        W = [pb(f"W{i}", [P, 512]) for i in range(2)]
        Yo, Yd = pb("Yo", [P, XT, P]), pb("Yd", [P, XT, P])
        (own, preset, t_done, xm_ready, xd_ready, bt_ready, cb_done, cbm_ready, yo_done, st_done, st_ready, sT_done,
         s_ready, diff_done, exp_done, m_ready, yd_done, yo_used, summed, comb, dx_ready, out_ready,
         st_upd) = [sem(n) for n in (
             "own", "preset", "t_done", "xm_ready", "xd_ready", "bt_ready", "cb_done", "cbm_ready", "yo_done",
             "st_done", "st_ready", "sT_done", "s_ready", "diff_done", "exp_done", "m_ready", "yd_done", "yo_used",
             "summed", "comb", "dx_ready", "out_ready", "st_upd")]
        x_in = [sem(f"x_in{u}") for u in range(2)]
        dl_in = [sem(f"dl_in{u}") for u in range(2)]
        dm_in = [sem(f"dm_in{r}") for r in range(4)]
        b_in, bz_in, rep_in, ind_in = [sem(n) for n in ("b_in", "bz_in", "rep_in", "ind_in")]
        zeroed = sem("zeroed")
        turn = sem("turn")

        def chunks(eng, body):
            body(0, 0, False)
            with eng.Fori(0, (NC - 2) // 2) as b:
                body(b * 2 + 1, 1, False)
                body(b * 2 + 2, 0, False)
            body(NC - 1, (NC - 1) % 2, True)

        def passed(n):
            return max(n, 0) if isinstance(n, int) else n

        with nc.Block() as block:

            @block.sync
            def _(sp):
                def load_x(c, u):
                    cols = bass.ds(c * P, P)
                    sp.dma_start(xr[:, u, :, :], xc[:, 0:XT, cols]).then_inc(x_in[u], 16)
                    sp.dma_start(Br[:, :, :], xc[:, XT:2 * XT, cols]).then_inc(b_in, 16)

                def load_bz(c):
                    cols = bass.ds(c * P, P)
                    for k in range(2):
                        sp.dma_start(Bz[k * SN:(k + 1) * SN, :, k, :],
                                     xc[k * SN:(k + 1) * SN, XT:2 * XT, cols]).then_inc(bz_in, 16)

                def load_dl(c, u):
                    for i in range(3):
                        sp.dma_start(dl[3 + i * GV:3 + (i + 1) * GV, u, :, :],
                                     g.ac_dram[i, :, bass.ds(c * P, P)].rearrange("(s h) n -> h s n", h=GV)
                                     ).then_inc(dl_in[u], 16)

                def load_dm(c, s):
                    sp.dma_start(dm[0:3, s % 4, :, :], g.ac_dram[:, s * GV:(s + 1) * GV, bass.ds(c * P, P)]
                                 ).then_inc(dm_in[s % 4], 16)

                def load_rep(c):
                    for a in range(2):
                        for i in range(XT):
                            src = g.rep_dram[a, i * (VH // XT):(i + 1) * (VH // XT), bass.ds(c * P, P)]
                            sp.dma_start(rep[:, a, i, :],
                                         src.unsqueeze(1).to_broadcast([VH // XT, VP, P])).then_inc(rep_in, 16)

                load_x(0, 0)
                sp.wait_ge(zeroed, 1)
                load_dl(0, 0)
                sp.wait_ge(own, 2)
                for i in range(3):
                    sp.dma_start(dm[3 + i * GV:3 + (i + 1) * GV, :, :, :],
                                 dmi.unsqueeze(1).to_broadcast([GV, 4, GV, P])).then_inc(ind_in, 16)
                for s in range(4):
                    load_dm(0, s)
                sp.wait_ge(zeroed, 2)
                load_bz(0)
                load_rep(0)

                def body(c, u, last):
                    for s in range(SG):
                        if last and s >= 4:
                            continue
                        sp.wait_ge(diff_done, c * SG + s + 1)
                        sp.sem_inc(turn, 1)
                        if s < 4:
                            load_dm(c, s + 4)
                        else:
                            load_dm(c + 1, s - 4)
                        if s == 0 and not last:
                            sp.wait_ge(cb_done, c + 1)
                            sp.wait_ge(t_done, c + 1)
                            sp.wait_ge(dx_ready, passed(c))
                            sp.sem_inc(turn, 1)
                            load_x(c + 1, 1 - u)
                            load_bz(c + 1)
                            load_dl(c + 1, 1 - u)
                        if s == 3 and not last:
                            sp.wait_ge(st_ready, c + 1)
                            sp.wait_ge(yo_used, c + 1)
                            sp.wait_ge(dx_ready, c + 1)
                            sp.sem_inc(turn, 1)
                            load_rep(c + 1)

                chunks(sp, body)

            @block.gpsimd
            def _(pool):
                n = 0
                for op in (
                    lambda: pool.memset(dmi, -1.0),
                    lambda: pool.affine_select(out=dmi, in_=dmi, compare_op=ALU.is_equal, fill=0.0,
                                               base=0, pattern=[[-1, GV], [0, P]], channel_multiplier=1),
                    lambda: pool.memset(mask[:, :], 0.0),
                    lambda: pool.affine_select(out=mask[:, :], in_=mask[:, :], compare_op=ALU.is_ge, fill=PAD_SCORE,
                                               base=0, pattern=[[1, P]], channel_multiplier=-1),
                ):
                    op().then_inc(own, 1)
                    n += 1
                    pool.wait_ge(own, n)
                pool.wait_ge(zeroed, 5)
                pool.sem_inc(preset, 1)

                def body(c, u, last):
                    pool.wait_ge(rep_in, (c + 1) * (16 * 2 * XT))
                    pool.wait_ge(x_in[u], (c - u) * 8 + 16)
                    pool.wait_ge(summed, passed(c))
                    pool.tensor_tensor(tmp2[:, :].rearrange("p (i n) -> p i n", n=P), xr[:, u, :, :],
                                       rep[:, 1, :, :], ALU.mult).then_inc(dx_ready, 1)
                    pool.wait_ge(comb, c + 1)
                    zc = z[:, :, bass.ds(c * P, P)]
                    pool.tensor_tensor(zc, zc, tmp[:, :].rearrange("p (i n) -> p i n", n=P),
                                       ALU.mult).then_inc(out_ready, 1)
                chunks(pool, body)

            @block.vector
            def _(dve):
                dve.memset(dl[:, :, :, :], 1.0).then_inc(zeroed, 1)
                for op in (Bz[:, :, :, :], ST[:, :, :], Sn[:, :, :], Xm):
                    dve.memset(op, 0.0).then_inc(zeroed, 1)
                dve.wait_ge(preset, 1)

                def turned_x(c, u):
                    dve.wait_ge(t_done, c + 1)
                    dve.wait_ge(yd_done, passed((c - 1) * SG))
                    xm = Xm[:, u, :].rearrange("p (q n) -> p q n", q=NQD)
                    for k in range(2):
                        dve.tensor_copy(
                            xm[:, :, 56 * k:56 * k + 40].rearrange("p q (j w) -> p q j w", w=VP)[:, :, 0:5:4, :],
                            W[0][:, :].rearrange("p (q a j v) -> p q a j v", q=NQD, a=2, j=2)[:, :, k, :, :]
                        ).then_inc(xm_ready, 1)
                    dve.wait_ge(st_done, passed(c))
                    dve.tensor_tensor(Xd[:, :].rearrange("p (h v) -> p h v", v=VP),
                                      W[0][:, :].rearrange("p (h v) -> p h v", v=VP),
                                      decT[:, bass.ds(c, 1), :].rearrange("p c h -> p (c h)").unsqueeze(2)
                                      .to_broadcast([P, VH, VP]), ALU.mult).then_inc(xd_ready, 1)

                def products_out(c, u):
                    dve.wait_ge(cb_done, c + 1)
                    for k in range(2):
                        dve.tensor_copy(CBm[:, u, 4 * k:4 * k + 4, :], W[k][:, :].rearrange("p (s n) -> p s n", n=P)
                                        ).then_inc(cbm_ready, 1)

                turned_x(0, 0)
                products_out(0, 0)

                def body(c, u, last):
                    t3 = tmp[:, :].rearrange("p (i n) -> p i n", n=P)
                    dve.wait_ge(cbm_ready, 2 * c + 2)
                    for s in range(SG):
                        dve.wait_ge(exp_done, c * SG + s + 1)
                        dve.tensor_tensor(EX[:, s % 4, :, :], EX[:, s % 4, :, :],
                                          CBm[:, u, s, :].unsqueeze(1).to_broadcast([P, GV, P]),
                                          ALU.mult).then_inc(m_ready, 1)
                        if s == 0:
                            dve.wait_ge(st_done, c + 1)
                            dve.wait_ge(rep_in, (c + 1) * (16 * 2 * XT))
                            for i in range(XT):
                                for k in range(2):
                                    r = slice(k * SN, (k + 1) * SN)
                                    dve.scalar_tensor_tensor(
                                        out=ST[r, i, r], in0=ST[r, i, r], scalar=rep[r, 0, i, P - 1:P],
                                        in1=W[0][r, i * P + k * SN:i * P + (k + 1) * SN],
                                        op0=ALU.mult, op1=ALU.add).then_inc(st_upd, 1)
                            dve.wait_ge(st_upd, (c + 1) * (2 * XT))
                            dve.sem_inc(st_ready, 1)
                        if s == 1:
                            dve.wait_ge(yo_done, c + 1)
                            dve.wait_ge(out_ready, passed(c))
                            dve.tensor_tensor(t3, Yo[:, :, :], rep[:, 0, :, :], ALU.mult).then_inc(yo_used, 1)
                        if s == 2:
                            dve.wait_ge(yo_used, c + 1)
                            dve.wait_ge(dx_ready, c + 1)
                            dve.tensor_tensor(tmp[:, :], tmp[:, :], tmp2[:, :], ALU.add).then_inc(summed, 1)
                        if s == 4 and not last:
                            turned_x(c + 1, 1 - u)
                        if s == 6 and not last:
                            products_out(c + 1, 1 - u)
                    dve.wait_ge(summed, c + 1)
                    dve.wait_ge(yd_done, (c + 1) * SG)
                    dve.tensor_tensor(t3, t3, Yd[:, :, :], ALU.add).then_inc(comb, 1)
                chunks(dve, body)

            @block.scalar
            def _(act):
                def turned_b(c):
                    act.wait_ge(t_done, c + 1)
                    act.wait_ge(st_done, passed(c))
                    act.activation(Bt[:, :], W[1][:, :], ACT.Copy).then_inc(bt_ready, 1)
                turned_b(0)

                def body(c, u, last):
                    for s in range(SG):
                        act.wait_ge(diff_done, c * SG + s + 1)
                        act.wait_ge(yd_done, passed(c * SG + s - 3))
                        act.activation(EX[:, s % 4, :, :].rearrange("p h n -> p (h n)"),
                                       D0[s % 2][:, :, :].rearrange("p a n -> p (a n)"), ACT.Exp).then_inc(exp_done, 1)
                        if s == 3 and not last:
                            act.wait_ge(sT_done, c + 1)
                            act.wait_ge(yo_done, c + 1)
                            act.activation(Sn[:, :, :].rearrange("p i n -> p (i n)"), W[1][:, :],
                                           ACT.Copy).then_inc(s_ready, 1)
                        if s == 5 and not last:
                            turned_b(c + 1)
                chunks(act, body)

            @block.tensor
            def _(pe):
                pe.wait_ge(preset, 1)
                pe.wait_ge(ind_in, 16 * 3)

                def turn_xb(c, u):
                    pe.wait_ge(x_in[u], (c - u) * 8 + 16)
                    pe.wait_ge(b_in, (c + 1) * 16)
                    pe.wait_ge(st_ready, passed(c))
                    pe.wait_ge(s_ready, passed(c))
                    for a in range(2):
                        for i in range(XT):
                            mm = pe.transpose(W[a][:, i * P:(i + 1) * P], Br[:, i, :] if a else xr[:, u, i, :],
                                              g.ident[:, :])
                    mm.then_inc(t_done, 1)

                def diff(c, u, s):
                    if s == 0:
                        pe.wait_ge(dl_in[u], (c - u) * 24 + 48)
                    pe.wait_ge(dm_in[s % 4], (c * 2 + s // 4 + 1) * 16)
                    pe.wait_ge(exp_done, passed(c * SG + s - 1))
                    for k in range(2):
                        pe.matmul(D0[s % 2][:, k, :], g.identb[:, :],
                                  mask[:, :].unsqueeze(1).to_broadcast([P, 4, P]), start=True, stop=False)
                        mm = pe.matmul(D0[s % 2][:, k, :], dl[:, u, s, :],
                                       dm[:, s % 4, 4 * k:4 * k + 4, :], start=False, stop=True)
                    mm.then_inc(diff_done, 1)

                def products(c):
                    pe.wait_ge(xm_ready, 2 * c + 2)
                    pe.wait_ge(xd_ready, c + 1)
                    pe.wait_ge(bt_ready, c + 1)
                    pe.wait_ge(bz_in, (c + 1) * 32)
                    for s in range(SG):
                        mm = pe.matmul(W[s // 4][:, (s % 4) * P:(s % 4 + 1) * P], Bz[:, s // 2, s % 2, :],
                                       xc[:, 2 * XT + s // 2, bass.ds(c * P, P)], start=True, stop=True)
                    mm.then_inc(cb_done, 1)

                def from_state(c):
                    pe.wait_ge(yo_used, passed(c))
                    pe.wait_ge(s_ready, passed(c))
                    for i in range(XT):
                        mm = pe.matmul(Yo[:, i, :], Sn[:, i, :], xc[:, 2 * XT + i, bass.ds(c * P, P)],
                                       start=True, stop=True)
                    mm.then_inc(yo_done, 1)

                turn_xb(0, 0)
                diff(0, 0, 0)
                diff(0, 0, 1)
                products(0)
                from_state(0)

                def body(c, u, last):
                    pe.wait_ge(cbm_ready, 2 * c + 2)
                    for i in range(XT):
                        mm = pe.matmul(W[0][:, i * P:(i + 1) * P], Xd[:, i * P:(i + 1) * P],
                                       Bt[:, i * P:(i + 1) * P], start=True, stop=True)
                    mm.then_inc(st_done, 1)
                    for s in range(SG):
                        pe.wait_ge(m_ready, c * SG + s + 1)
                        if s == 0:
                            pe.wait_ge(comb, passed(c))
                        for j in range(4):
                            for k in range(2):
                                quad = 2 * s + k
                                r = (quad % 4) * 32
                                w0 = quad * QW + WINDOW[j]
                                mm = pe.matmul(Yd[r:r + 32, s // 2, :], Xm[:, u, w0:w0 + 32],
                                               EX[:, s % 4, 4 * k + j, :], start=(j == 0), stop=(j == 3),
                                               skip_group_check=True)
                        mm.then_inc(yd_done, 1)
                        if s + 2 < SG:
                            diff(c, u, s + 2)
                        elif not last:
                            diff(c + 1, 1 - u, s + 2 - SG)
                        if s == 1 and not last:
                            pe.wait_ge(st_ready, c + 1)
                            for i in range(XT):
                                mm = pe.transpose(W[1][:, i * P:(i + 1) * P], ST[:, i, :], g.ident[:, :])
                            mm.then_inc(sT_done, 1)
                        if s == 3 and not last:
                            turn_xb(c + 1, 1 - u)
                        if s == 4 and not last:
                            from_state(c + 1)
                        if s == 5 and not last:
                            products(c + 1)
                chunks(pe, body)


def project_out(nc, g, z, out_w):
    with ExitStack() as ctx:
        sem = lambda n: nc.alloc_semaphore(f"po_{n}")
        sb = lambda n, s, d=F32: ctx.enter_context(nc.sbuf_tensor(f"po_{n}", s, d))
        pb = lambda n, s, d=F32: ctx.enter_context(nc.psum_tensor(f"po_{n}", s, d))
        wrow = sb("wrow", [P, CT, DI])
        wT = sb("wT", [P, XT, H])
        ZR = 4
        zt = sb("zt", [P, ZR, XT, P])
        banks = [pb(f"bank{i}", [P, 512]) for i in range(ZR + CT)]
        w_in, x_in, turned, w_ready, y_done, y_copied, y_stats = [sem(n) for n in (
            "w_in", "x_in", "turned", "w_ready", "y_done", "y_copied", "y_stats")]
        z_in = [sem(f"z_in{u}") for u in range(ZR)]
        with nc.Block() as block:

            @block.sync
            def _(sp):
                sp.dma_start(wrow[:, :, :], out_w.rearrange("(a p) n -> p a n", p=P)).then_inc(w_in, 16)
                for u in range(ZR):
                    sp.dma_start(zt[:, u, :, :], z[:, :, u * P:(u + 1) * P]).then_inc(z_in[u], 16)
                sp.dma_start(g.x[:, :, :], g.x_dram.rearrange("(t p) c -> p t c", p=P)).then_inc(x_in, 16)
                with sp.Fori(1, NT // ZR) as b:
                    for u in range(ZR):
                        sp.wait_ge(y_done, ZR * b + u + 1 - ZR)
                        sp.dma_start(zt[:, u, :, :], z[:, :, bass.ds((ZR * b + u) * P, P)]).then_inc(z_in[u], 16)
                sp.wait_ge(x_in, 16)

            @block.vector
            def _(dve):
                for a in range(CT):
                    dve.wait_ge(turned, a + 1)
                    dve.tensor_copy(wT[:, :, a * P:(a + 1) * P],
                                    banks[ZR + a][:, :].rearrange("p (k n) -> p k n", n=P)).then_inc(w_ready, 1)
                with dve.Fori(0, NT // ZR) as b:
                    for u in range(ZR):
                        dve.wait_ge(y_copied, ZR * b + u + 1)
                        dve.bn_stats(g.stats[:, ZR * b + u, :], g.y[:, ZR * b + u, :]).then_inc(y_stats, 1)

            @block.scalar
            def _(act):
                with act.Fori(0, NT // ZR) as b:
                    for u in range(ZR):
                        act.wait_ge(y_done, ZR * b + u + 1)
                        act.activation(g.y[:, ZR * b + u, :], banks[u][:, 0:H], ACT.Copy).then_inc(y_copied, 1)

            @block.tensor
            def _(pe):
                pe.wait_ge(w_in, 16)
                for a in range(CT):
                    for k in range(XT):
                        mm = pe.transpose(banks[ZR + a][:, k * P:(k + 1) * P], wrow[:, a, k * P:(k + 1) * P],
                                          g.ident[:, :])
                    mm.then_inc(turned, 1)
                pe.wait_ge(w_ready, CT)
                with pe.Fori(0, NT // ZR) as b:
                    for u in range(ZR):
                        pe.wait_ge(z_in[u], (b + 1) * 16)
                        pe.wait_ge(y_copied, ZR * b)
                        for k in range(XT):
                            mm = pe.matmul(banks[u][:, 0:H], zt[:, u, k, :], wT[:, k, :],
                                           start=(k == 0), stop=(k == XT - 1))
                        mm.then_inc(y_done, 1)


def state_space(nc, g, in_w, conv_w, conv_b, z_bias, D, out_w):
    with ExitStack() as ctx:
        z = ctx.enter_context(nc.sbuf_tensor("ss_z", [P, XT, T], F32))
        with ExitStack() as inner:
            xc = inner.enter_context(nc.sbuf_tensor("ss_xc", [P, CONV_T, T], F32))
            decT = inner.enter_context(nc.sbuf_tensor("ss_decT", [P, NC, VH], F32))
            with ExitStack() as a:
                alog = a.enter_context(nc.sbuf_tensor("ss_alog", [P, HT], F32))
                project_state(nc, g, xc, z, alog, in_w, conv_w, conv_b, z_bias)
                decays(nc, g, alog, decT, D)
            scan(nc, g, xc, z, decT)
        project_out(nc, g, z, out_w)

MLP = 2048
MT = MLP // P
BLK = 32


def unpack(nc, g, w1T, w2T, mats):
    CODES = MLP * H // 2 // P
    with ExitStack() as ctx:
        sem = lambda n: nc.alloc_semaphore(f"up_{n}")
        sb = lambda n, s, d=F32: ctx.enter_context(nc.sbuf_tensor(f"up_{n}", s, d))
        pb = lambda n, s, d=F32: ctx.enter_context(nc.psum_tensor(f"up_{n}", s, d))
        codes = sb("codes", [P, 3, CODES], I32)
        scales = sb("scales", [P, 3, 2 * CODES // BLK])
        mag = sb("mag", [P, 2, CODES], I16)
        neg = sb("neg", [P, 2, CODES], I16)
        magf = sb("magf", [P, 2, CODES], BF16)
        sign = sb("sign", [P, 2, CODES], BF16)
        a = sb("a", [P, 2, CODES], BF16)
        b = sb("b", [P, 2, CODES], BF16)
        w = sb("w", [P, 2, 2 * CODES])
        banks = [pb(f"bank{i}", [P, 512]) for i in range(4)]
        (bits, magf_ready, sign_ready, chain, magf_used, sign_used, low, high, turned, evac) = [sem(n) for n in (
            "bits", "magf_ready", "sign_ready", "chain", "magf_used", "sign_used", "low", "high", "turned",
            "evac")]
        codes_in = [sem(f"codes_in{m}") for m in range(3)]
        NTURN = 2 * CODES // 512

        def scaled(eng, m, k, done):
            if m >= 2:
                eng.wait_ge(turned, NTURN * (m - 1))
            out = w[:, m % 2, :].rearrange("p (n i two) -> p n i two", i=BLK // 2, two=2)[:, :, :, k]
            eng.tensor_tensor(out, a[:, k, :].rearrange("p (n i) -> p n i", i=BLK // 2),
                              scales[:, m, :].unsqueeze(2).to_broadcast([P, 2 * CODES // BLK, BLK // 2]),
                              ALU.mult).then_inc(done, 1)

        with nc.Block() as block:

            @block.sync
            def _(sp):
                for m, (codes_d, scales_d) in enumerate(mats):
                    sp.dma_start(codes[:, m, :].rearrange("p (a n) -> p a n", n=codes_d.shape[1]),
                                 codes_d.rearrange("(a p) n -> p a n", p=P)).then_inc(codes_in[m], 16)
                    sp.dma_start(scales[:, m, :].rearrange("p (a n) -> p a n", n=scales_d.shape[1]),
                                 scales_d.rearrange("(a p) n -> p a n", p=P)).then_inc(codes_in[m], 16)

            @block.vector
            def _(dve):
                me = Tally(chain)

                def run(ins):
                    me.mark(ins)
                    me.done(dve)

                def take_bits(m):
                    dve.wait_ge(codes_in[m], 32)
                    src = codes[:, m, :].bitcast(I16).rearrange("p (n two) -> p n two", two=2)[:, :, 0]
                    for out, bit in ((mag, 7), (neg, 8)):
                        dve.tensor_scalar(out[:, 0, :], src, bit, None, ALU.bitwise_and).then_inc(bits, 1)
                        dve.tensor_scalar(out[:, 1, :], src, 4, bit, ALU.logical_shift_right,
                                          ALU.bitwise_and).then_inc(bits, 1)
                take_bits(0)
                for m in range(3):
                    dve.wait_ge(magf_ready, m + 1)
                    dve.wait_ge(sign_ready, m + 1)
                    if m < 2:
                        take_bits(m + 1)
                    if m:
                        dve.wait_ge(high, m)
                        dve.wait_ge(low, m)
                    run(dve.tensor_scalar(a[:, :, :], magf[:, :, :], -4.0, 0.0, ALU.add, ALU.max))
                    run(dve.tensor_scalar(b[:, :, :], magf[:, :, :], -6.0, 0.0, ALU.add, ALU.max))
                    run(dve.tensor_tensor(a[:, :, :], a[:, :, :], magf[:, :, :], ALU.add))
                    dve.sem_inc(magf_used, 1)
                    run(dve.tensor_tensor(a[:, :, :], a[:, :, :], b[:, :, :], ALU.add))
                    run(dve.tensor_tensor(a[:, :, :], a[:, :, :], b[:, :, :], ALU.add))
                    dve.tensor_tensor(a[:, :, :], a[:, :, :], sign[:, :, :], ALU.mult).then_inc(sign_used, 1)
                    dve.wait_ge(sign_used, m + 1)
                    scaled(dve, m, 0, low)

            @block.gpsimd
            def _(pool):
                for m in range(3):
                    pool.wait_ge(codes_in[m], 32)
                    pool.wait_ge(sign_used, m + 1)
                    scaled(pool, m, 1, high)

            def turns():
                for m in range(3):
                    for n in range(NTURN):
                        if m < 2:
                            cols = [((2 * n + i) * H + c * P) for c in range(CT) for i in range(2)]
                            out = w1T[:, m, :, 2 * n * P:(2 * n + 2) * P]
                        else:
                            cols = [(c * MLP + (2 * n + i) * P) for i in range(2) for c in range(CT)]
                            out = w2T[:, 2 * n:2 * n + 2, :]
                        yield m, n, cols, out

            @block.tensor
            def _(pe):
                for q, (m, n, cols, _) in enumerate(turns()):
                    if n == 0:
                        pe.wait_ge(low, m + 1)
                        pe.wait_ge(high, m + 1)
                    if q >= 4:
                        pe.wait_ge(evac, q - 3)
                    for i, c in enumerate(cols):
                        mm = pe.transpose(banks[q % 4][:, i * P:(i + 1) * P], w[:, m % 2, c:c + P], g.ident[:, :])
                    mm.then_inc(turned, 1)

            @block.scalar
            def _(act):
                def as_floats(m):
                    act.wait_ge(bits, 4 * m + 4)
                    if m:
                        act.wait_ge(magf_used, m)
                    act.activation(magf[:, :, :], mag[:, :, :], ACT.Copy).then_inc(magf_ready, 1)
                    if m:
                        act.wait_ge(sign_used, m)
                    act.activation(sign[:, :, :], neg[:, :, :], ACT.Copy, bias=0.5, scale=-0.125
                                   ).then_inc(sign_ready, 1)

                as_floats(0)
                for q, (m, n, cols, out) in enumerate(turns()):
                    if n == 0 and m < 2:
                        as_floats(m + 1)
                    act.wait_ge(turned, q + 1)
                    act.activation(out, banks[q % 4][:, :].rearrange("p (a n) -> p a n", a=2), ACT.Copy).then_inc(evac, 1)


def feed_forward(nc, g, w1T, w2T):
    with ExitStack() as ctx:
        sem = lambda n: nc.alloc_semaphore(f"ff_{n}")
        sb = lambda n, s, d=F32: ctx.enter_context(nc.sbuf_tensor(f"ff_{n}", s, d))
        pb = lambda n, s, d=F32: ctx.enter_context(nc.psum_tensor(f"ff_{n}", s, d))
        xn = sb("xn", [P, 2, H])
        xT = sb("xT", [P, 2, CT, P])
        gelu = sb("gelu", [P, 2, 512])
        hid = sb("hid", [P, 2, 512])
        hidT = sb("hidT", [P, 2, 4, P])
        G = [pb(f"G{i}", [P, 512]) for i in range(2)]
        U = [pb(f"U{i}", [P, 512]) for i in range(2)]
        TH = [pb(f"TH{i}", [P, 512]) for i in range(2)]
        O, X = pb("O", [P, 512]), pb("X", [P, 512])
        y_stats = sem("y_stats")
        normed, turned, xT_ready, gu_done, gelu_ready, h_ready, h_turned, hT_ready, d_done, y_ready = [
            sem(n) for n in ("normed", "turned", "xT_ready", "gu_done", "gelu_ready", "h_ready", "h_turned",
                             "hT_ready", "d_done", "y_ready")]

        def slices(eng, tile, step, lag):
            for j in range(8):
                if j % 4 == 0:
                    tile(j // 4, j // 4)
                step(j // 4, j, j, [k for k in range(lag + 1) if k <= j])
            with eng.Fori(1, NT // 2) as b:
                for j in range(8):
                    if j % 4 == 0:
                        tile(b * 2 + j // 4, j // 4)
                    step(b * 2 + j // 4, b * 8 + j, j, list(range(lag + 1)))
            for j in range(lag):
                step(NT, 4 * NT + j, j, [k for k in range(lag + 1) if k > j])

        with nc.Block() as block:

            @block.vector
            def _(dve):
                def rows_stats(t):
                    dve.wait_ge(y_ready, t + 1)
                    dve.bn_stats(g.stats[:, t, :], g.y[:, t, :]).then_inc(y_stats, 1)

                def tile(t, u):
                    if not isinstance(t, int) or t >= 2:
                        dve.wait_ge(turned, t - 1)
                    dve.tensor_scalar(xn[:, u, :], g.x[:, t, :], g.mean[:, bass.ds(t, 1)],
                                      g.rstd[:, bass.ds(t, 1)], ALU.subtract, ALU.mult).then_inc(normed, 1)

                def step(t, n, j, live):
                    if 0 in live:
                        s = j % 2
                        dve.wait_ge(gelu_ready, n + 1)
                        if not isinstance(n, int) or n >= 2:
                            dve.wait_ge(h_turned, n - 1)
                        dve.tensor_tensor(hid[:, s, :], gelu[:, s, :], U[s][:, :], ALU.mult).then_inc(h_ready, 1)
                    if j % 4 == 2 and (not isinstance(n, int) or n >= 4):
                        rows_stats(t - 1)
                slices(dve, tile, step, 0)
                rows_stats(NT - 1)

            @block.scalar
            def _(act):
                def tile(t, u):
                    act.wait_ge(turned, t + 1)
                    if not isinstance(t, int) or t >= 2:
                        act.wait_ge(gu_done, t * 4 - 4)
                    act.activation(xT[:, u, :, :].rearrange("p c n -> p (c n)"), X[:, 0:H],
                                   ACT.Copy).then_inc(xT_ready, 1)

                def step(t, n, j, live):
                    if 0 in live:
                        s = j % 2
                        act.wait_ge(gu_done, n + 1)
                        if not isinstance(n, int) or n >= 2:
                            act.wait_ge(h_ready, n - 1)
                        act.activation(gelu[:, s, :], G[s][:, :], ACT.Gelu_apprx_tanh).then_inc(gelu_ready, 1)
                    if 1 in live:
                        s = (j - 1) % 2
                        act.wait_ge(h_turned, n)
                        if not isinstance(n, int) or n >= 3:
                            act.wait_ge(d_done, n - 2)
                        act.activation(hidT[:, s, :, :].rearrange("p k n -> p (k n)"), TH[s][:, :],
                                       ACT.Copy).then_inc(hT_ready, 1)
                    if 2 in live and j % 4 == 1:
                        act.wait_ge(d_done, n - 1)
                        act.activation(g.y[:, t - 1, :], O[:, 0:H], ACT.Copy).then_inc(y_ready, 1)

                def guarded(t, n, j, live):
                    if isinstance(n, int) and n < 4:
                        live = [k for k in live if k < 2]
                    step(t, n, j, live)
                slices(act, tile, guarded, 2)

            @block.tensor
            def _(pe):
                def tile(t, u):
                    pe.wait_ge(normed, t + 1)
                    if not isinstance(t, int) or t >= 1:
                        pe.wait_ge(xT_ready, t)
                    for c in range(CT):
                        mm = pe.transpose(X[:, c * P:(c + 1) * P], xn[:, u, c * P:(c + 1) * P], g.ident[:, :])
                    mm.then_inc(turned, 1)

                def step(t, n, j, live):
                    if 0 in live:
                        s, u = j % 2, (j // 4) % 2
                        pe.wait_ge(xT_ready, t + 1)
                        if not isinstance(n, int) or n >= 2:
                            pe.wait_ge(h_ready, n - 1)
                        for i, bank in enumerate((G[s], U[s])):
                            for c in range(CT):
                                mm = pe.matmul(bank[:, :], xT[:, u, c, :],
                                               w1T[:, i, c, (j % 4) * 512:(j % 4 + 1) * 512],
                                               start=(c == 0), stop=(c == CT - 1))
                        mm.then_inc(gu_done, 1)
                    if 1 in live:
                        s = (j - 1) % 2
                        pe.wait_ge(h_ready, n)
                        if not isinstance(n, int) or n >= 3:
                            pe.wait_ge(hT_ready, n - 2)
                        for k in range(4):
                            mm = pe.transpose(TH[s][:, k * P:(k + 1) * P], hid[:, s, k * P:(k + 1) * P],
                                              g.ident[:, :])
                        mm.then_inc(h_turned, 1)
                    if 2 in live:
                        s, jj = j % 2, (j - 2) % 4
                        pe.wait_ge(hT_ready, n - 1)
                        if jj == 0:
                            pe.wait_ge(y_ready, t)
                        for k in range(4):
                            mm = pe.matmul(O[:, 0:H], hidT[:, s, k, :], w2T[:, jj * 4 + k, :],
                                           start=(jj == 0 and k == 0), stop=(jj == 3 and k == 3))
                        mm.then_inc(d_done, 1)
                slices(pe, tile, step, 2)


def mlp4(nc, g, gate, gate_s, up, up_s, down, down_s):
    with ExitStack() as ctx:
        w1T = ctx.enter_context(nc.sbuf_tensor("m4_w1T", [P, 2, CT, MLP], F32))
        w2T = ctx.enter_context(nc.sbuf_tensor("m4_w2T", [P, MT, H], F32))
        unpack(nc, g, w1T, w2T, ((gate, gate_s), (up, up_s), (down, down_s)))
        feed_forward(nc, g, w1T, w2T)


def build_program(nc, hidden, Wq, bq, Wk, bk, Wv, bv, router_w, gate_up, down, shared_gate, shared_up, shared_down,
                  in_w, conv_w, conv_b, z_bias, D, out_w, gate4, gate4_s, up4, up4_s, down4, down4_s, out):
    g = Shared()
    dram = lambda n, s, d=F32: nc.dram_tensor(f"rest_{n}", s, d, kind="Internal").ap()
    g.q_dram, g.v_dram = dram("q", (T, H)), dram("v", (TP, NH * VW))
    g.qk_dram, g.gq_dram = dram("qk", (3, 2 * H, T), BF16), dram("gq", (3, H, SLOTS), BF16)
    g.c_dram, g.x_dram = dram("c", (T, H)), dram("x", (T, H))
    g.xr_dram, g.yr_dram = dram("xr", (NS * P, H)), dram("yr", (NS * P, H))
    g.ac_dram, g.rep_dram = dram("ac", (3, VH, T), BF16), dram("rep", (2, VH, T))
    with ExitStack() as ctx:
        sb = lambda n, s, d=F32: ctx.enter_context(nc.sbuf_tensor(n, s, d))
        g.x, g.y = sb("x", [P, NT, H]), sb("y", [P, NT, H])
        g.ident, g.identb = sb("ident", [P, P]), sb("identb", [P, P], BF16)
        g.mean, g.rstd = sb("mean", [P, NT]), sb("rstd", [P, NT])
        g.slot = sb("slot", [P, NT], U32)
        g.stats = sb("stats", [P, NT, 6])
        with nc.cleanup_on_exit(), ExitStack() as att:
            g.kst = att.enter_context(nc.sbuf_tensor("kst", [KALL, 2, HG, TP], BF16))
            g.qst = att.enter_context(nc.sbuf_tensor("qst", [KALL, 2, HG, T], BF16))
            g.norms = att.enter_context(nc.sbuf_tensor("norms", [NH, T], F32))
            g.idxf = att.enter_context(nc.sbuf_tensor("idxf", [NH, SLOTS], F32))
            g.places = att.enter_context(nc.sbuf_tensor("places", [SLOTS, NH], U32))
            constants(nc, g, hidden)
            residual_and_stats(nc, g, None, True, "ln0")
            project(nc, g, Wq, bq, Wk, bk, Wv, bv)
            local_attention(nc, g)
            pick_queries(nc, g)
            global_attention(nc, g)
        with nc.cleanup_on_exit():
            residual_and_stats(nc, g, g.y, False, "ln1", source=g.c_dram)
            mixture(nc, g, router_w, gate_up, down, shared_gate, shared_up, shared_down)
        with nc.cleanup_on_exit():
            residual_and_stats(nc, g, g.y, False, "ln2", routed=True)
            state_space(nc, g, in_w, conv_w, conv_b, z_bias, D, out_w)
        with nc.cleanup_on_exit():
            residual_and_stats(nc, g, g.y, False, "ln3", counted=True)
            mlp4(nc, g, gate4, gate4_s, up4, up4_s, down4, down4_s)
            residual_and_stats(nc, g, g.y, False, "ln4", out, counted=True)


INPUTS = ['L0_attn_hidden_states', 'L0_attn_Wq', 'L0_attn_bq', 'L0_attn_Wk', 'L0_attn_bk', 'L0_attn_Wv',
          'L0_attn_bv', 'L0_ffn_router_w', 'L0_ffn_gate_up_proj', 'L0_ffn_down_proj', 'L0_ffn_shared_gate_w',
          'L0_ffn_shared_up_w', 'L0_ffn_shared_down_w', 'L1_attn_in_proj_w', 'L1_attn_conv1d_weight',
          'L1_attn_conv1d_bias', 'L1_attn_z_bias', 'L1_attn_D', 'L1_attn_out_proj_w', 'L1_ffn_gate_W_packed',
          'L1_ffn_gate_scales', 'L1_ffn_up_W_packed', 'L1_ffn_up_scales', 'L1_ffn_down_W_packed',
          'L1_ffn_down_scales']


def kernel(**inputs):
    import numpy as np
    import concourse.bacc as bacc
    from concourse.bass_utils import run_bass_kernel_spmd

    nc = bacc.Bacc("TRN2", target_bir_lowering=False, num_devices=1)
    arrays, args = {}, []
    for name in INPUTS:
        a = np.ascontiguousarray(inputs[name])
        arrays[f"in_{name}"] = a
        args.append(nc.dram_tensor(f"in_{name}", a.shape, mybir.dt.from_np(a.dtype), kind="ExternalInput").ap())
    out = nc.dram_tensor("out_0", (1, T, H), F32, kind="ExternalOutput").ap()
    build_program(nc, *args, out)
    r = run_bass_kernel_spmd(nc, [arrays], core_ids=[0])
    return r.results[0]["out_0"]
```
